# Optimizing a Trainium2 kernel written in Bass

```python
import numpy as np
import jax
import jax.numpy as jnp

def _softmax(x, axis=-1):
    return jax.nn.softmax(x, axis=axis)

def _gelu(x):
    return jax.nn.gelu(x, approximate=True)

def _silu(x):
    return jax.nn.silu(x)

def _sigmoid(x):
    return jax.nn.sigmoid(x)

def _layernorm(x, axis=-1, eps=1e-05):
    m = jnp.mean(x, axis=axis, keepdims=True)
    v = jnp.var(x, axis=axis, keepdims=True)
    return (x - m) / jnp.sqrt(v + eps)

def _scatter_add(tgt, idx, src, axis=0):
    return tgt.at[idx].add(src)

def _segment_sum(src, seg, n):
    return jax.ops.segment_sum(src, seg, n)
kernel_name = 'mk_perceiver_d2_seqx_r4_0f5827'

def setup_inputs(seed: int=0):
    np.random.seed(seed)
    _w = jnp.asarray

    def _rec_inputs():
        import jax
        import jax.numpy as jnp
        _rk = jax.random.key(seed)
        x = -0.0002928 + 1 * jax.random.normal(jax.random.fold_in(_rk, 1), (32, 64, 256), jnp.float32)
        _lenS = 64 - jax.random.randint(jax.random.fold_in(_rk, 7), (32,), 0, max(1, 64 // 4) + 1, jnp.int32)
        _lenS2 = 256 - jax.random.randint(jax.random.fold_in(_rk, 8), (32,), 0, max(1, 256 // 4) + 1, jnp.int32)
        _ctx_1024P = jax.random.normal(jax.random.fold_in(_rk, 11), (32, 16, 256), jnp.float32)
        _ctx_1024c = jax.random.dirichlet(jax.random.fold_in(_rk, 511), 0.3 * jnp.ones((16,), jnp.float32), (32, 256))
        _ctx_1024t = jnp.einsum('bsk,bkd->bsd', _ctx_1024c, _ctx_1024P)
        _ctx_1024t = _ctx_1024t * jax.lax.rsqrt(jnp.mean(jnp.square(_ctx_1024t)) + 1e-12) * 0.953939
        ctx_1024 = -1.39393e-06 + 0.999914 * (_ctx_1024t + 0.3 * jax.random.normal(jax.random.fold_in(_rk, 611), (32, 256, 256), jnp.float32))
        _validS = jnp.arange(64)[None, :] < _lenS[:, None]
        _validS2 = jnp.arange(256)[None, :] < _lenS2[:, None]
        _causal = jnp.tril(jnp.ones((64, 64), dtype=bool))
        mask_1x1xSxS2_ff0 = jnp.where(jnp.ones((1, 1, 64, 256), dtype=bool), 0.0, -1000000000.0).astype(jnp.float32)
        mask_BxS2_ik0 = jnp.where(jnp.broadcast_to(_validS2[:, :], (32, 256)), 0, 1).astype(jnp.int32)
        return (x, ctx_1024, mask_1x1xSxS2_ff0, mask_BxS2_ik0)
    x, ctx_1024, mask_1x1xSxS2_ff0, mask_BxS2_ik0 = _rec_inputs()

    def _L0_xattn_setup():
        import jax, jax.numpy as jnp
        import numpy as np
        D_MODEL = 256
        H = 16
        HEAD_DIM = D_MODEL // H
        key = jax.random.key(seed)
        ks = jax.random.split(key, 11)
        B, S, D = (1, 1024, D_MODEL)
        scale = 1.0 / np.sqrt(D)
        inp = {'q': jax.random.normal(ks[0], (B, S, D), jnp.float32), 'k': jax.random.normal(ks[1], (B, S, D), jnp.float32), 'v': jax.random.normal(ks[2], (B, S, D), jnp.float32), 'w_q': jax.random.normal(ks[3], (D, D), jnp.float32) * scale, 'b_q': jnp.zeros((D,), jnp.float32), 'w_k': jax.random.normal(ks[4], (D, D), jnp.float32) * scale, 'b_k': jnp.zeros((D,), jnp.float32), 'w_v': jax.random.normal(ks[5], (D, D), jnp.float32) * scale, 'b_v': jnp.zeros((D,), jnp.float32), 'w_o': jax.random.normal(ks[6], (D, D), jnp.float32) * scale, 'b_o': jnp.zeros((D,), jnp.float32)}
        return inp
    _L0_xattn_all = _L0_xattn_setup()
    _L0_xattn_in = {k: v for k, v in _L0_xattn_all.items() if k in ('w_q', 'b_q', 'w_k', 'b_k', 'w_v', 'b_v', 'w_o', 'b_o')}
    del _L0_xattn_all

    def _L0_attn_setup():
        import jax, jax.numpy as jnp
        import numpy as np
        HEADS = 16
        BIAS_STRENGTH = 0.1
        LN_EPS = 1e-05

        def _layernorm(x, gamma, beta):
            mu = jnp.mean(x, axis=-1, keepdims=True)
            var = jnp.mean((x - mu) ** 2, axis=-1, keepdims=True)
            return (x - mu) * jax.lax.rsqrt(var + LN_EPS) * gamma + beta

        def _spatial_bias(spatial_centers, N, dtype):
            diff = spatial_centers[:, None, :] - spatial_centers[None, :, :]
            dist = jnp.sqrt(jnp.sum(diff * diff, axis=-1))
            max_dist = jnp.max(dist)
            core = jnp.where(max_dist > 1e-06, -dist / max_dist, 0.0) * BIAS_STRENGTH
            P = spatial_centers.shape[0]
            bias = jnp.zeros((N, N), dtype=dtype)
            return bias.at[1:P + 1, 1:P + 1].set(core.astype(dtype))
        key = jax.random.key(seed)
        ks = jax.random.split(key, 4)
        B, N, D, P = (2, 512, 256, 256)
        return {'x': jax.random.normal(ks[0], (B, N, D), dtype=jnp.float32), 'W_qkv': jax.random.normal(ks[1], (3 * D, D), dtype=jnp.float32) * D ** (-0.5), 'W_proj': jax.random.normal(ks[2], (D, D), dtype=jnp.float32) * D ** (-0.5), 'b_proj': jnp.zeros((D,), dtype=jnp.float32), 'ln_gamma': jnp.ones((D,), dtype=jnp.float32), 'ln_beta': jnp.zeros((D,), dtype=jnp.float32), 'spatial_centers': jax.random.uniform(ks[3], (P, 2), dtype=jnp.float32)}
    _L0_attn_all = _L0_attn_setup()
    _L0_attn_in = {k: v for k, v in _L0_attn_all.items() if k in ('W_qkv', 'W_proj', 'b_proj', 'ln_gamma', 'ln_beta', 'spatial_centers')}
    del _L0_attn_all

    def _L0_ffn_setup():
        import jax, jax.numpy as jnp
        import numpy as np
        B, T, D = (4, 256, 256)
        E, K, F_EXP = (8, 2, 256)
        NUM_BLOCK = 12
        key = jax.random.key(seed)
        k_x, k_b, k_r, k_1, k_2 = jax.random.split(key, 5)
        x = jax.random.normal(k_x, (B, T, D), dtype=jnp.float32)
        auxfree_bias = jax.random.normal(k_b, (E,), dtype=jnp.float32) * 0.1
        router_w = jax.random.normal(k_r, (E, D), dtype=jnp.float32) * 0.02
        w1 = jax.random.normal(k_1, (E, F_EXP, D), dtype=jnp.float32) * 0.02
        w2 = jax.random.normal(k_2, (E, D, F_EXP), dtype=jnp.float32) * (0.02 / np.sqrt(2.0 * NUM_BLOCK))
        return {'x': x, 'auxfree_bias': auxfree_bias, 'router_w': router_w, 'w1': w1, 'w2': w2}
    _L0_ffn_all = _L0_ffn_setup()
    _L0_ffn_in = {k: v for k, v in _L0_ffn_all.items() if k in ('auxfree_bias', 'router_w', 'w1', 'w2')}
    del _L0_ffn_all

    def _L1_xattn_setup():
        import jax, jax.numpy as jnp
        import numpy as np
        H = 16
        D_MODEL = 256
        D_K = D_MODEL // H
        B, S = (4, 512)

        def _split_heads(x):
            b, s, _ = x.shape
            return x.reshape(b, s, H, D_K).transpose(0, 2, 1, 3)
        key = jax.random.key(seed)
        ks = jax.random.split(key, 12)
        scale = 1.0 / np.sqrt(D_MODEL)
        inp = {'query': jax.random.normal(ks[0], (B, S, D_MODEL), jnp.float32), 'key_in': jax.random.normal(ks[1], (B, S, D_MODEL), jnp.float32), 'value': jax.random.normal(ks[2], (B, S, D_MODEL), jnp.float32), 'src_mask': jnp.zeros((1, 1, S, S), jnp.float32), 'pad_mask': jax.random.randint(ks[3], (B, S), 0, 2, jnp.int32), 'Wq': jax.random.normal(ks[4], (D_MODEL, D_MODEL), jnp.float32) * scale, 'bq': jnp.zeros((D_MODEL,), jnp.float32), 'Wk': jax.random.normal(ks[5], (D_MODEL, D_MODEL), jnp.float32) * scale, 'bk': jnp.zeros((D_MODEL,), jnp.float32), 'Wv': jax.random.normal(ks[6], (D_MODEL, D_MODEL), jnp.float32) * scale, 'bv': jnp.zeros((D_MODEL,), jnp.float32), 'Wo': jax.random.normal(ks[7], (D_MODEL, D_MODEL), jnp.float32) * scale, 'bo': jnp.zeros((D_MODEL,), jnp.float32)}
        return inp
    _L1_xattn_all = _L1_xattn_setup()
    _L1_xattn_in = {k: v for k, v in _L1_xattn_all.items() if k in ('Wq', 'bq', 'Wk', 'bk', 'Wv', 'bv', 'Wo', 'bo')}
    del _L1_xattn_all

    def _L1_attn_setup():
        import jax, jax.numpy as jnp
        import numpy as np
        import math
        DIM = 256
        NUM_HEADS = 16
        HEAD_DIM = DIM // NUM_HEADS
        B, S = (2, 512)
        key = jax.random.key(seed)
        ks = jax.random.split(key, 9)
        sc = 0.02
        return {'x': jax.random.normal(ks[0], (B, S, DIM), jnp.float32), 'Wq': jax.random.normal(ks[1], (DIM, DIM), jnp.float32) * sc, 'bq': jax.random.normal(ks[2], (DIM,), jnp.float32) * sc, 'Wk': jax.random.normal(ks[3], (DIM, DIM), jnp.float32) * sc, 'bk': jax.random.normal(ks[4], (DIM,), jnp.float32) * sc, 'Wv': jax.random.normal(ks[5], (DIM, DIM), jnp.float32) * sc, 'bv': jax.random.normal(ks[6], (DIM,), jnp.float32) * sc, 'Wo': jax.random.normal(ks[7], (DIM, DIM), jnp.float32) * sc, 'bo': jax.random.normal(ks[8], (DIM,), jnp.float32) * sc}
    _L1_attn_all = _L1_attn_setup()
    _L1_attn_in = {k: v for k, v in _L1_attn_all.items() if k in ('Wq', 'bq', 'Wk', 'bk', 'Wv', 'bv', 'Wo', 'bo')}
    del _L1_attn_all

    def _L1_ffn_setup():
        import jax, jax.numpy as jnp
        import numpy as np
        CAPACITY_FACTOR = 1.0
        key = jax.random.key(seed)
        ks = jax.random.split(key, 5)
        B, S, D, E, F = (2, 512, 256, 8, 1024)
        x = jax.random.normal(ks[0], (B, S, D), dtype=jnp.float32)
        Ws = jax.random.normal(ks[1], (D, E), dtype=jnp.float32) * (1.0 / np.sqrt(D))
        bs = jnp.zeros((E,), dtype=jnp.float32)
        W1 = jax.random.normal(ks[2], (E, D, F), dtype=jnp.float32) * (1.0 / np.sqrt(D))
        b1 = jnp.zeros((E, F), dtype=jnp.float32)
        W2 = jax.random.normal(ks[3], (E, F, D), dtype=jnp.float32) * (1.0 / np.sqrt(F))
        b2 = jnp.zeros((E, D), dtype=jnp.float32)
        return {'x': x, 'Ws': Ws, 'bs': bs, 'W1': W1, 'b1': b1, 'W2': W2, 'b2': b2}
    _L1_ffn_all = _L1_ffn_setup()
    _L1_ffn_in = {k: v for k, v in _L1_ffn_all.items() if k in ('Ws', 'bs', 'W1', 'b1', 'W2', 'b2')}
    del _L1_ffn_all
    return {'x': x, 'ctx_1024': ctx_1024, 'mask_1x1xSxS2_ff0': mask_1x1xSxS2_ff0, 'mask_BxS2_ik0': mask_BxS2_ik0, 'L0_xattn_w_q': _L0_xattn_in['w_q'], 'L0_xattn_b_q': _L0_xattn_in['b_q'], 'L0_xattn_w_k': _L0_xattn_in['w_k'], 'L0_xattn_b_k': _L0_xattn_in['b_k'], 'L0_xattn_w_v': _L0_xattn_in['w_v'], 'L0_xattn_b_v': _L0_xattn_in['b_v'], 'L0_xattn_w_o': _L0_xattn_in['w_o'], 'L0_xattn_b_o': _L0_xattn_in['b_o'], 'L0_attn_W_qkv': _L0_attn_in['W_qkv'], 'L0_attn_W_proj': _L0_attn_in['W_proj'], 'L0_attn_b_proj': _L0_attn_in['b_proj'], 'L0_attn_ln_gamma': _L0_attn_in['ln_gamma'], 'L0_attn_ln_beta': _L0_attn_in['ln_beta'], 'L0_attn_spatial_centers': _L0_attn_in['spatial_centers'], 'L0_ffn_auxfree_bias': _L0_ffn_in['auxfree_bias'], 'L0_ffn_router_w': _L0_ffn_in['router_w'], 'L0_ffn_w1': _L0_ffn_in['w1'], 'L0_ffn_w2': _L0_ffn_in['w2'], 'L1_xattn_Wq': _L1_xattn_in['Wq'], 'L1_xattn_bq': _L1_xattn_in['bq'], 'L1_xattn_Wk': _L1_xattn_in['Wk'], 'L1_xattn_bk': _L1_xattn_in['bk'], 'L1_xattn_Wv': _L1_xattn_in['Wv'], 'L1_xattn_bv': _L1_xattn_in['bv'], 'L1_xattn_Wo': _L1_xattn_in['Wo'], 'L1_xattn_bo': _L1_xattn_in['bo'], 'L1_attn_Wq': _L1_attn_in['Wq'], 'L1_attn_bq': _L1_attn_in['bq'], 'L1_attn_Wk': _L1_attn_in['Wk'], 'L1_attn_bk': _L1_attn_in['bk'], 'L1_attn_Wv': _L1_attn_in['Wv'], 'L1_attn_bv': _L1_attn_in['bv'], 'L1_attn_Wo': _L1_attn_in['Wo'], 'L1_attn_bo': _L1_attn_in['bo'], 'L1_ffn_Ws': _L1_ffn_in['Ws'], 'L1_ffn_bs': _L1_ffn_in['bs'], 'L1_ffn_W1': _L1_ffn_in['W1'], 'L1_ffn_b1': _L1_ffn_in['b1'], 'L1_ffn_W2': _L1_ffn_in['W2'], 'L1_ffn_b2': _L1_ffn_in['b2']}

def reference(x, ctx_1024, mask_1x1xSxS2_ff0, mask_BxS2_ik0, L0_xattn_w_q, L0_xattn_b_q, L0_xattn_w_k, L0_xattn_b_k, L0_xattn_w_v, L0_xattn_b_v, L0_xattn_w_o, L0_xattn_b_o, L0_attn_W_qkv, L0_attn_W_proj, L0_attn_b_proj, L0_attn_ln_gamma, L0_attn_ln_beta, L0_attn_spatial_centers, L0_ffn_auxfree_bias, L0_ffn_router_w, L0_ffn_w1, L0_ffn_w2, L1_xattn_Wq, L1_xattn_bq, L1_xattn_Wk, L1_xattn_bk, L1_xattn_Wv, L1_xattn_bv, L1_xattn_Wo, L1_xattn_bo, L1_attn_Wq, L1_attn_bq, L1_attn_Wk, L1_attn_bk, L1_attn_Wv, L1_attn_bv, L1_attn_Wo, L1_attn_bo, L1_ffn_Ws, L1_ffn_bs, L1_ffn_W1, L1_ffn_b1, L1_ffn_W2, L1_ffn_b2):
    import jax
    import jax.numpy as jnp

    def _L0_xattn_ref(q, k, v, w_q, b_q, w_k, b_k, w_v, b_v, w_o, b_o):
        import jax, jax.numpy as jnp
        import numpy as np
        D_MODEL = 256
        H = 16
        HEAD_DIM = D_MODEL // H
        B, Sq, D = q.shape
        Sk = k.shape[1]
        Q = (q @ w_q.T + b_q).reshape(B, Sq, H, HEAD_DIM).transpose(0, 2, 1, 3)
        K = (k @ w_k.T + b_k).reshape(B, Sk, H, HEAD_DIM).transpose(0, 2, 1, 3)
        V = (v @ w_v.T + b_v).reshape(B, Sk, H, HEAD_DIM).transpose(0, 2, 1, 3)
        scores = jnp.einsum('bhqd,bhkd->bhqk', Q, K) / jnp.sqrt(jnp.float32(HEAD_DIM))
        attn = jax.nn.softmax(scores, axis=-1)
        ctx = jnp.einsum('bhqk,bhkd->bhqd', attn, V)
        concat = ctx.transpose(0, 2, 1, 3).reshape(B, Sq, D)
        return concat @ w_o.T + b_o

    def _L0_attn_ref(x, W_qkv, W_proj, b_proj, ln_gamma, ln_beta, spatial_centers):
        import jax, jax.numpy as jnp
        import numpy as np
        HEADS = 16
        BIAS_STRENGTH = 0.1
        LN_EPS = 1e-05

        def _layernorm(x, gamma, beta):
            mu = jnp.mean(x, axis=-1, keepdims=True)
            var = jnp.mean((x - mu) ** 2, axis=-1, keepdims=True)
            return (x - mu) * jax.lax.rsqrt(var + LN_EPS) * gamma + beta

        def _spatial_bias(spatial_centers, N, dtype):
            diff = spatial_centers[:, None, :] - spatial_centers[None, :, :]
            dist = jnp.sqrt(jnp.sum(diff * diff, axis=-1))
            max_dist = jnp.max(dist)
            core = jnp.where(max_dist > 1e-06, -dist / max_dist, 0.0) * BIAS_STRENGTH
            P = spatial_centers.shape[0]
            bias = jnp.zeros((N, N), dtype=dtype)
            return bias.at[1:P + 1, 1:P + 1].set(core.astype(dtype))
        B, N, D = x.shape
        H = HEADS
        hd = D // H
        scale = hd ** (-0.5)
        qkv = jnp.einsum('bnd,ed->bne', x, W_qkv)
        qkv = qkv.reshape(B, N, 3, H, hd).transpose(2, 0, 3, 1, 4)
        q, k, v = (qkv[0], qkv[1], qkv[2])
        attn = jnp.einsum('bhnd,bhmd->bhnm', q, k) * scale
        P = spatial_centers.shape[0]
        if N >= P + 1:
            attn = attn + _spatial_bias(spatial_centers, N, x.dtype)[None, None]
        attn = jax.nn.softmax(attn, axis=-1)
        out = jnp.einsum('bhnm,bhmd->bhnd', attn, v)
        out = out.transpose(0, 2, 1, 3).reshape(B, N, D)
        out = jnp.einsum('bnd,ed->bne', out, W_proj) + b_proj
        return out + _layernorm(x, ln_gamma, ln_beta)

    def _L0_ffn_ref(x, auxfree_bias, router_w, w1, w2):
        import jax, jax.numpy as jnp
        import numpy as np
        B, T, D = (4, 256, 256)
        E, K, F_EXP = (8, 2, 256)
        NUM_BLOCK = 12
        logits = jnp.einsum('btd,ed->bte', x, router_w)
        biased = jax.lax.stop_gradient(logits) + auxfree_bias
        _, idx = jax.lax.top_k(biased, K)
        gathered = jnp.take_along_axis(logits, idx, axis=-1)
        probs = jax.nn.softmax(gathered, axis=-1)
        combine = jnp.sum(jax.nn.one_hot(idx, E, dtype=x.dtype) * probs[..., None], axis=2)
        out = jnp.zeros_like(x)
        for e in range(E):
            h = jax.nn.gelu(jnp.einsum('btd,fd->btf', x, w1[e]), approximate=False)
            out = out + combine[:, :, e:e + 1] * jnp.einsum('btf,df->btd', h, w2[e])
        return out

    def _L1_xattn_ref(query, key_in, value, src_mask, pad_mask, Wq, bq, Wk, bk, Wv, bv, Wo, bo):
        import jax, jax.numpy as jnp
        import numpy as np
        H = 16
        D_MODEL = 256
        D_K = D_MODEL // H
        B, S = (4, 512)

        def _split_heads(x):
            b, s, _ = x.shape
            return x.reshape(b, s, H, D_K).transpose(0, 2, 1, 3)
        q = _split_heads(query @ Wq.T + bq)
        k = _split_heads(key_in @ Wk.T + bk)
        v = _split_heads(value @ Wv.T + bv)
        scores = jnp.einsum('bhqd,bhkd->bhqk', q, k) / jnp.sqrt(jnp.float32(D_K))
        pm = pad_mask[:, None, None, :]
        scores = jnp.where(pm == 0, jnp.float32(-1000000000.0), scores)
        scores = scores + src_mask
        p_attn = jax.nn.softmax(scores, axis=-1)
        x = jnp.einsum('bhqk,bhkd->bhqd', p_attn, v)
        x = x.transpose(0, 2, 1, 3).reshape(query.shape[0], -1, H * D_K)
        return x @ Wo.T + bo

    def _L1_attn_ref(x, Wq, bq, Wk, bk, Wv, bv, Wo, bo):
        import jax, jax.numpy as jnp
        import numpy as np
        import math
        DIM = 256
        NUM_HEADS = 16
        HEAD_DIM = DIM // NUM_HEADS
        B, S = (2, 512)
        b, s, d = x.shape
        h, hd = (NUM_HEADS, HEAD_DIM)

        def split_heads(t):
            return t.reshape(b, s, h, hd).transpose(0, 2, 1, 3)
        q = split_heads(x @ Wq + bq)
        k = split_heads(x @ Wk + bk)
        v = split_heads(x @ Wv + bv)
        scores = jnp.einsum('bhqd,bhkd->bhqk', q, k) / math.sqrt(hd)
        causal = jnp.tril(jnp.ones((s, s), dtype=bool))
        scores = jnp.where(causal[None, None], scores, jnp.asarray(-10000.0, scores.dtype))
        probs = jax.nn.softmax(scores, axis=-1)
        ctx = jnp.einsum('bhqk,bhkd->bhqd', probs, v)
        ctx = ctx.transpose(0, 2, 1, 3).reshape(b, s, d)
        return ctx @ Wo + bo

    def _L1_ffn_ref(x, Ws, bs, W1, b1, W2, b2):
        import jax, jax.numpy as jnp
        import numpy as np
        CAPACITY_FACTOR = 1.0
        B, S, D = x.shape
        E = Ws.shape[1]
        N = B * S
        k = int(CAPACITY_FACTOR * N / E)
        xf = x.reshape(N, D)
        route_prob = jax.nn.softmax(xf @ Ws + bs, axis=-1).T
        route_vals, routes = jax.lax.top_k(route_prob, k)
        xin = xf[routes]
        h = jax.nn.gelu(jnp.einsum('ekd,edf->ekf', xin, W1) + b1[:, None, :])
        out = jnp.einsum('ekf,efd->ekd', h, W2) + b2[:, None, :]
        out = out * route_vals[..., None]
        final = jnp.zeros((N, D), dtype=x.dtype).at[routes.reshape(-1)].add(out.reshape(-1, D))
        return final.reshape(B, S, D)
    x = x + _L0_xattn_ref(_layernorm(x, axis=-1), ctx_1024, ctx_1024, L0_xattn_w_q, L0_xattn_b_q, L0_xattn_w_k, L0_xattn_b_k, L0_xattn_w_v, L0_xattn_b_v, L0_xattn_w_o, L0_xattn_b_o)
    x = x + _L0_attn_ref(_layernorm(x, axis=-1), L0_attn_W_qkv, L0_attn_W_proj, L0_attn_b_proj, L0_attn_ln_gamma, L0_attn_ln_beta, L0_attn_spatial_centers)
    x = x + _L0_ffn_ref(_layernorm(x, axis=-1), L0_ffn_auxfree_bias, L0_ffn_router_w, L0_ffn_w1, L0_ffn_w2)
    x = x + _L1_xattn_ref(_layernorm(x, axis=-1), ctx_1024, ctx_1024, mask_1x1xSxS2_ff0, mask_BxS2_ik0, L1_xattn_Wq, L1_xattn_bq, L1_xattn_Wk, L1_xattn_bk, L1_xattn_Wv, L1_xattn_bv, L1_xattn_Wo, L1_xattn_bo)
    x = x + _L1_attn_ref(_layernorm(x, axis=-1), L1_attn_Wq, L1_attn_bq, L1_attn_Wk, L1_attn_bk, L1_attn_Wv, L1_attn_bv, L1_attn_Wo, L1_attn_bo)
    x = x + _L1_ffn_ref(_layernorm(x, axis=-1), L1_ffn_Ws, L1_ffn_bs, L1_ffn_W1, L1_ffn_b1, L1_ffn_W2, L1_ffn_b2)
    return x

_drawn_inputs = setup_inputs


def setup_inputs(seed=0):
    import zlib

    import numpy as np

    out = dict(_drawn_inputs(seed))
    spreads = {'L0_xattn_b_q': (0.0, 0.335),
     'L0_xattn_b_k': (0.0, 2.0),
     'L0_xattn_b_v': (0.0, 0.1),
     'L0_xattn_b_o': (0.0, 0.1),
     'L0_attn_b_proj': (0.0, 0.1),
     'L0_attn_ln_gamma': (1.0, 0.2),
     'L0_attn_ln_beta': (0.0, 0.1),
     'L1_xattn_bq': (0.0, 0.491),
     'L1_xattn_bk': (0.0, 2.0),
     'L1_xattn_bv': (0.0, 0.1),
     'L1_xattn_bo': (0.0, 0.1),
     'L1_ffn_bs': (0.0, 0.579),
     'L1_ffn_b1': (0.0, 0.69),
     'L1_ffn_b2': (0.0, 0.468)}
    factors = {'L0_ffn_auxfree_bias': 8.0,
     'L0_ffn_router_w': 8.0,
     'L0_ffn_w1': 8.0,
     'L0_ffn_w2': 8.0,
     'L1_attn_Wq': 8.0,
     'L1_attn_bq': 64.0,
     'L1_attn_Wk': 8.0,
     'L1_attn_bk': 64.0,
     'L1_attn_bv': 8.0,
     'L1_attn_bo': 6.233}
    for name, (base, spread) in spreads.items():
        noise = np.random.default_rng([zlib.crc32(name.encode()), seed]).standard_normal(out[name].shape)
        drawn = base * np.exp(spread * noise) if base else spread * noise
        out[name] = jnp.asarray(drawn.astype(out[name].dtype))
    for name, factor in factors.items():
        out[name] = (out[name] * factor).astype(out[name].dtype)
    return out
```

```python
from contextlib import ExitStack

import concourse.bass as bass
from concourse import mybir

F32 = mybir.dt.float32
I32 = mybir.dt.int32
BF16 = mybir.dt.bfloat16
ALU = mybir.AluOpType
ACT = mybir.ActivationFunctionType
AX_X = mybir.AxisListType.X

P = 128
D = 256
DC = D // P
H = 16
HD = D // H
B = 32
S = 64
S2 = 256
KT = S2 // P
N = B * S
NT = N // P
BT = P // S
NP = H // 2
PG = NP // DC
E8 = 8
EPS = 1e-5
NEG_PAD = -1.0e9
NEG_CAUSAL = -1.0e4


class Link:

    def __init__(self, eng, sem, base):
        self.eng, self.sem, self.count = eng, sem, base

    def __call__(self, ins):
        ins.then_inc(self.sem, 1)
        self.count = self.count + 1
        self.eng.wait_ge(self.sem, self.count)


class Named(dict):

    def __getattr__(self, name):
        return self[name]

    def __setattr__(self, name, value):
        self[name] = value


def bc(ap, shape):
    return ap.broadcast_to(shape)


NORM = ["chain", "var_ready", "rstd_ready"]


def norm_vector(nc, dve, m, x_tile, y, n):
    link = Link(dve, m.norm.chain, 3 * n)
    link(nc.vector.bn_stats(m.stats[:, :], x_tile))
    nc.vector.memset(m.carrier[:, 4:5], 0.0)
    link(nc.vector.bn_aggr(m.moments[:, :], m.stats[:, :]))
    nc.vector.tensor_scalar(m.var_eps[:, :], m.moments[:, 1:2], EPS, None, ALU.add).then_inc(m.norm.var_ready, 1)
    dve.wait_ge(m.norm.rstd_ready, n + 1)
    nc.vector.tensor_scalar(y, x_tile, m.moments[:, 0:1], m.rstd[:, :], ALU.subtract,
                            ALU.mult).then_inc(m.norm.chain, 1)


def norm_gpsimd(nc, pool, m, n):
    pool.wait_ge(m.norm.var_ready, n + 1)
    nc.gpsimd.tensor_tensor(m.rstd[:, :], m.var_eps[:, :], m.minus_half[:, :],
                            ALU.pow).then_inc(m.norm.rstd_ready, 1)


CROSS = ["yT_in_psum", "yT_ready", "q_in_psum", "q_ready", "qbd_ready", "k_in_psum", "k_ready",
                "v_in_psum", "v_ready", "scores_in_psum", "max_ready", "exp_done", "probs_ready",
                "pT_in_psum", "pT_even_ready", "pT_odd_ready", "context_in_psum", "context_ready",
                "out_in_psum", "x_done", "bias_added", "context_chain", "recip_chain", "ctx_loaded0", "ctx_loaded1"]
MASKED = ["pad_loaded0", "pad_loaded1", "keep_ready", "mask_part_ready", "mask_ready", "scores_taken"]
P_SLOT = [2, 0, 1, 2]


def cross_sync(nc, sp, m, L, s):
    ctx_loaded = [s.ctx_loaded0, s.ctx_loaded1]
    pad_loaded = [s.pad_loaded0, s.pad_loaded1] if L.masked else None

    def load(b, c):
        sp.dma_start(m.ctxT[:, c, :, :], m.ctxT_dram[:, :, bass.ts(b, S2)]).then_inc(ctx_loaded[c], 16)
        if L.masked:
            sp.dma_start(m.pad[:, c, :], bc(m.pad_dram[bass.ts(b, 1), :], [P, S2])).then_inc(pad_loaded[c], 16)

    if L.ctx_free is not None:
        sp.wait_ge(L.ctx_free, B)
    for c in range(BT):
        load(c, c)
    with sp.Fori(1, NT) as t:
        for c in range(BT):
            b = t * BT + c
            sp.wait_ge(s.v_in_psum, b - 1)
            if L.masked:
                sp.wait_ge(s.keep_ready, b - 1)
            load(b, c)


def cross_tensor(nc, pe, m, L, s):
    ctx_loaded = [s.ctx_loaded0, s.ctx_loaded1]
    pT_ready = [s.pT_even_ready, s.pT_odd_ready]

    def transpose_y(t):
        pe.wait_ge(m.norm.chain, 3 * (L.norms + t) + 3)
        for d in range(DC):
            last = nc.tensor.transpose(m.ring[0][:, d * P:(d + 1) * P], m.y[:, 0, d * P:(d + 1) * P], m.ident[:, :])
        last.then_inc(s.yT_in_psum, 1)

    def query(t):
        pe.wait_ge(s.yT_ready, t + 1)
        for g in range(DC):
            for d in range(DC):
                last = nc.tensor.matmul(m.ring[2][:, g * P:(g + 1) * P], L.wq[:, d, g * P:(g + 1) * P],
                                        m.yT[:, 0, d, :], start=d == 0, stop=d == DC - 1)
        last.then_inc(s.q_in_psum, 1)

    def key(b, c):
        pe.wait_ge(ctx_loaded[c], (b - c) * 8 + 16)
        for g in range(DC):
            for d in range(DC):
                last = nc.tensor.matmul(m.ring[1][:, g * S2:(g + 1) * S2], L.wk[:, d, g * P:(g + 1) * P],
                                        m.ctxT[:, c, d, :], start=d == 0, stop=d == DC - 1)
        last.then_inc(s.k_in_psum, 1)

    def value(b, c):
        for k in range(KT):
            for d in range(DC):
                last = nc.tensor.matmul(m.ring[0][:, k * D:(k + 1) * D], m.ctxT[:, c, d, k * P:(k + 1) * P],
                                        L.wv[:, d, :], start=d == 0, stop=d == DC - 1)
        last.then_inc(s.v_in_psum, 1)

    def scores(b, c, first=False):
        pe.wait_ge(s.k_ready, b + 1)
        pe.wait_ge(s.qbd_ready, b + 1)
        for p in range(NP):
            if p % 2 == 0 and not first:
                pe.wait_ge(s.scores_taken if L.masked else s.exp_done, b * NP - NP + p + 2)
            last = nc.tensor.matmul(m.scores[:, p * S2:(p + 1) * S2], m.qbd[:, c, p, :], m.K[:, c, p // PG, :],
                                    start=True, stop=True)
            if p % 2 == 1:
                last.then_inc(s.scores_in_psum, 1)

    def turn(b, c, r):
        pe.wait_ge(s.probs_ready, b * NP + 2 * r + 2)
        for j in range(2):
            for k in range(KT):
                n = j * KT + k
                last = nc.tensor.transpose(m.ring[P_SLOT[r]][:, n * P:(n + 1) * P],
                                           m.probs[:, c, 2 * r + j, k * P:(k + 1) * P], m.ident[:, :])
        last.then_inc(s.pT_in_psum, 1)

    def product(b, c, r):
        pe.wait_ge(pT_ready[r % 2], b * 2 + r // 2 + 1)
        for p in (2 * r, 2 * r + 1):
            row, g = 32 * (p % PG), p // PG
            for k in range(KT):
                last = nc.tensor.matmul(m.context[row:row + 32, g * P:(g + 1) * P], m.V[:, c, k, 32 * p:32 * p + 32],
                                        m.pT[:, r % 2, p % 2, k, :], start=k == 0, stop=k == KT - 1)
        if r == 3:
            last.then_inc(s.context_in_psum, 1)

    def context(b, c, slot2=None, slot0=None, slot1=None, first=False):
        if slot2:
            pe.wait_ge(*slot2)
        turn(b, c, 0)
        if slot0:
            pe.wait_ge(*slot0)
        turn(b, c, 1)
        if not first:
            pe.wait_ge(s.context_ready, b)
        product(b, c, 0)
        if slot1:
            pe.wait_ge(*slot1)
        turn(b, c, 2)
        product(b, c, 1)
        turn(b, c, 3)
        product(b, c, 2)
        product(b, c, 3)

    def output(t):
        pe.wait_ge(s.context_ready, t * BT + BT)
        for g in range(DC):
            last = nc.tensor.matmul(m.ring[1][:, 0:D], m.contextT[:, g, :], L.wo[:, g, :],
                                    start=g == 0, stop=g == DC - 1)
        last.then_inc(s.out_in_psum, 1)

    def tile(t, first=False, last=False):
        b = t * BT
        scores(b, 0, first)
        value(b, 0)
        key(b + 1, 1)
        if not first:
            context(b - 1, 1, slot0=(s.v_ready, b + 1), slot1=(s.k_ready, b + 2))
        scores(b + 1, 1)
        if not last:
            if first:
                pe.wait_ge(s.v_ready, 1)
            transpose_y(t + 1)
        if not first:
            output(t - 1)
        if not last:
            query(t + 1)
        value(b + 1, 1)
        if not last:
            if not first:
                pe.wait_ge(s.x_done, t)
            key(b + 2, 0)
            context(b, 0, (s.q_ready, t + 2), (s.v_ready, b + 2), (s.k_ready, b + 3), first)
        else:
            context(b, 0, None, (s.v_ready, b + 2), (s.x_done, t))

    pe.wait_ge(L.weights_loaded, 16)
    if L.before is not None:
        pe.wait_ge(L.before, NT * L.x_steps)
    transpose_y(0)
    query(0)
    key(0, 0)
    tile(0, first=True)
    with pe.Fori(1, NT - 1) as t:
        tile(t)
    tile(NT - 1, last=True)
    context(B - 1, 1)
    output(NT - 1)


def cross_scalar(nc, act, m, L, s):
    def yT(t):
        act.wait_ge(s.yT_in_psum, t + 1)
        nc.scalar.activation(m.yT[:, 0, :, :], m.ring[0][:, 0:D], ACT.Identity).then_inc(s.yT_ready, 1)

    def query(t):
        act.wait_ge(s.q_in_psum, t + 1)
        for g in range(DC):
            last = nc.scalar.activation(m.q[:, g, :], m.ring[2][:, g * P:(g + 1) * P], ACT.Identity,
                                        bias=L.bq[:, g:g + 1], scale=HD ** -0.5)
        last.then_inc(s.q_ready, 1)

    def key(b, c):
        if L.masked:
            return
        act.wait_ge(s.k_in_psum, b + 1)
        for g in range(DC):
            last = nc.scalar.activation(m.K[:, c, g, :], m.ring[1][:, g * S2:(g + 1) * S2], ACT.Identity,
                                        bias=L.bk[:, g:g + 1])
        last.then_inc(s.k_ready, 1)

    def exps(b, c, pairs):
        for p in pairs:
            if L.masked:
                if p % 4 == 0:
                    act.wait_ge(s.max_ready, b * 2 + p // 4 + 1)
                source = m.probs[:, c, p, :]
            else:
                if p % 2 == 0:
                    act.wait_ge(s.max_ready, b * 4 + p // 2 + 1)
                source = m.scores[:, p * S2:(p + 1) * S2]
            nc.scalar.activation(m.probs[:, c, p, :], source, ACT.Exp, bias=m.neg_max[:, c, p:p + 1],
                                 accum_out=m.row_sum[:, c, p:p + 1]).then_inc(s.exp_done, 1)

    def even_turn(b, r):
        act.wait_ge(s.pT_in_psum, b * 4 + r + 1)
        nc.scalar.activation(m.pT[:, 0, :, :, :], m.ring[P_SLOT[r]][:, :], ACT.Identity).then_inc(s.pT_even_ready, 1)

    def tile(t, first=False, last=False):
        b = t * BT
        exps(b, 0, range(NP))
        key(b + 1, 1)
        if not first:
            even_turn(b - 1, 0)
            even_turn(b - 1, 2)
        exps(b + 1, 1, range(NP // 2))
        if not last:
            yT(t + 1)
            query(t + 1)
        exps(b + 1, 1, range(NP // 2, NP))
        if not last:
            key(b + 2, 0)
        even_turn(b, 0)
        even_turn(b, 2)

    yT(0)
    query(0)
    key(0, 0)
    tile(0, first=True)
    with act.Fori(1, NT - 1) as t:
        tile(t)
    tile(NT - 1, last=True)
    even_turn(B - 1, 0)
    even_turn(B - 1, 2)


def cross_vector(nc, dve, m, L, s):
    def norm(t, first=False):
        if L.x_ready is None:
            dve.wait_ge(L.x_first if first else L.x_rest, 16)
        else:
            dve.wait_ge(L.x_ready, L.x_steps * (t + 1))
        if not first:
            dve.wait_ge(s.yT_in_psum, t)
        norm_vector(nc, dve, m, m.x[:, bass.ts(t, D)], m.y[:, 0, :], L.norms + t)

    def keep(b, c):
        dve.wait_ge([s.pad_loaded0, s.pad_loaded1][c], (b - c) * 8 + 16)
        nc.vector.tensor_scalar(m.keep[:, c, :], m.pad[:, c, :], 0.0, None, ALU.not_equal)
        nc.vector.tensor_scalar(m.drop[:, c, :], m.pad[:, c, :], 0.0, -1.0, ALU.not_equal,
                                ALU.add).then_inc(s.keep_ready, 1)

    def key(b, c):
        dve.wait_ge(s.k_in_psum, b + 1)
        dve.wait_ge(s.keep_ready, b + 1)
        for g in range(DC):
            last = nc.vector.scalar_tensor_tensor(m.K[:, c, g, :], m.ring[1][:, g * S2:(g + 1) * S2],
                                                  L.bk[:, g:g + 1], m.keep[:, c, :], ALU.add, ALU.mult)
        last.then_inc(s.k_ready, 1)

    def maxima(b, c):
        if not L.masked:
            for k in range(NP // 2):
                dve.wait_ge(s.scores_in_psum, b * 4 + k + 1)
                bank = m.scores[:, 2 * k * S2:(2 * k + 2) * S2].rearrange("p (j k) -> p j k", j=2)
                nc.vector.tensor_reduce(m.neg_max[:, c, 2 * k:2 * k + 2], bank, AX_X, ALU.max,
                                        negate=True).then_inc(s.max_ready, 1)
            return
        dve.wait_ge(s.mask_ready, b + 1)
        for p in range(NP):
            if p % 2 == 0:
                dve.wait_ge(s.scores_in_psum, b * 4 + p // 2 + 1)
                nc.vector.memset(m.carrier[:, p // 2:p // 2 + 1], 0.0)
            nc.vector.tensor_tensor_reduce(out=m.probs[:, c, p, :], in0=m.scores[:, p * S2:(p + 1) * S2],
                                           in1=m.add_mask[:, c, :], scale=1.0, scalar=-3.0e38, op0=ALU.add,
                                           op1=ALU.max, accum_out=m.row_max[:, p:p + 1]).then_inc(s.scores_taken, 1)
            if p % 4 == 3:
                dve.wait_ge(s.scores_taken, b * NP + p + 1)
                nc.vector.tensor_scalar(m.neg_max[:, c, p - 3:p + 1], m.row_max[:, p - 3:p + 1], -1.0, None,
                                        ALU.mult).then_inc(s.max_ready, 1)

    def value(b, c):
        dve.wait_ge(s.v_in_psum, b + 1)
        nc.vector.tensor_copy(m.V[:, c, :, :], m.ring[0][:, :]).then_inc(s.v_ready, 1)

    def odd_turn(b, r):
        dve.wait_ge(s.pT_in_psum, b * 4 + r + 1)
        nc.vector.tensor_copy(m.pT[:, 1, :, :, :], m.ring[P_SLOT[r]][:, :]).then_inc(s.pT_odd_ready, 1)

    def context(b, c):
        link = Link(dve, s.context_chain, b)
        dve.wait_ge(s.context_in_psum, b + 1)
        for g in range(DC):
            part = nc.vector.tensor_scalar(m.half[:, g, :], m.context[:, g * P:g * P + S], m.even_head[:, :],
                                           L.bv[:, g:g + 1], ALU.mult, ALU.add)
        link(part)
        both = m.context[:, 0:D].rearrange("p (g a q) -> p g a q", g=DC, a=2)
        nc.vector.scalar_tensor_tensor(m.contextT[:, :, c * S:(c + 1) * S], both[:, :, 1, :], m.odd_head[:, :],
                                       m.half[:, 0:DC, :], ALU.mult, ALU.add).then_inc(s.context_ready, 1)

    def normalise(b, c):
        dve.wait_ge(s.exp_done, b * NP + NP)
        Link(dve, s.recip_chain, b)(nc.vector.reciprocal(m.inv_sum[:, :], m.row_sum[:, c, :]))
        for p in range(NP):
            nc.vector.tensor_scalar(m.probs[:, c, p, :], m.probs[:, c, p, :], m.inv_sum[:, p:p + 1], None,
                                    ALU.mult).then_inc(s.probs_ready, 1)

    def output(t):
        dve.wait_ge(s.out_in_psum, t + 1)
        dve.wait_ge(s.bias_added, t + 1)
        x = m.x[:, bass.ts(t, D)]
        nc.vector.tensor_tensor(x, m.ring[1][:, 0:D], x, ALU.add).then_inc(s.x_done, 1)

    def tile(t, first=False, last=False):
        b = t * BT
        maxima(b, 0)
        value(b, 0)
        if L.masked:
            key(b + 1, 1)
            if not last:
                keep(b + 2, 0)
        if not first:
            odd_turn(b - 1, 1)
            odd_turn(b - 1, 3)
            context(b - 1, 1)
        if not last:
            norm(t + 1)
        normalise(b, 0)
        maxima(b + 1, 1)
        if not first:
            output(t - 1)
        value(b + 1, 1)
        if L.masked and not last:
            key(b + 2, 0)
            keep(b + 3, 1)
        odd_turn(b, 1)
        odd_turn(b, 3)
        context(b, 0)
        normalise(b + 1, 1)

    norm(0, first=True)
    if L.masked:
        keep(0, 0)
        keep(1, 1)
        key(0, 0)
    tile(0, first=True)
    with dve.Fori(1, NT - 1) as t:
        tile(t)
    tile(NT - 1, last=True)
    odd_turn(B - 1, 1)
    odd_turn(B - 1, 3)
    context(B - 1, 1)
    output(NT - 1)


def cross_gpsimd(nc, pool, m, L, s):
    def mask(b, c, first=False):
        if not first:
            pool.wait_ge(s.mask_ready, b)
        pool.wait_ge(s.keep_ready, b + 1)
        nc.gpsimd.tensor_tensor(m.mask_part[:, :], m.drop[:, c, :], bc(m.big[:, 0:1], [P, S2]),
                                ALU.mult).then_inc(s.mask_part_ready, 1)
        pool.wait_ge(s.mask_part_ready, b + 1)
        nc.gpsimd.tensor_tensor(m.add_mask[:, c, :], m.mask_part[:, :], m.src_mask[:, :],
                                ALU.add).then_inc(s.mask_ready, 1)

    def bias(t):
        pool.wait_ge(m.norm.chain, 3 * (L.norms + t) + 3)
        x = m.x[:, bass.ts(t, D)]
        nc.gpsimd.tensor_tensor(x, x, L.bo[:, :], ALU.add).then_inc(s.bias_added, 1)

    def spread(t):
        pool.wait_ge(s.q_ready, t + 1)
        for c in range(BT):
            for g in range(DC):
                q = m.q[:, g:g + 1, c * S:(c + 1) * S]
                last = nc.gpsimd.tensor_tensor(
                    m.qbd[:, c, g * PG:(g + 1) * PG, :].rearrange("p j (a q) -> p (j a) q", a=2),
                    bc(q, [P, H // DC, S]), bc(m.head[:, :, None], [P, H // DC, S]), ALU.mult)
            last.then_inc(s.qbd_ready, 1)

    def tile(t, last=False):
        if L.masked:
            mask(t * BT + 2, 0) if not last else None
        if not last:
            norm_gpsimd(nc, pool, m, L.norms + t + 1)
            bias(t + 1)
            spread(t + 1)
        if L.masked:
            mask(t * BT + 3, 1) if not last else None

    norm_gpsimd(nc, pool, m, L.norms)
    bias(0)
    if L.masked:
        mask(0, 0, True)
        mask(1, 1)
    spread(0)
    with pool.Fori(0, NT - 1) as t:
        tile(t)
SELF = ["yT_in_psum", "yT_ready", "q_in_psum", "q_ready", "qbd_ready", "k_in_psum", "k_ready",
               "v_in_psum", "v_ready", "scores_in_psum", "scores_taken", "exp_done",
               "inv_ready", "probs_ready", "pT_in_psum", "pT_low_ready", "pT_high_ready", "context_in_psum",
               "context_ready", "out_in_psum", "bias_added", "context_chain", "sum_chain"]


def self_tensor(nc, pe, m, L, s):
    def transpose_y(t, c):
        pe.wait_ge(m.norm.chain, 3 * (L.norms + L.tile_norms * (t + 1)))
        for d in range(DC):
            last = nc.tensor.transpose(m.ring[0][:, d * P:(d + 1) * P], m.y[:, c, d * P:(d + 1) * P], m.ident[:, :])
        last.then_inc(s.yT_in_psum, 1)

    def query(t, c):
        for g in range(DC):
            for d in range(DC):
                last = nc.tensor.matmul(m.ring[1][:, g * P:(g + 1) * P], L.wq[:, d, g * P:(g + 1) * P],
                                        m.yT[:, c, d, :], start=d == 0, stop=d == DC - 1)
        last.then_inc(s.q_in_psum, 1)

    def key(t, c):
        for g in range(DC):
            for d in range(DC):
                last = nc.tensor.matmul(m.ring[0][:, g * P:(g + 1) * P], L.wk[:, d, g * P:(g + 1) * P],
                                        m.yT[:, c, d, :], start=d == 0, stop=d == DC - 1)
        last.then_inc(s.k_in_psum, 1)

    def value(t, c):
        for d in range(DC):
            last = nc.tensor.matmul(m.ring[2][:, 0:D], m.yT[:, c, d, :], L.wv[:, d, :],
                                    start=d == 0, stop=d == DC - 1)
        last.then_inc(s.v_in_psum, 1)

    def scores(t, first=False):
        pe.wait_ge(s.k_ready, L.first + t + 1)
        for c in range(BT):
            pe.wait_ge(s.qbd_ready, (L.first + t) * BT + c + 1)
            if not first:
                pe.wait_ge(s.scores_taken, (L.first + t) * BT + c - 1)
            for p in range(NP):
                n = c * NP + p
                last = nc.tensor.matmul(m.scores[:, n * P:(n + 1) * P], m.qbd[:, c, p, :],
                                        m.K[:, 0, p // PG, 0:P], start=True, stop=True)
            last.then_inc(s.scores_in_psum, 1)

    def turn(t, c, r):
        for j in range(PG):
            last = nc.tensor.transpose(m.ring[r][:, j * P:(j + 1) * P],
                                       m.probs[:, c, (r * PG + j) // 2, (j % 2) * P:(j % 2 + 1) * P], m.ident[:, :])
        last.then_inc(s.pT_in_psum, 1)

    def product(t, c, r):
        pe.wait_ge(s.pT_low_ready, 2 * (L.first + t) + r + 1)
        pe.wait_ge(s.pT_high_ready, 2 * (L.first + t) + r + 1)
        for j in range(PG):
            last = nc.tensor.matmul(m.context[32 * j:32 * j + 32, r * D:(r + 1) * D],
                                    m.V[:, c, 0, 32 * (r * PG + j):32 * (r * PG + j) + 32],
                                    m.pT_blocks[:, r, j, :, :], start=True, stop=True)
        if r == 1:
            last.then_inc(s.context_in_psum, 1)

    def context(t, c, bank1, first=False):
        pe.wait_ge(s.probs_ready, L.first + t + 1)
        turn(t, c, 0)
        pe.wait_ge(*bank1)
        turn(t, c, 1)
        if not first:
            pe.wait_ge(s.context_ready, L.first + t)
        product(t, c, 0)
        product(t, c, 1)

    def output(t):
        pe.wait_ge(s.context_ready, L.first + t + 1)
        for g in range(DC):
            last = nc.tensor.matmul(m.ring[1][:, 0:D], m.contextT[:, g, :], L.wo[:, g, :],
                                    start=g == 0, stop=g == DC - 1)
        last.then_inc(s.out_in_psum, 1)

    def tile(t, c, stage=None):
        scores(t, stage == 0)
        if stage != "last":
            transpose_y(t + 1, 1 - c)
        pe.wait_ge(s.v_ready, L.first + t) if stage != 0 else None
        value(t, c)
        if stage != "last":
            pe.wait_ge(s.yT_ready, L.first + t + 2)
            if stage not in (0, 1):
                pe.wait_ge(s.x_done, t - 1)
            query(t + 1, 1 - c)
        if stage != 0:
            context(t - 1, 1 - c, (s.x_done, t - 1) if stage == "last" else (s.q_ready, L.first + t + 2), stage == 1)
        if stage != "last":
            key(t + 1, 1 - c)
        if stage != 0:
            output(t - 1)

    pe.wait_ge(L.weights_loaded, 16)
    pe.wait_ge(L.before, NT * L.x_steps)
    transpose_y(0, 0)
    pe.wait_ge(s.yT_ready, L.first + 1)
    query(0, 0)
    key(0, 0)
    tile(0, 0, 0)
    tile(1, 1, 1)
    with pe.Fori(1, NT // 2 - 1) as i:
        for c in range(2):
            tile(i * 2 + c, c)
    tile(NT - 2, 0)
    tile(NT - 1, 1, "last")
    context(NT - 1, 1, (s.x_done, NT - 1))
    output(NT - 1)


def self_scalar(nc, act, m, L, s):
    def yT(t, c):
        act.wait_ge(s.yT_in_psum, L.first + t + 1)
        nc.scalar.activation(m.yT[:, c, :, :], m.ring[0][:, 0:D], ACT.Identity).then_inc(s.yT_ready, 1)

    def query(t):
        act.wait_ge(s.q_in_psum, L.first + t + 1)
        for g in range(DC):
            last = nc.scalar.activation(m.q[:, g, :], m.ring[1][:, g * P:(g + 1) * P], ACT.Identity,
                                        bias=L.bq[:, g:g + 1], scale=HD ** -0.5)
        last.then_inc(s.q_ready, 1)

    def key(t):
        act.wait_ge(s.k_in_psum, L.first + t + 1)
        for g in range(DC):
            last = nc.scalar.activation(m.K[:, 0, g, 0:P], m.ring[0][:, g * P:(g + 1) * P], ACT.Identity,
                                        bias=L.bk[:, g:g + 1])
        last.then_inc(s.k_ready, 1)

    def value(t, c):
        act.wait_ge(s.v_in_psum, L.first + t + 1)
        nc.scalar.activation(m.V[:, c, 0, :], m.ring[2][:, 0:D], ACT.Identity).then_inc(s.v_ready, 1)

    def exps(t, c):
        if L.causal:
            act.wait_ge(s.shifted, t + 1)
        else:
            act.wait_ge(s.scores_taken, (L.first + t) * BT + BT)
        nc.scalar.activation(m.probs[:, c, 0:PG, :], m.probs[:, c, 0:PG, :], ACT.Exp).then_inc(s.exp_done, 1)

    def low(t):
        for r in range(2):
            act.wait_ge(s.pT_in_psum, 2 * (L.first + t) + r + 1)
            nc.scalar.activation(m.pT_blocks[0:S, r, :, 0, :], m.ring[r][0:S, :].rearrange("p (j q) -> p j q", j=PG),
                                 ACT.Identity).then_inc(s.pT_low_ready, 1)

    def tile(t, c, stage=None):
        if stage != "last":
            yT(t + 1, 1 - c)
        value(t, c)
        if stage != "last":
            query(t + 1)
        if stage != 0:
            low(t - 1)
        exps(t, c)
        if stage != "last":
            key(t + 1)

    yT(0, 0)
    query(0)
    key(0)
    tile(0, 0, 0)
    with act.Fori(0, NT // 2 - 1) as i:
        for c in range(2):
            tile(i * 2 + 1 + c, 1 - c)
    tile(NT - 1, 1, "last")
    low(NT - 1)


def self_vector(nc, dve, m, L, s):
    def norm(t, c):
        dve.wait_ge(L.x_ready, L.x_steps * (t + 1))
        n = L.norms + L.tile_norms * t
        norm_vector(nc, dve, m, m.x[:, bass.ts(t, D)], m.y[:, c, :], n)
        if L.tile_norms == 2:
            dve.wait_ge(m.norm.chain, 3 * n + 3)
            norm_vector(nc, dve, m, m.y[:, c, :], m.z[:, c, :], n + 1)

    def block(c):
        part = m.scores[:, c * NP * P:(c + 1) * NP * P].rearrange("p (n k) -> p n k", k=P)
        return part[:, :, c * S:(c + 1) * S]

    def softmax(t, c):
        probs = m.probs[:, c, 0:PG, :].rearrange("p a k -> p (a k)").rearrange("p (n b k) -> p n b k", b=BT, k=S)
        link = Link(dve, s.soft_chain, (4 if L.causal else 2) * t)
        for b in range(BT):
            dve.wait_ge(s.scores_in_psum, (L.first + t) * BT + b + 1)
            source = block(b)
            if L.causal:
                link(nc.vector.tensor_tensor(probs[:, :, b, :], source, bc(m.causal[:, None, :], [P, NP, S]), ALU.mult))
                nc.vector.tensor_tensor(probs[:, :, b, :], probs[:, :, b, :],
                                        bc(m.causal_add[:, None, :], [P, NP, S]), ALU.add).then_inc(s.scores_taken, 1)
                dve.wait_ge(s.scores_taken, (L.first + t) * BT + b + 1)
                source = probs[:, :, b, :]
            link(nc.vector.tensor_reduce(m.tile_max[:, :, b], source, AX_X, ALU.max))
            ins = nc.vector.tensor_tensor(probs[:, :, b, :], source, bc(m.tile_max[:, :, b:b + 1], [P, NP, S]),
                                          ALU.subtract)
            if L.causal:
                if b == BT - 1:
                    ins.then_inc(s.shifted, 1)
            else:
                ins.then_inc(s.scores_taken, 1)

    def sums(t, c):
        dve.wait_ge(s.exp_done, L.first + t + 1)
        link = Link(dve, s.sum_chain, L.first + t)
        rows = m.probs[:, c, 0:PG, :].rearrange("p a k -> p (a k)").rearrange("p (n k) -> p n k", k=S)
        link(nc.vector.tensor_reduce(m.tile_sum[:, :], rows, AX_X, ALU.add))
        nc.vector.reciprocal(m.tile_inv[:, :], m.tile_sum[:, :]).then_inc(s.inv_ready, 1)

    def high(t):
        for r in range(2):
            dve.wait_ge(s.pT_in_psum, 2 * (L.first + t) + r + 1)
            nc.vector.tensor_copy(m.pT_blocks[S:P, r, :, 1, :],
                                  m.ring[r][S:P, :].rearrange("p (j q) -> p j q", j=PG)).then_inc(s.pT_high_ready, 1)

    def context(t):
        link = Link(dve, s.context_chain, L.first + t)
        dve.wait_ge(s.context_in_psum, L.first + t + 1)
        for g in range(DC):
            both = m.context[:, g * D:(g + 1) * D].rearrange("p (b a q) -> p b a q", b=BT, a=2)
            part = nc.vector.tensor_scalar(m.halves[:, g, :, :], both[:, :, 0, :], m.even_head[:, :],
                                           L.bv[:, g:g + 1], ALU.mult, ALU.add)
        link(part)
        for g in range(DC):
            both = m.context[:, g * D:(g + 1) * D].rearrange("p (b a q) -> p b a q", b=BT, a=2)
            last = nc.vector.scalar_tensor_tensor(
                m.contextT[:, g, :].rearrange("p (b q) -> p b q", b=BT), both[:, :, 1, :], m.odd_head[:, :],
                m.halves[:, g, :, :], ALU.mult, ALU.add)
        last.then_inc(s.context_ready, 1)

    def output(t):
        dve.wait_ge(s.out_in_psum, L.first + t + 1)
        dve.wait_ge(s.bias_added, L.first + t + 1)
        x = m.x[:, bass.ts(t, D)]
        nc.vector.tensor_tensor(x, m.ring[1][:, 0:D], x, ALU.add).then_inc(s.x_done, 1)

    def tile(t, c, stage=None):
        softmax(t, c)
        if stage != 0:
            high(t - 1)
            context(t - 1)
        sums(t, c)
        if stage not in ("last", "last but one"):
            dve.wait_ge(s.yT_in_psum, L.first + t + 1)
            if L.tile_norms == 2:
                dve.wait_ge(s.bias_added, L.first + t + 1)
            norm(t + 2, c)
        if stage != 0:
            output(t - 1)

    norm(0, 0)
    norm(1, 1)
    tile(0, 0, 0)
    with dve.Fori(0, NT // 2 - 2) as i:
        for c in range(2):
            tile(i * 2 + 1 + c, 1 - c)
    tile(NT - 3, 1)
    tile(NT - 2, 0, "last but one")
    tile(NT - 1, 1, "last")
    high(NT - 1)
    context(NT - 1)
    output(NT - 1)


def self_gpsimd(nc, pool, m, L, s):
    def norm(t):
        for n in range(L.tile_norms):
            norm_gpsimd(nc, pool, m, L.norms + t * L.tile_norms + n)

    def bias(t, c):
        pool.wait_ge(m.norm.chain, 3 * (L.norms + L.tile_norms * (t + 1)))
        x = m.x[:, bass.ts(t, D)]
        if L.tile_norms == 2:
            link = Link(pool, s.z_chain, 2 * t)
            link(nc.gpsimd.tensor_tensor(m.z[:, c, :], m.z[:, c, :], m.gamma[:, :], ALU.mult))
            link(nc.gpsimd.tensor_tensor(m.z[:, c, :], m.z[:, c, :], L.bo[:, :], ALU.add))
            nc.gpsimd.tensor_tensor(x, x, m.z[:, c, :], ALU.add).then_inc(s.bias_added, 1)
        else:
            nc.gpsimd.tensor_tensor(x, x, L.bo[:, :], ALU.add).then_inc(s.bias_added, 1)

    def spread(t):
        pool.wait_ge(s.q_ready, L.first + t + 1)
        for c in range(BT):
            for g in range(DC):
                q = m.q[:, g:g + 1, c * S:(c + 1) * S]
                last = nc.gpsimd.tensor_tensor(
                    m.qbd[:, c, g * PG:(g + 1) * PG, :].rearrange("p j (a q) -> p (j a) q", a=2),
                    bc(q, [P, H // DC, S]), bc(m.head[:, :, None], [P, H // DC, S]), ALU.mult)
            last.then_inc(s.qbd_ready, 1)

    def normalise(t, c):
        pool.wait_ge(s.inv_ready, L.first + t + 1)
        rows = m.probs[:, c, 0:PG, :].rearrange("p a k -> p (a k)").rearrange("p (n k) -> p n k", k=S)
        nc.gpsimd.tensor_tensor(rows, rows, bc(m.tile_inv[:, :, None], [P, NP * BT, S]),
                                ALU.mult).then_inc(s.probs_ready, 1)

    def tile(t, c, stage=None):
        if stage != "last":
            spread(t + 1)
        normalise(t, c)
        if stage not in ("last", "last but one"):
            norm(t + 2)
            bias(t + 2, c)

    norm(0)
    bias(0, 0)
    norm(1)
    bias(1, 1)
    spread(0)
    with pool.Fori(0, NT // 2 - 1) as i:
        for c in range(2):
            tile(i * 2 + c, c)
    tile(NT - 2, 0, "last but one")
    tile(NT - 1, 1, "last")
ROUTER = ["yT_in_psum", "yT_ready", "logits_in_psum", "logits_ready"]


def router_tensor(nc, pe, m, L, s):
    def transpose_y(t, c):
        pe.wait_ge(m.norm.chain, 3 * (L.norms + t) + 3)
        for d in range(DC):
            last = nc.tensor.transpose(m.ring[c][:, d * P:(d + 1) * P], m.y[:, c, d * P:(d + 1) * P], m.ident[:, :])
        last.then_inc(s.yT_in_psum, 1)

    def logits(t, c, first=False):
        pe.wait_ge(s.yT_ready, t + 1)
        if not first:
            pe.wait_ge(s.logits_ready, t)
        for d in range(DC):
            last = nc.tensor.matmul(m.ring[2][:, 0:E8], m.yT[:, c, d, :], L.router[:, d, :],
                                    start=d == 0, stop=d == DC - 1)
        last.then_inc(s.logits_in_psum, 1)

    pe.wait_ge(L.weights_loaded, 32)
    pe.wait_ge(L.before, NT * L.x_steps)
    transpose_y(0, 0)
    transpose_y(1, 1)
    logits(0, 0, True)
    with pe.Fori(0, NT // 2 - 1) as i:
        for c in range(2):
            transpose_y(i * 2 + 2 + c, c)
            logits(i * 2 + 1 + c, 1 - c)
    logits(NT - 1, 1)


def router_scalar(nc, act, m, L, s):
    with act.Fori(0, NT // 2) as i:
        for c in range(2):
            t = i * 2 + c
            act.wait_ge(s.yT_in_psum, t + 1)
            if L.keep_yT:
                nc.scalar.activation(m.yT_all[:, bass.ts(t, D)], m.ring[c][:, 0:D], ACT.Identity)
            nc.scalar.activation(m.yT[:, c, :, :], m.ring[c][:, 0:D], ACT.Identity).then_inc(s.yT_ready, 1)


def router_vector(nc, dve, m, L, s):
    def norm(t, c):
        dve.wait_ge(L.x_ready, L.x_steps * (t + 1))
        if L.stored is not None and not isinstance(t, int):
            dve.wait_ge(L.stored[c], (t - c) * 8)
        norm_vector(nc, dve, m, m.x[:, bass.ts(t, D)], m.y[:, c, :], L.norms + t)

    def logits(t):
        dve.wait_ge(s.logits_in_psum, t + 1)
        nc.vector.tensor_tensor(m.logits[:, bass.ts(t, E8)], m.ring[2][:, 0:E8], L.router_bias[:, :],
                                ALU.add).then_inc(s.logits_ready, 1)

    norm(0, 0)
    norm(1, 1)
    with dve.Fori(1, NT // 2) as i:
        for c in range(2):
            t = i * 2 + c
            dve.wait_ge(s.yT_in_psum, t - 1)
            norm(t, c)
            logits(t - 2)
    logits(NT - 2)
    logits(NT - 1)


def router_gpsimd(nc, pool, m, L, s):
    with pool.Fori(0, NT) as t:
        norm_gpsimd(nc, pool, m, L.norms + t)


MIX0 = ["route_chain", "exp_asked", "exp_done", "combine_ready", "h_in_psum", "gelu_done", "out_in_psum", "x_done"]


def mix0_route_vector(nc, dve, m, s):
    link = Link(dve, s.route_chain, 0)
    v = nc.vector
    grid = [P, NT, E8]
    logits = m.logits[:, :].rearrange("p (t e) -> p t e", e=E8)
    biased, hit, best0, best1 = (m.route[:, n, :].rearrange("p (t e) -> p t e", e=E8) for n in range(4))
    top, low, high = m.route_col[:, 0, :], m.route_col[:, 1, :], m.route_col[:, 2, :]
    dve.wait_ge(m.logits_ready, NT)
    link(v.tensor_tensor(biased, logits, bc(m.aux_bias[:, None, :], grid), ALU.add))
    for n, best in enumerate((best0, best1)):
        link(v.tensor_reduce(top, biased, AX_X, ALU.max))
        link(v.tensor_tensor(hit, biased, bc(top[:, :, None], grid), ALU.is_equal))
        link(v.tensor_tensor(hit, hit, bc(m.order[:, None, :], grid), ALU.mult))
        link(v.tensor_reduce(top, hit, AX_X, ALU.max))
        link(v.tensor_tensor(best, hit, bc(top[:, :, None], grid), ALU.is_equal))
        if n == 0:
            link(v.scalar_tensor_tensor(biased, best, -3.0e38, biased, ALU.mult, ALU.add))
    for best, value in ((best0, low), (best1, high)):
        link(v.tensor_tensor(hit, best, logits, ALU.mult))
        link(v.tensor_reduce(value, hit, AX_X, ALU.add))
    link(v.tensor_tensor(top, low, high, ALU.max))
    link(v.tensor_tensor(low, low, top, ALU.subtract))
    v.tensor_tensor(high, high, top, ALU.subtract).then_inc(s.exp_asked, 1)
    dve.wait_ge(s.exp_done, 1)
    link(v.tensor_tensor(top, low, high, ALU.add))
    link(v.reciprocal(top, top))
    link(v.tensor_tensor(low, low, top, ALU.mult))
    link(v.tensor_tensor(high, high, top, ALU.mult))
    link(v.tensor_tensor(best0, best0, bc(low[:, :, None], grid), ALU.mult))
    link(v.tensor_tensor(best1, best1, bc(high[:, :, None], grid), ALU.mult))
    v.tensor_tensor(m.combine[:, :].rearrange("p (t e) -> p t e", e=E8), best0, best1,
                    ALU.add).then_inc(s.combine_ready, 1)


def mix0_tensor(nc, pe, m, L, s):
    def hidden(t, e, first):
        n = t * E8 + e
        if not first or e >= 2:
            pe.wait_ge(s.gelu_done, n - 1)
        for f in range(DC):
            for d in range(DC):
                last = nc.tensor.matmul(m.ring[e % 2][:, f * P:(f + 1) * P], m.w1[:, e, d, f * P:(f + 1) * P],
                                        m.yT_all[:, bass.ts(t * DC + d, P)], start=d == 0, stop=d == DC - 1)
        last.then_inc(s.h_in_psum, 1)

    def out(t, e, first):
        n = t * E8 + e
        pe.wait_ge(s.gelu_done, n + 1)
        if not first or e >= 2:
            pe.wait_ge(s.x_done, n - 1)
        for f in range(DC):
            last = nc.tensor.matmul(m.scores[:, (e % 2) * 512:(e % 2) * 512 + D], m.hT[:, e % 2, f, :],
                                    m.w2[:, e, f, :], start=f == 0, stop=f == DC - 1)
        last.then_inc(s.out_in_psum, 1)

    def tile(t, first=False):
        for e in range(E8):
            hidden(t, e, first)
            if e > 0:
                out(t, e - 1, first)
            elif not first:
                out(t - 1, E8 - 1, False)

    pe.wait_ge(L.experts_loaded, 32)
    tile(0, True)
    with pe.Fori(1, NT) as t:
        tile(t)
    out(NT - 1, E8 - 1, False)


def mix0_scalar(nc, act, m, L, s):
    act.wait_ge(s.exp_asked, 1)
    nc.scalar.activation(m.route_col[:, 1:3, :], m.route_col[:, 1:3, :], ACT.Exp).then_inc(s.exp_done, 1)
    with act.Fori(0, NT) as t:
        for e in range(E8):
            act.wait_ge(s.h_in_psum, t * E8 + e + 1)
            nc.scalar.activation(m.hT[:, e % 2, :, :], m.ring[e % 2][:, 0:D], ACT.Gelu).then_inc(s.gelu_done, 1)


def mix0_vector(nc, dve, m, L, s):
    dve.wait_ge(s.combine_ready, 1)
    with dve.Fori(0, NT) as t:
        for e in range(E8):
            n = t * E8 + e
            dve.wait_ge(s.out_in_psum, n + 1)
            if e > 0:
                dve.wait_ge(s.x_done, n)
            x = m.x[:, bass.ts(t, D)]
            nc.vector.scalar_tensor_tensor(x, m.scores[:, (e % 2) * 512:(e % 2) * 512 + D],
                                           m.combine[:, bass.ds(n, 1)], x, ALU.mult, ALU.add).then_inc(s.x_done, 1)


CAP = N // E8
HALVES = CAP // P
F1 = 1024
FC1 = F1 // P
ROW = D + E8
TOP_BIT = 29
MIX1 = ["soft_chain", "exp_asked", "exp_done", "probs_ready", "cand_chain", "compare_ready", "count_in_psum",
        "pick_chain", "marks_ready", "ranks_in_psum", "slots_ready", "onehot_ready", "onehot_used", "index_ready",
        "y_stored0", "y_stored1", "probs_stored", "x_stored", "gathered0", "gathered1", "xinT_in_psum", "xinT_ready",
        "h_in_psum", "gelu_done", "out_in_psum", "bias_done", "out_ready", "w1_loaded0", "w1_loaded1", "w2_loaded0",
        "w2_loaded1", "scattered"]


def mix1_softmax_vector(nc, dve, m, s):
    link = Link(dve, s.soft_chain, 0)
    v = nc.vector
    grid = [P, NT, E8]
    logits = m.logits[:, :].rearrange("p (t e) -> p t e", e=E8)
    probs = m.combine[:, :].rearrange("p (t e) -> p t e", e=E8)
    col = m.route_col[:, 0, :]
    dve.wait_ge(m.logits1_ready, NT)
    link(v.tensor_reduce(col, logits, AX_X, ALU.max))
    v.tensor_tensor(probs, logits, bc(col[:, :, None], grid), ALU.subtract).then_inc(s.exp_asked, 1)
    dve.wait_ge(s.exp_done, 1)
    link(v.tensor_reduce(col, probs, AX_X, ALU.add))
    link(v.reciprocal(col, col))
    v.tensor_tensor(probs, probs, bc(col[:, :, None], grid), ALU.mult).then_inc(s.probs_ready, 1)
    dve.wait_ge(s.probs_ready, 1)


def mix1_threshold_vector(nc, dve, m, s):
    v = nc.vector
    grid = [P, NT, E8]
    probs = m.combine[:, :].rearrange("p (t e) -> p t e", e=E8)
    hit = m.route[:, 0, :]
    with dve.Fori(0, TOP_BIT + 1) as r:
        link = Link(dve, s.cand_chain, 5 * r)
        link(v.tensor_tensor(m.cand[:, :], m.threshold[:, :], m.bit[:, :], ALU.bitwise_or))
        link(v.tensor_tensor(hit.rearrange("p (t e) -> p t e", e=E8), probs,
                             bc(m.cand[:, None, :].bitcast(F32), grid), ALU.is_ge))
        with nc.allow_low_precision(reason="counts up to NT are exact in bfloat16"):
            v.tensor_reduce(m.hits[:, :], hit.rearrange("p (t e) -> p e t", e=E8), AX_X,
                            ALU.add).then_inc(s.compare_ready, 1)
        dve.wait_ge(s.count_in_psum, r + 1)
        link(v.scalar_tensor_tensor(m.gain[:, :], m.ring[0][:, 0:E8], float(CAP), m.bit[:, :], ALU.is_ge, ALU.mult))
        link(v.tensor_tensor(m.threshold[:, :], m.threshold[:, :], m.gain[:, :], ALU.bitwise_or))
        link(v.tensor_scalar(m.bit[:, :], m.bit[:, :], 0.5, None, ALU.mult))


def mix1_slots_vector(nc, dve, m, s):
    link = Link(dve, s.pick_chain, 0)
    v = nc.vector
    grid = [P, NT, E8]
    probs = m.combine[:, :].rearrange("p (t e) -> p t e", e=E8)
    above, equal, taken, place = (m.route[:, n, :] for n in range(4))
    level = bc(m.threshold[:, None, :].bitcast(F32), grid)
    cube = "p (t e) -> p t e"

    def before_tile(total):
        link(v.tensor_copy(m.scan0[:, 9 * E8:], total[:, 0:(NT - 1) * E8]))
        source, target = m.scan0, m.scan1
        for step in (1, 2, 4, 8):
            link(v.tensor_tensor(target[:, 8 * E8:], source[:, 8 * E8:], source[:, (8 - step) * E8:-step * E8],
                                 ALU.add))
            source, target = target, source
        return source[:, 8 * E8:]

    link(v.tensor_tensor(above.rearrange(cube, e=E8), probs, level, ALU.is_gt))
    link(v.tensor_tensor(equal.rearrange(cube, e=E8), probs, level, ALU.is_equal))
    link(v.tensor_copy(m.marks[:, 0, :], above))
    v.tensor_copy(m.marks[:, 1, :], equal).then_inc(s.marks_ready, 1)
    dve.wait_ge(s.ranks_in_psum, 1)
    total_above, total, within = (m.ring[0][:, n * P:(n + 1) * P] for n in range(3))
    link(v.tensor_reduce(m.need[:, :], total_above.rearrange("p (t e) -> p e t", e=E8), AX_X, ALU.add))
    link(v.tensor_scalar(m.need[:, :], m.need[:, :], -1.0, float(CAP), ALU.mult, ALU.add))
    link(v.tensor_tensor(place, within, before_tile(total), ALU.add))
    link(v.tensor_tensor(taken.rearrange(cube, e=E8), place.rearrange(cube, e=E8), bc(m.need[:, None, :], grid),
                         ALU.is_lt))
    link(v.tensor_tensor(taken, taken, equal, ALU.mult))
    link(v.tensor_tensor(taken, taken, above, ALU.add))
    v.tensor_copy(m.marks[:, 0, :], taken).then_inc(s.marks_ready, 1)
    dve.wait_ge(s.ranks_in_psum, 2)
    link(v.tensor_tensor(place, within, before_tile(total), ALU.add))
    link(v.scalar_tensor_tensor(place, place, -1000.0, taken, ALU.add, ALU.mult))
    v.tensor_scalar(m.slot[:, :], place, 1000.0, None, ALU.add).then_inc(s.slots_ready, 1)
    dve.wait_ge(s.slots_ready, 1)


def mix1_index_vector(nc, dve, m, s):
    def expert(e, first=False):
        for t in range(NT):
            n = e * NT + t
            if not first or t >= 4:
                dve.wait_ge(s.onehot_used, n - 3)
            nc.vector.tensor_scalar(m.onehot[:, t % 4, :], m.slots_row[:, :], m.slot[:, bass.ds(e + t * E8, 1)], None,
                                    ALU.is_equal).then_inc(s.onehot_ready, 1)
        dve.wait_ge(s.onehot_used, e * NT + NT)
        for half in range(HALVES):
            with nc.allow_low_precision(reason="token indices are whole numbers"):
                last = nc.vector.tensor_reduce(m.index[:, bass.ds(e * HALVES + half, 1)], m.ring[half][:, 0:2], AX_X,
                                               ALU.add)
        last.then_inc(s.index_ready, 1)

    expert(0, True)
    with dve.Fori(1, E8) as e:
        expert(e)


def mix1_sync(nc, sp, m, L, s, out):
    def weights(e, c):
        sp.dma_start(m.w1_slot[:, c, :, :], m.mix1_w1[bass.ds(e, 1), :, :, :].rearrange("o p c f -> p (o c) f")) \
            .then_inc([s.w1_loaded0, s.w1_loaded1][c], 16)
        sp.dma_start(m.w2_slot[:, c, :, :], m.mix1_w2[bass.ds(e, 1), :, :, :].rearrange("o p f d -> p (o f) d")) \
            .then_inc([s.w2_loaded0, s.w2_loaded1][c], 16)

    sp.wait_ge(L.mix0_done, NT * E8)
    weights(0, 0)
    weights(1, 1)
    for c, sem in enumerate((s.y_stored0, s.y_stored1)):
        sp.wait_ge(m.norm.chain, 3 * (L.norms + c) + 3)
        sp.dma_start(m.y_rows[c * P:(c + 1) * P, 0:D], m.y[:, c, :]).then_inc(sem, 16)
    with sp.Fori(1, NT // 2) as i:
        for c, sem in enumerate((s.y_stored0, s.y_stored1)):
            t = i * 2 + c
            sp.wait_ge(m.norm.chain, 3 * (L.norms + t) + 3)
            sp.dma_start(m.y_rows[bass.ts(t, P), 0:D], m.y[:, c, :]).then_inc(sem, 16)
    sp.dma_start(out.rearrange("(t p) d -> p t d", p=P),
                 m.x[:, :].rearrange("p (t d) -> p t d", d=D)).then_inc(s.x_stored, 16)
    sp.wait_ge(s.probs_ready, 1)
    sp.dma_start(m.y_rows[:, D:ROW].rearrange("(t p) e -> p t e", p=P),
                 m.combine[:, :].rearrange("p (t e) -> p t e", e=E8)).then_inc(s.probs_stored, 16)
    with sp.Fori(1, E8 // 2) as i:
        for c in range(2):
            sp.wait_ge(s.out_in_psum, (i * 2 + c) * HALVES - HALVES)
            weights(i * 2 + c, c)
    sp.wait_ge(s.scattered, 16 * E8 * HALVES)


def mix1_gpsimd(nc, pool, m, s, out):
    gathered = [s.gathered0, s.gathered1]

    def gather(e):
        c = e % 2
        pool.wait_ge(s.index_ready, e + 1)
        if e >= 2:
            pool.wait_ge(s.xinT_in_psum, e - 1)
            pool.wait_ge(s.out_ready, (e - 1) * HALVES)
        for half in range(HALVES):
            n = e * HALVES + half
            pool.indirect_dma_start(m.xin[:, c, half, :], None, m.y_rows,
                                    bass.IndirectOffsetOnAxis(m.index[:, n:n + 1], 0)).then_inc(gathered[c], 16)

    def scatter(e):
        for half in range(HALVES):
            n = e * HALVES + half
            pool.wait_ge(s.out_ready, n + 1)
            if n:
                pool.wait_ge(s.scattered, 16 * n)
            pool.indirect_dma_start(out, bass.IndirectOffsetOnAxis(m.index[:, n:n + 1], 0),
                                    m.out_rows[:, e % 2, half, :], None, compute_op=ALU.add).then_inc(s.scattered, 16)

    pool.wait_ge(s.y_stored0, 16 * (NT // 2))
    pool.wait_ge(s.y_stored1, 16 * (NT // 2))
    pool.wait_ge(s.probs_stored, 16)
    gather(0)
    gather(1)
    pool.wait_ge(s.x_stored, 16)
    for e in range(E8):
        scatter(e)
        if e + 2 < E8:
            gather(e + 2)


def mix1_tensor(nc, pe, m, s):
    gathered = [s.gathered0, s.gathered1]
    w1_loaded, w2_loaded = [s.w1_loaded0, s.w1_loaded1], [s.w2_loaded0, s.w2_loaded1]

    with pe.Fori(0, TOP_BIT + 1) as r:
        pe.wait_ge(s.compare_ready, r + 1)
        nc.tensor.matmul(m.ring[0][:, 0:E8], m.ones[:, :], m.hits[:, :], start=True,
                         stop=True).then_inc(s.count_in_psum, 1)
    for n in range(2):
        pe.wait_ge(s.marks_ready, n + 1)
        for k, (weight, marks) in enumerate(((m.ones, 0), (m.ones, 1 - n), (m.earlier, 1 - n))):
            last = nc.tensor.matmul(m.ring[0][:, k * P:(k + 1) * P], weight[:, :], m.marks[:, marks, :],
                                    start=True, stop=True)
        last.then_inc(s.ranks_in_psum, 1)

    def index(e, first=False):
        if not first:
            pe.wait_ge(s.index_ready, e)
        for t in range(NT):
            pe.wait_ge(s.onehot_ready, e * NT + t + 1)
            for half in range(HALVES):
                last = nc.tensor.matmul(m.ring[half][:, 0:2], m.onehot[:, t % 4, half * P:(half + 1) * P],
                                        m.token[:, t, :], start=t == 0, stop=t == NT - 1)
            last.then_inc(s.onehot_used, 1)

    index(0, True)
    with pe.Fori(1, E8) as e:
        index(e)

    def transpose_rows(e, c):
        pe.wait_ge(gathered[c], (e - c) * 16 + 32)
        for d in range(DC):
            for half in range(HALVES):
                at = d * CAP + half * P
                last = nc.tensor.transpose(m.ring[0][:, at:at + P], m.xin[:, c, half, d * P:(d + 1) * P],
                                           m.ident[:, :])
        last.then_inc(s.xinT_in_psum, 1)

    def hidden(e, c, first=False):
        pe.wait_ge(w1_loaded[c], (e - c) * 8 + 16)
        pe.wait_ge(s.xinT_ready, e + 1)
        for f in range(FC1):
            n = e * FC1 + f
            if not first or f >= 2:
                pe.wait_ge(s.gelu_done, n - 1)
            for d in range(DC):
                last = nc.tensor.matmul(m.ring[1 + f % 2][:, 0:CAP], m.w1_slot[:, c, d, f * P:(f + 1) * P],
                                        m.xinT[:, d, :], start=d == 0, stop=d == DC - 1)
            last.then_inc(s.h_in_psum, 1)

    def out_rows(e, c, first=False):
        pe.wait_ge(w2_loaded[c], (e - c) * 8 + 16)
        for half in range(HALVES):
            if not first:
                pe.wait_ge(s.out_ready, (e - 1) * HALVES + half + 1)
            for f in range(FC1):
                if half == 0:
                    pe.wait_ge(s.gelu_done, e * FC1 + f + 1)
                last = nc.tensor.matmul(m.scores[:, half * 512:half * 512 + D], m.h1T[:, f, half * P:(half + 1) * P],
                                        m.w2_slot[:, c, f, :], start=f == 0, stop=f == FC1 - 1)
            last.then_inc(s.out_in_psum, 1)

    pe.wait_ge(s.index_ready, E8)
    transpose_rows(0, 0)
    hidden(0, 0, True)
    transpose_rows(1, 1)
    out_rows(0, 0, True)
    with pe.Fori(0, E8 // 2 - 1) as i:
        for c in range(2):
            e = i * 2 + 1 + c
            hidden(e, 1 - c)
            transpose_rows(e + 1, c)
            out_rows(e, 1 - c)
    hidden(E8 - 1, 1)
    out_rows(E8 - 1, 1)


def mix1_scalar(nc, act, m, s):
    act.wait_ge(s.exp_asked, 1)
    nc.scalar.activation(m.combine[:, :], m.combine[:, :], ACT.Exp).then_inc(s.exp_done, 1)

    def rows(e):
        act.wait_ge(s.xinT_in_psum, e + 1)
        nc.scalar.activation(m.xinT[:, :, :], m.ring[0][:, :], ACT.Identity).then_inc(s.xinT_ready, 1)

    def hidden(e):
        for f in range(FC1):
            act.wait_ge(s.h_in_psum, e * FC1 + f + 1)
            nc.scalar.activation(m.h1T[:, f, :], m.ring[1 + f % 2][:, 0:CAP], ACT.Gelu_apprx_tanh,
                                 bias=m.b1[:, bass.ds(e * FC1 + f, 1)]).then_inc(s.gelu_done, 1)

    rows(0)
    with act.Fori(0, E8 - 1) as e:
        hidden(e)
        rows(e + 1)
    hidden(E8 - 1)


def mix1_vector(nc, dve, m, s):
    gathered = [s.gathered0, s.gathered1]

    def expert(e, c, first=False):
        for half in range(HALVES):
            n = e * HALVES + half
            link = Link(dve, s.bias_done, n)
            if not first:
                dve.wait_ge(s.scattered, 16 * n - 48)
            dve.wait_ge(s.out_in_psum, n + 1)
            link(nc.vector.tensor_tensor(m.out_rows[:, c, half, :], m.scores[:, half * 512:half * 512 + D],
                                         m.b2[:, bass.ts(e, D)], ALU.add))
            nc.vector.tensor_scalar(m.out_rows[:, c, half, :], m.out_rows[:, c, half, :],
                                    m.xin[:, c, half, bass.ds(e + D, 1)], None, ALU.mult).then_inc(s.out_ready, 1)

    for e in range(2):
        dve.wait_ge(gathered[e], 32)
        expert(e, e, True)
    with dve.Fori(1, E8 // 2) as i:
        for c in range(2):
            dve.wait_ge(gathered[c], i * 32 + 32)
            expert(i * 2 + c, c)
COL_BIAS = ["c0q", "c0k", "c0v", "c1q", "c1k", "c1v", "s1q", "s1k", "s1v", "zero"]
ROW_BIAS = ["c0o", "s0o", "c1o", "s1o", "gamma", "beta"]
N_COLS = DC * len(COL_BIAS) + FC1 * E8
LAYERS = ["c0", "s0", "c1", "s1"]


def perceiver(nc, x, ctxT, pad, src_mask, proj, cols, rows, small, shapes, mix0_w1, mix0_w2, mix0_router,
              mix1_w1, mix1_w2, mix1_router, mix1_b2, out):
    y_rows = nc.dram_tensor("y_rows", [N, ROW], F32, kind="Internal").ap()
    with ExitStack() as ctx:
        def sb(name, shape, dt=F32):
            return ctx.enter_context(nc.sbuf_tensor(f"sb_{name}", [P, *shape], dt))

        def by_name(stage, names):
            return {n: ctx.enter_context(nc.semaphore(f"{stage}_{n}")) for n in names}

        def sems(stage, names):
            return Named(**by_name(stage, names))

        m = Named(
            x=sb("x", [NT * D]), y=sb("y", [2, D]), z=sb("z", [2, D]), yT=sb("yT", [2, DC, P]),
            stats=sb("stats", [6]), moments=sb("moments", [2]), var_eps=sb("var_eps", [1]), rstd=sb("rstd", [1]),
            carrier=sb("carrier", [5]), drop=sb("drop", [2, S2]), big=sb("big", [1]),
            minus_half=sb("minus_half", [1]), q=sb("q", [DC, P]), qbd=sb("qbd", [BT, NP, P]), K=sb("K", [2, DC, S2]),
            V=sb("V", [2, KT, D]), probs=sb("probs", [2, NP, S2]), pT=sb("pT", [2, 2, KT, P]),
            pT_blocks=sb("pT_blocks", [2, PG, BT, P]), contextT=sb("contextT", [DC, P]), half=sb("half", [DC, S]),
            halves=sb("halves", [DC, BT, S]), neg_max=sb("neg_max", [2, NP]), row_sum=sb("row_sum", [2, NP]),
            row_max=sb("row_max", [NP]), inv_sum=sb("inv_sum", [NP]), tile_max=sb("tile_max", [NP, BT]),
            tile_sum=sb("tile_sum", [NP * BT]), tile_inv=sb("tile_inv", [NP * BT]), ctxT=sb("ctxT", [2, DC, S2]),
            pad=sb("pad", [2, S2], I32), keep=sb("keep", [2, S2]), add_mask=sb("add_mask", [2, S2]),
            mask_part=sb("mask_part", [S2]), src_mask=sb("src_mask", [S2]), proj=sb("proj", [16, DC, D]),
            cols=sb("cols", [N_COLS]), cols4=sb("cols4", [DC * len(COL_BIAS)]), rows=sb("rows", [len(ROW_BIAS), D]),
            s0_row=sb("s0_row", [D]), shapes=sb("shapes", [P + P + E8 + 2 + 2 * S + CAP + 2 * NT]),
            yT_all=sb("yT_all", [NT * D]), router0=sb("router0", [DC, E8]), router1=sb("router1", [DC, E8]),
            small=sb("small", [2, E8]), zero_bias=sb("zero_bias", [E8]), logits=sb("logits", [NT * E8]),
            route=sb("route", [4, NT * E8]), route_col=sb("route_col", [3, NT]), combine=sb("combine", [NT * E8]),
            w1=sb("w1", [E8, DC, D]), w2=sb("w2", [E8, DC, D]), hT=sb("hT", [2, DC, P]),
            threshold=sb("threshold", [E8], I32), bit=sb("bit", [E8], I32), cand=sb("cand", [E8], I32),
            gain=sb("gain", [E8], I32), hits=sb("hits", [E8], BF16), need=sb("need", [E8]),
            marks=sb("marks", [2, NT * E8], BF16), scan0=sb("scan0", [(8 + NT) * E8]),
            scan1=sb("scan1", [(8 + NT) * E8]), slot=sb("slot", [NT * E8]), onehot=sb("onehot", [4, CAP], BF16),
            slots_row=sb("slots_row", [CAP], BF16), token=sb("token", [NT, 2], BF16), ones=sb("ones", [P], BF16),
            earlier=sb("earlier", [P], BF16), index=sb("index", [E8 * HALVES], I32),
            xin=sb("xin", [2, HALVES, ROW]), b2=sb("b2", [E8 * D]),
        )
        m.h1T = m.yT_all[:, 0:FC1 * CAP].rearrange("p (f k) -> p f k", k=CAP)
        m.xinT = m.yT_all[:, FC1 * CAP:(FC1 + DC) * CAP].rearrange("p (d k) -> p d k", k=CAP)
        m.out_rows = m.yT_all[:, (FC1 + DC) * CAP:(FC1 + DC + 4) * CAP].rearrange(
            "p (c h d) -> p c h d", c=2, d=D)
        m.w1_slot = m.w1[:, :, :, :].rearrange("p (c g) d f -> p c (g d f)", c=2).rearrange(
            "p c (d f) -> p c d f", d=DC)
        m.w2_slot = m.w2[:, :, :, :].rearrange("p (c g) d f -> p c (g d f)", c=2).rearrange(
            "p c (f d) -> p c f d", f=FC1)
        m.y_rows, m.mix1_w1, m.mix1_w2 = y_rows, mix1_w1, mix1_w2
        m.b1 = m.cols[:, DC * len(COL_BIAS):]
        m.ring = [ctx.enter_context(nc.psum_tensor(f"ring{n}", [P, 512], F32)) for n in range(3)]
        m.context = ctx.enter_context(nc.psum_tensor("context", [P, 512], F32))
        m.scores = ctx.enter_context(nc.psum_tensor("scores", [P, 4 * 512], F32))
        m.ctxT_dram, m.pad_dram = ctxT.rearrange("(c p) n -> p c n", p=P), pad
        at = [0]

        def shape_part(width):
            at[0] += width
            return m.shapes[:, at[0] - width:at[0]]

        m.ident, m.before, m.order = shape_part(P), shape_part(P), shape_part(E8)
        m.even_head, m.odd_head = shape_part(1), shape_part(1)
        m.causal, m.causal_add = shape_part(S), shape_part(S)
        m.slots_row_f, m.token_f = shape_part(CAP), shape_part(2 * NT)
        m.head = sb("head", [E8])
        m.gamma = m.rows[:, ROW_BIAS.index("gamma"), :]
        m.aux_bias = m.small[:, 0, :]

        load = sems("load", ["x_first", "x_rest", "consts", "proj0", "proj1", "proj2", "proj3", "experts0",
                             "routers", "consts_ready"])

        m.consts_ready = load.consts_ready

        def layer(n, x_ready, x_steps, before, norms, **more):
            name = LAYERS[n]
            wq, wk, wv, wo = (m.proj[:, 4 * n + k, :, :] for k in range(4))

            def col(kind, of=m.cols):
                i = COL_BIAS.index(name + kind if name + kind in COL_BIAS else "zero") * DC
                return of[:, i:i + DC]

            return Named(wq=wq, wk=wk, wv=wv, wo=wo, bq=col("q", m.cols4), bk=col("k"), bv=col("v"),
                         bo=m.s0_row[:, :] if n == 1 else m.rows[:, ROW_BIAS.index(name + "o"), :],
                         weights_loaded=[load.proj0, load.proj1, load.proj2, load.proj3][n],
                         x_ready=x_ready, x_steps=x_steps, before=before, masked=n == 2, causal=n == 3,
                         norms=norms, tile_norms=2 if n == 1 else 1, first=NT if n == 3 else 0, **more)

        m.norm = sems("norm", NORM)
        self_sems = by_name("self", SELF)
        c0, r0, m0 = sems("c0", CROSS), sems("r0", ROUTER), sems("m0", MIX0)
        c1, r1, m1 = sems("c1", CROSS + MASKED), sems("r1", ROUTER), sems("m1", MIX1)
        s0 = Named(**self_sems, **by_name("s0", ["x_done", "soft_chain", "z_chain"]))
        s1 = Named(**self_sems, **by_name("s1", ["x_done", "soft_chain", "shifted"]))
        m.logits1_ready = r1.logits_ready
        m.logits_ready = r0.logits_ready
        C0 = layer(0, None, 1, None, 0, x_first=load.x_first, x_rest=load.x_rest, ctx_free=None)
        S0 = layer(1, c0.x_done, 1, c0.x_done, NT)
        R0 = Named(x_steps=1, norms=3 * NT, router=m.router0, router_bias=m.zero_bias, x_ready=s0.x_done,
                   before=s0.x_done, weights_loaded=load.routers, keep_yT=True, stored=None)
        M0 = Named(experts_loaded=load.experts0)
        C1 = layer(2, m0.x_done, E8, m0.x_done, 4 * NT, ctx_free=c0.v_in_psum)
        S1 = layer(3, c1.x_done, 1, c1.x_done, 5 * NT)
        R1 = Named(x_steps=1, norms=6 * NT, router=m.router1, router_bias=m.small[:, 1, :], x_ready=s1.x_done,
                   before=s1.x_done, weights_loaded=load.routers, keep_yT=False, stored=(m1.y_stored0, m1.y_stored1))
        M1 = Named(mix0_done=m0.x_done, norms=6 * NT)

        block = ctx.enter_context(nc.Block())

        @block.sync
        def _(sp):
            sp.dma_start(m.x[:, 0:D], x[0:P, :]).then_inc(load.x_first, 16)
            sp.dma_start(m.shapes[:, :], shapes[:, 0:m.shapes.shape[1]]).then_inc(load.consts, 16)
            sp.dma_start(m.head[:, :], shapes[:, m.shapes.shape[1]:]).then_inc(load.consts, 16)
            sp.dma_start(m.cols[:, :], cols).then_inc(load.consts, 16)
            sp.dma_start(m.rows[:, :, :], bc(rows[None, :, :], [P, len(ROW_BIAS), D])).then_inc(load.consts, 16)
            sp.dma_start(m.small[:, :, :], bc(small[None, :, :], [P, 2, E8])).then_inc(load.consts, 16)
            sp.dma_start(m.b2[:, :], bc(mix1_b2.rearrange("(o e) d -> o (e d)", o=1), [P, E8 * D])) \
                .then_inc(load.consts, 16)
            for a in range(2):
                sp.dma_start(m.src_mask[a * S:(a + 1) * S, :], src_mask).then_inc(load.consts, 16)
            sp.dma_start(m.proj[:, 0:4, :, :], proj[:, 0:4, :, :]).then_inc(load.proj0, 16)
            sp.dma_start(m.x[:, D:].rearrange("p (t d) -> p t d", d=D),
                         x[P:, :].rearrange("(t p) d -> p t d", p=P)).then_inc(load.x_rest, 16)
            cross_sync(nc, sp, m, C0, c0)
            cross_sync(nc, sp, m, C1, c1)
            mix1_sync(nc, sp, m, M1, m1, out)

        @block.tensor
        def _(pe):
            pe.wait_ge(load.consts_ready, 1)
            cross_tensor(nc, pe, m, C0, c0)
            self_tensor(nc, pe, m, S0, s0)
            router_tensor(nc, pe, m, R0, r0)
            mix0_tensor(nc, pe, m, M0, m0)
            cross_tensor(nc, pe, m, C1, c1)
            self_tensor(nc, pe, m, S1, s1)
            router_tensor(nc, pe, m, R1, r1)
            mix1_tensor(nc, pe, m, m1)

        @block.scalar
        def _(act):
            for n, sem in ((1, load.proj1), (2, load.proj2), (3, load.proj3)):
                act.dma_start(m.proj[:, 4 * n:4 * n + 4, :, :], proj[:, 4 * n:4 * n + 4, :, :]).then_inc(sem, 16)
            act.dma_start(m.router0[:, :, :], mix0_router).then_inc(load.routers, 16)
            act.dma_start(m.router1[:, :, :], mix1_router).then_inc(load.routers, 16)
            act.dma_start(m.w1[:, :, :, :], mix0_w1).then_inc(load.experts0, 16)
            act.dma_start(m.w2[:, :, :, :], mix0_w2).then_inc(load.experts0, 16)
            act.wait_ge(load.consts_ready, 1)
            cross_scalar(nc, act, m, C0, c0)
            self_scalar(nc, act, m, S0, s0)
            router_scalar(nc, act, m, R0, r0)
            mix0_scalar(nc, act, m, M0, m0)
            cross_scalar(nc, act, m, C1, c1)
            self_scalar(nc, act, m, S1, s1)
            router_scalar(nc, act, m, R1, r1)
            mix1_scalar(nc, act, m, m1)

        @block.vector
        def _(dve):
            dve.wait_ge(load.consts, 16 * 8)
            nc.vector.tensor_scalar(m.cols4[:, :], m.cols[:, 0:DC * len(COL_BIAS)], HD ** -0.5, None, ALU.mult)
            nc.vector.memset(m.zero_bias[:, :], 0.0)
            nc.vector.memset(m.pT_blocks[:, :, :, :, :], 0.0)
            nc.vector.memset(m.threshold[:, :], 0)
            nc.vector.memset(m.bit[:, :], 1 << TOP_BIT)
            nc.vector.memset(m.scan0[:, :], 0.0)
            nc.vector.memset(m.scan1[:, :], 0.0)
            nc.vector.memset(m.ones[:, :], 1.0)
            nc.vector.tensor_copy(m.earlier[:, :], m.before)
            nc.vector.tensor_copy(m.slots_row[:, :], m.slots_row_f)
            nc.vector.tensor_copy(m.token[:, :, :], m.token_f)
            nc.vector.memset(m.minus_half[:, :], -0.5)
            nc.vector.memset(m.big[:, :], -NEG_PAD)
            nc.vector.tensor_tensor(m.s0_row[:, :], m.rows[:, ROW_BIAS.index("s0o"), :],
                                    m.rows[:, ROW_BIAS.index("beta"), :], ALU.add).then_inc(load.consts_ready, 1)
            dve.wait_ge(load.consts_ready, 1)
            cross_vector(nc, dve, m, C0, c0)
            self_vector(nc, dve, m, S0, s0)
            router_vector(nc, dve, m, R0, r0)
            mix0_route_vector(nc, dve, m, m0)
            mix0_vector(nc, dve, m, M0, m0)
            cross_vector(nc, dve, m, C1, c1)
            self_vector(nc, dve, m, S1, s1)
            router_vector(nc, dve, m, R1, r1)
            mix1_softmax_vector(nc, dve, m, m1)
            mix1_threshold_vector(nc, dve, m, m1)
            mix1_slots_vector(nc, dve, m, m1)
            mix1_index_vector(nc, dve, m, m1)
            mix1_vector(nc, dve, m, m1)

        @block.gpsimd
        def _(pool):
            pool.wait_ge(load.consts_ready, 1)
            cross_gpsimd(nc, pool, m, C0, c0)
            self_gpsimd(nc, pool, m, S0, s0)
            router_gpsimd(nc, pool, m, R0, r0)
            cross_gpsimd(nc, pool, m, C1, c1)
            self_gpsimd(nc, pool, m, S1, s1)
            router_gpsimd(nc, pool, m, R1, r1)
            mix1_gpsimd(nc, pool, m, m1, out)


def _constants(np):
    p = np.arange(P)
    q, k = np.arange(P)[:, None] % S, np.arange(S)[None, :]
    causal = (k <= q).astype(np.float32)
    return np.concatenate([
        np.eye(P, dtype=np.float32),
        (p[:, None] < p[None, :]).astype(np.float32),
        np.tile(E8 - np.arange(E8, dtype=np.float32), (P, 1)),
        ((p // HD) % 2 == 0).astype(np.float32)[:, None],
        ((p // HD) % 2 == 1).astype(np.float32)[:, None],
        causal,
        np.where(causal == 0, np.float32(NEG_CAUSAL), np.float32(0)),
        np.tile(np.arange(CAP, dtype=np.float32), (P, 1)),
        np.stack(np.broadcast_arrays(P * np.arange(NT)[None, :], p[:, None]), axis=2).reshape(P, 2 * NT),
        (p[:, None] // HD == np.arange(E8)[None, :]).astype(np.float32),
    ], axis=1).astype(np.float32)


def layout(np, i):
    def chunks(w):
        return np.ascontiguousarray(w.reshape(-1, P, w.shape[-1]).transpose(1, 0, 2))

    def col(v):
        return v.reshape(-1, P).T

    qkv = i["L0_attn_W_qkv"]
    proj = [i["L0_xattn_w_q"].T, i["L0_xattn_w_k"].T, i["L0_xattn_w_v"].T, i["L0_xattn_w_o"].T,
            qkv[0:D].T, qkv[D:2 * D].T, qkv[2 * D:].T, i["L0_attn_W_proj"].T,
            i["L1_xattn_Wq"].T, i["L1_xattn_Wk"].T, i["L1_xattn_Wv"].T, i["L1_xattn_Wo"].T,
            i["L1_attn_Wq"], i["L1_attn_Wk"], i["L1_attn_Wv"], i["L1_attn_Wo"]]
    biases = dict(c0q=i["L0_xattn_b_q"], c0k=i["L0_xattn_b_k"], c0v=i["L0_xattn_b_v"], c1q=i["L1_xattn_bq"],
                  c1k=i["L1_xattn_bk"], c1v=i["L1_xattn_bv"], s1q=i["L1_attn_bq"], s1k=i["L1_attn_bk"],
                  s1v=i["L1_attn_bv"], zero=np.zeros(D, np.float32))
    rows = dict(c0o=i["L0_xattn_b_o"], s0o=i["L0_attn_b_proj"], c1o=i["L1_xattn_bo"], s1o=i["L1_attn_bo"],
                gamma=i["L0_attn_ln_gamma"], beta=i["L0_attn_ln_beta"])
    return dict(
        x=i["x"].reshape(N, D),
        ctxT=np.ascontiguousarray(i["ctx_1024"].reshape(B * S2, D).T),
        pad=i["mask_BxS2_ik0"],
        src_mask=i["mask_1x1xSxS2_ff0"].reshape(S, S2),
        proj=np.ascontiguousarray(np.stack([chunks(w) for w in proj], axis=1)),
        cols=np.ascontiguousarray(np.concatenate(
            [col(biases[n]) for n in COL_BIAS] + [col(i["L1_ffn_b1"].reshape(-1))], axis=1)),
        rows=np.stack([rows[n] for n in ROW_BIAS]),
        small=np.stack([i["L0_ffn_auxfree_bias"], i["L1_ffn_bs"]]),
        shapes=_constants(np),
        mix0_w1=np.ascontiguousarray(i["L0_ffn_w1"].transpose(0, 2, 1).reshape(E8, DC, P, D).transpose(2, 0, 1, 3)),
        mix0_w2=np.ascontiguousarray(i["L0_ffn_w2"].transpose(0, 2, 1).reshape(E8, DC, P, D).transpose(2, 0, 1, 3)),
        mix0_router=chunks(i["L0_ffn_router_w"].T),
        mix1_w1=np.ascontiguousarray(i["L1_ffn_W1"].reshape(E8, DC, P, F1).transpose(0, 2, 1, 3)),
        mix1_w2=np.ascontiguousarray(i["L1_ffn_W2"].reshape(E8, FC1, P, D).transpose(0, 2, 1, 3)),
        mix1_router=chunks(i["L1_ffn_Ws"]),
        mix1_b2=i["L1_ffn_b2"],
    )


def kernel(**inputs):
    import numpy as np
    import concourse.bacc as bacc
    from concourse.bass_utils import run_bass_kernel_spmd

    nc = bacc.Bacc("TRN2", target_bir_lowering=False, num_devices=1)
    arrays = layout(np, {k: np.asarray(v) for k, v in inputs.items()})
    args = [nc.dram_tensor(f"in_{n}", a.shape, mybir.dt.from_np(a.dtype), kind="ExternalInput").ap()
            for n, a in arrays.items()]
    out = nc.dram_tensor("out_x", [N, D], F32, kind="ExternalOutput").ap()
    perceiver(nc, *args, out)
    r = run_bass_kernel_spmd(nc, [{f"in_{n}": a for n, a in arrays.items()}], core_ids=[0])
    return r.results[0]["out_x"].reshape(B, S, D)
```

```python
from contextlib import ExitStack

import concourse.bass as bass
from concourse import mybir

F32 = mybir.dt.float32
I32 = mybir.dt.int32
BF16 = mybir.dt.bfloat16
ALU = mybir.AluOpType
ACT = mybir.ActivationFunctionType
AX_X = mybir.AxisListType.X

P = 128
D = 256
DC = D // P
H = 16
HD = D // H
B = 32
S = 64
S2 = 256
KT = S2 // P
N = B * S
NT = N // P
BT = P // S
NP = H // 2
PG = NP // DC
E8 = 8
EPS = 1e-5
NEG_PAD = -1.0e9
NEG_CAUSAL = -1.0e4


class Link:

    def __init__(self, eng, sem, base):
        self.eng, self.sem, self.count = eng, sem, base

    def __call__(self, ins):
        ins.then_inc(self.sem, 1)
        self.count = self.count + 1
        self.eng.wait_ge(self.sem, self.count)


class Named(dict):

    def __getattr__(self, name):
        return self[name]

    def __setattr__(self, name, value):
        self[name] = value


def bc(ap, shape):
    return ap.broadcast_to(shape)


NORM = ["chain", "var_ready", "rstd_ready"]


def norm_vector(nc, dve, m, x_tile, y, n):
    norm_stats_vector(nc, dve, m, x_tile, n)
    norm_out_vector(nc, dve, m, x_tile, y, n)


def norm_stats_vector(nc, dve, m, x_tile, n):
    link = Link(dve, m.norm.chain, 3 * n)
    link(nc.vector.bn_stats(m.stats[:, :], x_tile))
    nc.vector.memset(m.carrier[:, 4:5], 0.0)
    link(nc.vector.bn_aggr(m.moments[:, :], m.stats[:, :]))
    nc.vector.tensor_scalar(m.var_eps[:, :], m.moments[:, 1:2], EPS, None, ALU.add).then_inc(m.norm.var_ready, 1)


def norm_out_vector(nc, dve, m, x_tile, y, n):
    dve.wait_ge(m.norm.rstd_ready, n + 1)
    nc.vector.tensor_scalar(y, x_tile, m.moments[:, 0:1], m.rstd[:, :], ALU.subtract,
                            ALU.mult).then_inc(m.norm.chain, 1)


def norm_gpsimd(nc, pool, m, n):
    pool.wait_ge(m.norm.var_ready, n + 1)
    nc.gpsimd.tensor_tensor(m.rstd[:, :], m.var_eps[:, :], m.minus_half[:, :],
                            ALU.pow).then_inc(m.norm.rstd_ready, 1)


CROSS = ["yT_in_psum", "yT_ready", "q_in_psum", "q_ready", "qbd_ready", "k_in_psum", "k_ready",
                "v_in_psum", "v_ready", "scores_in_psum", "max_ready", "exp_done", "probs_ready",
                "pT_in_psum", "pT_even_ready", "pT_odd_ready", "context_in_psum", "context_ready",
                "out_in_psum", "x_done", "bias_added", "context_chain", "recip_chain", "ctx_loaded0", "ctx_loaded1"]
MASKED = ["pad_loaded0", "pad_loaded1", "keep_ready", "mask_part_ready", "mask_ready", "scores_taken"]
P_SLOT = [2, 0, 1, 2]


def cross_sync(nc, sp, m, L, s, next_to_load=None, more_loads=None):
    ctx_loaded = [s.ctx_loaded0, s.ctx_loaded1]
    pad_loaded = [s.pad_loaded0, s.pad_loaded1] if L.masked else None

    def load(b, c):
        sp.dma_start(m.ctxT[:, c, :, :], m.ctxT_dram[:, :, bass.ts(b, S2)]).then_inc(ctx_loaded[c], 16)
        if L.masked:
            sp.dma_start(m.pad[:, c, :], bc(m.pad_dram[bass.ts(b, 1), :], [P, S2])).then_inc(pad_loaded[c], 16)

    if L.ctx_free is not None:
        sp.wait_ge(L.ctx_free, B)
    def next_loads(t):
        for c in range(BT):
            b = t * BT + c
            sp.wait_ge(s.v_in_psum, b - 1)
            if L.masked:
                sp.wait_ge(s.keep_ready, b - 1)
            load(b, c)

    for c in range(BT):
        load(c, c)
    if next_to_load is not None:
        next_to_load()
    if more_loads is not None:
        next_loads(1)
        more_loads()
        next_loads(2)
    with sp.Fori(1 if more_loads is None else 3, NT) as t:
        next_loads(t)


def cross_tensor(nc, pe, m, L, s):
    ctx_loaded = [s.ctx_loaded0, s.ctx_loaded1]
    pT_ready = [s.pT_even_ready, s.pT_odd_ready]

    def transpose_y(t):
        pe.wait_ge(m.norm.chain, 3 * (L.norms + t) + 3)
        for d in range(DC):
            last = nc.tensor.transpose(m.ring[0][:, d * P:(d + 1) * P], m.y[:, 0, d * P:(d + 1) * P], m.ident[:, :])
        last.then_inc(s.yT_in_psum, 1)

    def query(t):
        pe.wait_ge(s.yT_ready, t + 1)
        for g in range(DC):
            for d in range(DC):
                last = nc.tensor.matmul(m.ring[2][:, g * P:(g + 1) * P], L.wq[:, d, g * P:(g + 1) * P],
                                        m.yT[:, 0, d, :], start=d == 0, stop=d == DC - 1)
        last.then_inc(s.q_in_psum, 1)

    def key(b, c):
        pe.wait_ge(ctx_loaded[c], (b - c) * 8 + 16)
        for g in range(DC):
            for d in range(DC):
                last = nc.tensor.matmul(m.ring[0][:, g * S2:(g + 1) * S2], L.wk[:, d, g * P:(g + 1) * P],
                                        m.ctxT[:, c, d, :], start=d == 0, stop=d == DC - 1)
        last.then_inc(s.k_in_psum, 1)

    def value(b, c):
        for k in range(KT):
            for d in range(DC):
                last = nc.tensor.matmul(m.ring[1][:, k * D:(k + 1) * D], m.ctxT[:, c, d, k * P:(k + 1) * P],
                                        L.wv[:, d, :], start=d == 0, stop=d == DC - 1)
        last.then_inc(s.v_in_psum, 1)

    def scores(b, c, first=False):
        pe.wait_ge(s.k_ready, b + 1)
        pe.wait_ge(s.qbd_ready, b + 1)
        for p in range(NP):
            if p % 2 == 0 and not first:
                pe.wait_ge(s.scores_taken if L.masked else s.exp_done, b * NP - NP + p + 2)
            last = nc.tensor.matmul(m.scores[:, p * S2:(p + 1) * S2], m.qbd[:, c, p, :], m.K[:, c, p // PG, :],
                                    start=True, stop=True)
            if p % 2 == 1:
                last.then_inc(s.scores_in_psum, 1)

    def turn(b, c, r):
        pe.wait_ge(s.probs_ready, b * NP + 2 * r + 2)
        for j in range(2):
            for k in range(KT):
                n = j * KT + k
                last = nc.tensor.transpose(m.ring[P_SLOT[r]][:, n * P:(n + 1) * P],
                                           m.probs[:, c, 2 * r + j, k * P:(k + 1) * P], m.ident[:, :])
        last.then_inc(s.pT_in_psum, 1)

    def product(b, c, r):
        pe.wait_ge(pT_ready[r % 2], b * 2 + r // 2 + 1)
        for p in (2 * r, 2 * r + 1):
            row, g = 32 * (p % PG), p // PG
            for k in range(KT):
                last = nc.tensor.matmul(m.context[row:row + 32, g * P:(g + 1) * P], m.V[:, c, k, 32 * p:32 * p + 32],
                                        m.pT[:, r, p % 2, k, :], start=k == 0, stop=k == KT - 1)
        if r == 3:
            last.then_inc(s.context_in_psum, 1)

    def context(b, c, slot2=None, slot0=None, slot1=None, first=False):
        if slot2:
            pe.wait_ge(*slot2)
        turn(b, c, 0)
        if slot0:
            pe.wait_ge(*slot0)
        turn(b, c, 1)
        if slot1:
            pe.wait_ge(*slot1)
        turn(b, c, 2)
        if not first:
            pe.wait_ge(s.context_ready, b)
        product(b, c, 0)
        turn(b, c, 3)
        product(b, c, 1)
        product(b, c, 2)
        product(b, c, 3)

    def output(t):
        pe.wait_ge(s.context_ready, t * BT + BT)
        for g in range(DC):
            last = nc.tensor.matmul(m.ring[1][:, 0:D], m.contextT[:, g, :], L.wo[:, g, :],
                                    start=g == 0, stop=g == DC - 1)
        last.then_inc(s.out_in_psum, 1)

    def tile(t, first=False, last=False):
        b = t * BT
        scores(b, 0, first)
        key(b + 1, 1)
        value(b, 0)
        if not first:
            context(b - 1, 1, slot0=(s.k_ready, b + 2), slot1=(s.v_ready, b + 1))
        scores(b + 1, 1)
        if not last:
            transpose_y(t + 1)
        if not first:
            output(t - 1)
        if not last:
            query(t + 1)
            key(b + 2, 0)
        pe.wait_ge(*((s.v_ready, 1) if first else (s.x_done, t)))
        value(b + 1, 1)
        if not last:
            context(b, 0, (s.q_ready, t + 2), (s.k_ready, b + 3), (s.v_ready, b + 2), first)
        else:
            context(b, 0, slot1=(s.v_ready, b + 2))

    if L.before is not None:
        pe.wait_ge(L.before, NT * L.x_steps)
    transpose_y(0)
    pe.wait_ge(L.weights_loaded if L.proj_query is None else L.proj_query, 16)
    query(0)
    pe.wait_ge(L.weights_loaded, 16)
    key(0, 0)
    tile(0, first=True)
    with pe.Fori(0, NT // 2 - 1) as i:
        for c in range(2):
            tile(i * 2 + 1 + c)
    tile(NT - 1, last=True)
    context(B - 1, 1)
    output(NT - 1)


def cross_scalar(nc, act, m, L, s):
    def yT(t):
        act.wait_ge(s.yT_in_psum, t + 1)
        nc.scalar.activation(m.yT[:, 0, :, :], m.ring[0][:, 0:D], ACT.Identity).then_inc(s.yT_ready, 1)

    def query(t):
        act.wait_ge(s.q_in_psum, t + 1)
        for g in range(DC):
            last = nc.scalar.activation(m.q[:, g, :], m.ring[2][:, g * P:(g + 1) * P], ACT.Identity,
                                        bias=L.bq[:, g:g + 1], scale=HD ** -0.5)
        last.then_inc(s.q_ready, 1)

    def key(b, c):
        if L.masked:
            return
        act.wait_ge(s.k_in_psum, b + 1)
        for g in range(DC):
            last = nc.scalar.activation(m.K[:, c, g, :], m.ring[0][:, g * S2:(g + 1) * S2], ACT.Identity,
                                        bias=L.bk[:, g:g + 1])
        last.then_inc(s.k_ready, 1)

    def exps(b, c, pairs):
        for p in pairs:
            if L.masked:
                if p % 4 == 0:
                    act.wait_ge(s.max_ready, b * 2 + p // 4 + 1)
                source = m.probs[:, c, p, :]
            else:
                if p % 2 == 0:
                    act.wait_ge(s.max_ready, b * 4 + p // 2 + 1)
                source = m.scores[:, p * S2:(p + 1) * S2]
            nc.scalar.activation(m.probs[:, c, p, :], source, ACT.Exp, bias=m.neg_max[:, c, p:p + 1],
                                 accum_out=m.row_sum[:, c, p:p + 1]).then_inc(s.exp_done, 1)

    def even_turn(b, r):
        act.wait_ge(s.pT_in_psum, b * 4 + r + 1)
        nc.scalar.activation(m.pT[:, r, :, :, :], m.ring[P_SLOT[r]][:, :], ACT.Identity).then_inc(s.pT_even_ready, 1)

    def tile(t, first=False, last=False):
        b = t * BT
        exps(b, 0, range(NP))
        key(b + 1, 1)
        if not first:
            even_turn(b - 1, 0)
            even_turn(b - 1, 2)
        exps(b + 1, 1, range(NP // 2))
        if not last:
            yT(t + 1)
        exps(b + 1, 1, range(NP // 2, NP))
        if not last:
            query(t + 1)
        if not last:
            key(b + 2, 0)
        even_turn(b, 0)
        even_turn(b, 2)

    yT(0)
    query(0)
    key(0, 0)
    tile(0, first=True)
    with act.Fori(0, NT // 2 - 1) as i:
        for c in range(2):
            tile(i * 2 + 1 + c)
    tile(NT - 1, last=True)
    even_turn(B - 1, 0)
    even_turn(B - 1, 2)


def cross_vector(nc, dve, m, L, s):
    def norm_stats(t, first=False):
        if L.x_ready is None:
            dve.wait_ge(L.x_first if first else L.x_rest, 16)
        else:
            dve.wait_ge(L.x_ready, L.x_steps * (t + 1))
        norm_stats_vector(nc, dve, m, m.x[:, bass.ts(t, D)], L.norms + t)

    def norm_out(t, first=False):
        if not first:
            dve.wait_ge(s.yT_in_psum, t)
        norm_out_vector(nc, dve, m, m.x[:, bass.ts(t, D)], m.y[:, 0, :], L.norms + t)

    def keep(b, c):
        dve.wait_ge([s.pad_loaded0, s.pad_loaded1][c], (b - c) * 8 + 16)
        nc.vector.tensor_scalar(m.keep[:, c, :], m.pad[:, c, :], 0.0, None, ALU.not_equal)
        nc.vector.tensor_scalar(m.drop[:, c, :], m.pad[:, c, :], 0.0, -1.0, ALU.not_equal,
                                ALU.add).then_inc(s.keep_ready, 1)

    def key(b, c):
        dve.wait_ge(s.k_in_psum, b + 1)
        dve.wait_ge(s.keep_ready, b + 1)
        for g in range(DC):
            last = nc.vector.scalar_tensor_tensor(m.K[:, c, g, :], m.ring[0][:, g * S2:(g + 1) * S2],
                                                  L.bk[:, g:g + 1], m.keep[:, c, :], ALU.add, ALU.mult)
        last.then_inc(s.k_ready, 1)

    def maxima(b, c):
        if not L.masked:
            for k in range(NP // 2):
                dve.wait_ge(s.scores_in_psum, b * 4 + k + 1)
                bank = m.scores[:, 2 * k * S2:(2 * k + 2) * S2].rearrange("p (j k) -> p j k", j=2)
                nc.vector.tensor_reduce(m.neg_max[:, c, 2 * k:2 * k + 2], bank, AX_X, ALU.max,
                                        negate=True).then_inc(s.max_ready, 1)
            return
        dve.wait_ge(s.mask_ready, b + 1)
        for p in range(NP):
            if p % 2 == 0:
                dve.wait_ge(s.scores_in_psum, b * 4 + p // 2 + 1)
                nc.vector.memset(m.carrier[:, p // 2:p // 2 + 1], 0.0)
            nc.vector.tensor_tensor_reduce(out=m.probs[:, c, p, :], in0=m.scores[:, p * S2:(p + 1) * S2],
                                           in1=m.add_mask[:, c, :], scale=1.0, scalar=-3.0e38, op0=ALU.add,
                                           op1=ALU.max, accum_out=m.row_max[:, p:p + 1]).then_inc(s.scores_taken, 1)
            if p % 4 == 3:
                dve.wait_ge(s.scores_taken, b * NP + p + 1)
                nc.vector.tensor_scalar(m.neg_max[:, c, p - 3:p + 1], m.row_max[:, p - 3:p + 1], -1.0, None,
                                        ALU.mult).then_inc(s.max_ready, 1)

    def value(b, c):
        dve.wait_ge(s.v_in_psum, b + 1)
        nc.vector.tensor_copy(m.V[:, c, :, :], m.ring[1][:, :]).then_inc(s.v_ready, 1)

    def odd_turn(b, r):
        dve.wait_ge(s.pT_in_psum, b * 4 + r + 1)
        nc.vector.tensor_copy(m.pT[:, r, :, :, :], m.ring[P_SLOT[r]][:, :]).then_inc(s.pT_odd_ready, 1)

    def context(b, c):
        link = Link(dve, s.context_chain, b)
        dve.wait_ge(s.context_in_psum, b + 1)
        for g in range(DC):
            part = nc.vector.tensor_scalar(m.half[:, g, :], m.context[:, g * P:g * P + S], m.even_head[:, :],
                                           L.bv[:, g:g + 1], ALU.mult, ALU.add)
        link(part)
        both = m.context[:, 0:D].rearrange("p (g a q) -> p g a q", g=DC, a=2)
        nc.vector.scalar_tensor_tensor(m.contextT[:, :, c * S:(c + 1) * S], both[:, :, 1, :], m.odd_head[:, :],
                                       m.half[:, 0:DC, :], ALU.mult, ALU.add).then_inc(s.context_ready, 1)

    def normalise(b, c):
        dve.wait_ge(s.exp_done, b * NP + NP)
        Link(dve, s.recip_chain, b)(nc.vector.reciprocal(m.inv_sum[:, :], m.row_sum[:, c, :]))
        for p in range(NP):
            nc.vector.tensor_scalar(m.probs[:, c, p, :], m.probs[:, c, p, :], m.inv_sum[:, p:p + 1], None,
                                    ALU.mult).then_inc(s.probs_ready, 1)

    def output(t):
        dve.wait_ge(s.out_in_psum, t + 1)
        dve.wait_ge(s.bias_added, t + 1)
        x = m.x[:, bass.ts(t, D)]
        nc.vector.tensor_tensor(x, m.ring[1][:, 0:D], x, ALU.add).then_inc(s.x_done, 1)

    def tile(t, first=False, last=False):
        b = t * BT
        maxima(b, 0)
        if L.masked:
            keep(b + 1, 1)
        if not first:
            normalise(b - 1, 1)
        if L.masked:
            key(b + 1, 1)
        value(b, 0)
        if not last:
            norm_stats(t + 1)
        if not first:
            odd_turn(b - 1, 1)
            odd_turn(b - 1, 3)
            context(b - 1, 1)
        if not last:
            norm_out(t + 1)
        maxima(b + 1, 1)
        if not first:
            output(t - 1)
        if L.masked and not last:
            keep(b + 2, 0)
        normalise(b, 0)
        if L.masked and not last:
            key(b + 2, 0)
        value(b + 1, 1)
        odd_turn(b, 1)
        odd_turn(b, 3)
        context(b, 0)

    norm_stats(0, first=True)
    norm_out(0, first=True)
    if L.masked:
        keep(0, 0)
        key(0, 0)
    tile(0, first=True)
    with dve.Fori(0, NT // 2 - 1) as i:
        for c in range(2):
            tile(i * 2 + 1 + c)
    tile(NT - 1, last=True)
    normalise(B - 1, 1)
    odd_turn(B - 1, 1)
    odd_turn(B - 1, 3)
    context(B - 1, 1)
    output(NT - 1)


def cross_gpsimd(nc, pool, m, L, s):
    def mask(b, c, first=False):
        if not first:
            pool.wait_ge(s.mask_ready, b)
        pool.wait_ge(s.keep_ready, b + 1)
        nc.gpsimd.tensor_tensor(m.mask_part[:, :], m.drop[:, c, :], bc(m.big[:, 0:1], [P, S2]),
                                ALU.mult).then_inc(s.mask_part_ready, 1)
        pool.wait_ge(s.mask_part_ready, b + 1)
        nc.gpsimd.tensor_tensor(m.add_mask[:, c, :], m.mask_part[:, :], m.src_mask[:, :],
                                ALU.add).then_inc(s.mask_ready, 1)

    def bias(t):
        pool.wait_ge(m.norm.chain, 3 * (L.norms + t) + 3)
        x = m.x[:, bass.ts(t, D)]
        nc.gpsimd.tensor_tensor(x, x, L.bo[:, :], ALU.add).then_inc(s.bias_added, 1)

    def spread(t):
        pool.wait_ge(s.q_ready, t + 1)
        for c in range(BT):
            for g in range(DC):
                q = m.q[:, g:g + 1, c * S:(c + 1) * S]
                last = nc.gpsimd.tensor_tensor(
                    m.qbd[:, c, g * PG:(g + 1) * PG, :].rearrange("p j (a q) -> p (j a) q", a=2),
                    bc(q, [P, H // DC, S]), bc(m.head[:, :, None], [P, H // DC, S]), ALU.mult)
            last.then_inc(s.qbd_ready, 1)

    def tile(t, last=False):
        if L.masked:
            mask(t * BT + 1, 1)
        if not last:
            norm_gpsimd(nc, pool, m, L.norms + t + 1)
            bias(t + 1)
            if L.masked:
                mask(t * BT + 2, 0)
            spread(t + 1)

    norm_gpsimd(nc, pool, m, L.norms)
    if L.masked:
        bias(0)
        mask(0, 0, True)
    spread(0)
    if L.rows is not None:
        pool.wait_ge(L.rows, 16)
        bias(0)
    with pool.Fori(0, NT - 1) as t:
        tile(t)
    if L.masked:
        tile(NT - 1, last=True)
SELF = ["yT_in_psum", "yT_ready", "q_in_psum", "q_ready", "qbd_ready", "k_in_psum", "k_ready",
               "v_in_psum", "v_ready", "scores_in_psum", "scores_taken", "exp_done",
               "inv_ready", "probs_ready", "pT_in_psum", "pT_low_ready", "pT_high_ready", "context_in_psum",
               "context_ready", "out_in_psum", "bias_added", "context_chain", "sum_chain"]


def self_tensor(nc, pe, m, L, s):
    def transpose_y(t, c):
        pe.wait_ge(m.norm.chain, 3 * (L.norms + L.tile_norms * (t + 1)))
        for d in range(DC):
            last = nc.tensor.transpose(m.ring[0][:, d * P:(d + 1) * P], m.y[:, c, d * P:(d + 1) * P], m.ident[:, :])
        last.then_inc(s.yT_in_psum, 1)

    def query(t, c):
        for g in range(DC):
            for d in range(DC):
                last = nc.tensor.matmul(m.ring[1][:, g * P:(g + 1) * P], L.wq[:, d, g * P:(g + 1) * P],
                                        m.yT[:, c, d, :], start=d == 0, stop=d == DC - 1)
        last.then_inc(s.q_in_psum, 1)

    def key(t, c):
        for g in range(DC):
            for d in range(DC):
                last = nc.tensor.matmul(m.ring[0][:, g * P:(g + 1) * P], L.wk[:, d, g * P:(g + 1) * P],
                                        m.yT[:, c, d, :], start=d == 0, stop=d == DC - 1)
        last.then_inc(s.k_in_psum, 1)

    def value(t, c):
        for d in range(DC):
            last = nc.tensor.matmul(m.ring[2][:, 0:D], m.yT[:, c, d, :], L.wv[:, d, :],
                                    start=d == 0, stop=d == DC - 1)
        last.then_inc(s.v_in_psum, 1)

    def scores(t, first=False):
        pe.wait_ge(s.k_ready, L.first + t + 1)
        for c in range(BT):
            pe.wait_ge(s.qbd_ready, (L.first + t) * BT + c + 1)
            if not first:
                pe.wait_ge(s.scores_taken, (L.first + t) * BT + c - 1)
            for p in range(NP):
                n = c * NP + p
                last = nc.tensor.matmul(m.scores[:, n * P:(n + 1) * P], m.qbd[:, c, p, :],
                                        m.K[:, 0, p // PG, 0:P], start=True, stop=True)
            last.then_inc(s.scores_in_psum, 1)

    def turn(t, c, r):
        for j in range(PG):
            last = nc.tensor.transpose(m.ring[r][:, j * P:(j + 1) * P],
                                       m.probs[:, c, (r * PG + j) // 2, (j % 2) * P:(j % 2 + 1) * P], m.ident[:, :])
        last.then_inc(s.pT_in_psum, 1)

    def product(t, c, r):
        pe.wait_ge(s.pT_low_ready, 2 * (L.first + t) + r + 1)
        pe.wait_ge(s.pT_high_ready, 2 * (L.first + t) + r + 1)
        for j in range(PG):
            last = nc.tensor.matmul(m.context[32 * j:32 * j + 32, r * D:(r + 1) * D],
                                    m.V[:, c, 0, 32 * (r * PG + j):32 * (r * PG + j) + 32],
                                    m.pT_blocks[:, r, j, :, :], start=True, stop=True)
        if r == 1:
            last.then_inc(s.context_in_psum, 1)

    def context(t, c, bank1, first=False):
        pe.wait_ge(s.probs_ready, L.first + t + 1)
        turn(t, c, 0)
        pe.wait_ge(*bank1)
        turn(t, c, 1)
        if not first:
            pe.wait_ge(s.context_ready, L.first + t)
        product(t, c, 0)
        product(t, c, 1)

    def output(t):
        pe.wait_ge(s.context_ready, L.first + t + 1)
        for g in range(DC):
            last = nc.tensor.matmul(m.ring[1][:, 0:D], m.contextT[:, g, :], L.wo[:, g, :],
                                    start=g == 0, stop=g == DC - 1)
        last.then_inc(s.out_in_psum, 1)

    def tile(t, c, stage=None):
        scores(t, stage == 0)
        if stage != "last":
            transpose_y(t + 1, 1 - c)
        pe.wait_ge(s.v_ready, L.first + t) if stage != 0 else None
        value(t, c)
        if stage != "last":
            pe.wait_ge(s.yT_ready, L.first + t + 2)
            if stage not in (0, 1):
                pe.wait_ge(s.x_done, t - 1)
            query(t + 1, 1 - c)
        if stage != 0:
            context(t - 1, 1 - c, (s.x_done, t - 1) if stage == "last" else (s.q_ready, L.first + t + 2), stage == 1)
        if stage != "last":
            key(t + 1, 1 - c)
        if stage != 0:
            output(t - 1)

    pe.wait_ge(L.weights_loaded, 16)
    pe.wait_ge(L.before, NT * L.x_steps)
    transpose_y(0, 0)
    pe.wait_ge(s.yT_ready, L.first + 1)
    query(0, 0)
    key(0, 0)
    tile(0, 0, 0)
    tile(1, 1, 1)
    with pe.Fori(1, NT // 2 - 1) as i:
        for c in range(2):
            tile(i * 2 + c, c)
    tile(NT - 2, 0)
    tile(NT - 1, 1, "last")
    context(NT - 1, 1, (s.x_done, NT - 1))
    output(NT - 1)


def self_scalar(nc, act, m, L, s):
    def yT(t, c):
        act.wait_ge(s.yT_in_psum, L.first + t + 1)
        nc.scalar.activation(m.yT[:, c, :, :], m.ring[0][:, 0:D], ACT.Identity).then_inc(s.yT_ready, 1)

    def query(t):
        act.wait_ge(s.q_in_psum, L.first + t + 1)
        for g in range(DC):
            last = nc.scalar.activation(m.q[:, g, :], m.ring[1][:, g * P:(g + 1) * P], ACT.Identity,
                                        bias=L.bq[:, g:g + 1], scale=HD ** -0.5)
        last.then_inc(s.q_ready, 1)

    def key(t):
        act.wait_ge(s.k_in_psum, L.first + t + 1)
        for g in range(DC):
            last = nc.scalar.activation(m.K[:, 0, g, 0:P], m.ring[0][:, g * P:(g + 1) * P], ACT.Identity,
                                        bias=L.bk[:, g:g + 1])
        last.then_inc(s.k_ready, 1)

    def value(t, c):
        act.wait_ge(s.v_in_psum, L.first + t + 1)
        nc.scalar.activation(m.V[:, c, 0, :], m.ring[2][:, 0:D], ACT.Identity).then_inc(s.v_ready, 1)

    def exps(t, c):
        if L.causal:
            act.wait_ge(s.shifted, t + 1)
        else:
            act.wait_ge(s.scores_taken, (L.first + t) * BT + BT)
        nc.scalar.activation(m.probs[:, c, 0:PG, :], m.probs[:, c, 0:PG, :], ACT.Exp).then_inc(s.exp_done, 1)

    def low(t):
        for r in range(2):
            act.wait_ge(s.pT_in_psum, 2 * (L.first + t) + r + 1)
            nc.scalar.activation(m.pT_blocks[0:S, r, :, 0, :], m.ring[r][0:S, :].rearrange("p (j q) -> p j q", j=PG),
                                 ACT.Identity).then_inc(s.pT_low_ready, 1)

    def tile(t, c, stage=None):
        if stage != "last":
            yT(t + 1, 1 - c)
        value(t, c)
        if stage != "last":
            query(t + 1)
        if stage != 0:
            low(t - 1)
        exps(t, c)
        if stage != "last":
            key(t + 1)

    yT(0, 0)
    query(0)
    key(0)
    tile(0, 0, 0)
    with act.Fori(0, NT // 2 - 1) as i:
        for c in range(2):
            tile(i * 2 + 1 + c, 1 - c)
    tile(NT - 1, 1, "last")
    low(NT - 1)


def self_vector(nc, dve, m, L, s):
    def norm(t, c):
        dve.wait_ge(L.x_ready, L.x_steps * (t + 1))
        n = L.norms + L.tile_norms * t
        norm_vector(nc, dve, m, m.x[:, bass.ts(t, D)], m.y[:, c, :], n)
        if L.tile_norms == 2:
            dve.wait_ge(m.norm.chain, 3 * n + 3)
            norm_vector(nc, dve, m, m.y[:, c, :], m.z[:, c, :], n + 1)

    def block(c):
        part = m.scores[:, c * NP * P:(c + 1) * NP * P].rearrange("p (n k) -> p n k", k=P)
        return part[:, :, c * S:(c + 1) * S]

    def softmax(t, c):
        probs = m.probs[:, c, 0:PG, :].rearrange("p a k -> p (a k)").rearrange("p (n b k) -> p n b k", b=BT, k=S)
        link = Link(dve, s.soft_chain, (4 if L.causal else 2) * t)
        for b in range(BT):
            dve.wait_ge(s.scores_in_psum, (L.first + t) * BT + b + 1)
            source = block(b)
            if L.causal:
                link(nc.vector.tensor_tensor(probs[:, :, b, :], source, bc(m.causal[:, None, :], [P, NP, S]), ALU.mult))
                nc.vector.tensor_tensor(probs[:, :, b, :], probs[:, :, b, :],
                                        bc(m.causal_add[:, None, :], [P, NP, S]), ALU.add).then_inc(s.scores_taken, 1)
                dve.wait_ge(s.scores_taken, (L.first + t) * BT + b + 1)
                source = probs[:, :, b, :]
            link(nc.vector.tensor_reduce(m.tile_max[:, :, b], source, AX_X, ALU.max))
            ins = nc.vector.tensor_tensor(probs[:, :, b, :], source, bc(m.tile_max[:, :, b:b + 1], [P, NP, S]),
                                          ALU.subtract)
            if L.causal:
                if b == BT - 1:
                    ins.then_inc(s.shifted, 1)
            else:
                ins.then_inc(s.scores_taken, 1)

    def sums(t, c):
        dve.wait_ge(s.exp_done, L.first + t + 1)
        link = Link(dve, s.sum_chain, L.first + t)
        rows = m.probs[:, c, 0:PG, :].rearrange("p a k -> p (a k)").rearrange("p (n k) -> p n k", k=S)
        link(nc.vector.tensor_reduce(m.tile_sum[:, :], rows, AX_X, ALU.add))
        nc.vector.reciprocal(m.tile_inv[:, :], m.tile_sum[:, :]).then_inc(s.inv_ready, 1)

    def high(t):
        for r in range(2):
            dve.wait_ge(s.pT_in_psum, 2 * (L.first + t) + r + 1)
            nc.vector.tensor_copy(m.pT_blocks[S:P, r, :, 1, :],
                                  m.ring[r][S:P, :].rearrange("p (j q) -> p j q", j=PG)).then_inc(s.pT_high_ready, 1)

    def context(t):
        link = Link(dve, s.context_chain, L.first + t)
        dve.wait_ge(s.context_in_psum, L.first + t + 1)
        for g in range(DC):
            both = m.context[:, g * D:(g + 1) * D].rearrange("p (b a q) -> p b a q", b=BT, a=2)
            part = nc.vector.tensor_scalar(m.halves[:, g, :, :], both[:, :, 0, :], m.even_head[:, :],
                                           L.bv[:, g:g + 1], ALU.mult, ALU.add)
        link(part)
        for g in range(DC):
            both = m.context[:, g * D:(g + 1) * D].rearrange("p (b a q) -> p b a q", b=BT, a=2)
            last = nc.vector.scalar_tensor_tensor(
                m.contextT[:, g, :].rearrange("p (b q) -> p b q", b=BT), both[:, :, 1, :], m.odd_head[:, :],
                m.halves[:, g, :, :], ALU.mult, ALU.add)
        last.then_inc(s.context_ready, 1)

    def output(t):
        dve.wait_ge(s.out_in_psum, L.first + t + 1)
        dve.wait_ge(s.bias_added, L.first + t + 1)
        x = m.x[:, bass.ts(t, D)]
        nc.vector.tensor_tensor(x, m.ring[1][:, 0:D], x, ALU.add).then_inc(s.x_done, 1)

    def tile(t, c, stage=None):
        softmax(t, c)
        if stage != 0:
            high(t - 1)
            context(t - 1)
        sums(t, c)
        if stage not in ("last", "last but one"):
            dve.wait_ge(s.yT_in_psum, L.first + t + 1)
            if L.tile_norms == 2:
                dve.wait_ge(s.bias_added, L.first + t + 1)
            norm(t + 2, c)
        if stage != 0:
            output(t - 1)

    norm(0, 0)
    norm(1, 1)
    tile(0, 0, 0)
    with dve.Fori(0, NT // 2 - 2) as i:
        for c in range(2):
            tile(i * 2 + 1 + c, 1 - c)
    tile(NT - 3, 1)
    tile(NT - 2, 0, "last but one")
    tile(NT - 1, 1, "last")
    high(NT - 1)
    context(NT - 1)
    output(NT - 1)


def self_gpsimd(nc, pool, m, L, s):
    def norm(t):
        for n in range(L.tile_norms):
            norm_gpsimd(nc, pool, m, L.norms + t * L.tile_norms + n)

    def bias(t, c):
        pool.wait_ge(m.norm.chain, 3 * (L.norms + L.tile_norms * (t + 1)))
        x = m.x[:, bass.ts(t, D)]
        if L.tile_norms == 2:
            link = Link(pool, s.z_chain, 2 * t)
            link(nc.gpsimd.tensor_tensor(m.z[:, c, :], m.z[:, c, :], m.gamma[:, :], ALU.mult))
            link(nc.gpsimd.tensor_tensor(m.z[:, c, :], m.z[:, c, :], L.bo[:, :], ALU.add))
            nc.gpsimd.tensor_tensor(x, x, m.z[:, c, :], ALU.add).then_inc(s.bias_added, 1)
        else:
            nc.gpsimd.tensor_tensor(x, x, L.bo[:, :], ALU.add).then_inc(s.bias_added, 1)

    def spread(t):
        pool.wait_ge(s.q_ready, L.first + t + 1)
        for c in range(BT):
            for g in range(DC):
                q = m.q[:, g:g + 1, c * S:(c + 1) * S]
                last = nc.gpsimd.tensor_tensor(
                    m.qbd[:, c, g * PG:(g + 1) * PG, :].rearrange("p j (a q) -> p (j a) q", a=2),
                    bc(q, [P, H // DC, S]), bc(m.head[:, :, None], [P, H // DC, S]), ALU.mult)
            last.then_inc(s.qbd_ready, 1)

    def normalise(t, c):
        pool.wait_ge(s.inv_ready, L.first + t + 1)
        rows = m.probs[:, c, 0:PG, :].rearrange("p a k -> p (a k)").rearrange("p (n k) -> p n k", k=S)
        nc.gpsimd.tensor_tensor(rows, rows, bc(m.tile_inv[:, :, None], [P, NP * BT, S]),
                                ALU.mult).then_inc(s.probs_ready, 1)

    def tile(t, c, stage=None):
        if stage != "last":
            spread(t + 1)
        normalise(t, c)
        if stage not in ("last", "last but one"):
            norm(t + 2)
            bias(t + 2, c)

    norm(0)
    bias(0, 0)
    norm(1)
    bias(1, 1)
    spread(0)
    with pool.Fori(0, NT // 2 - 1) as i:
        for c in range(2):
            tile(i * 2 + c, c)
    tile(NT - 2, 0, "last but one")
    tile(NT - 1, 1, "last")
ROUTER = ["yT_in_psum", "yT_ready", "logits_in_psum", "logits_ready"]


def router_tensor(nc, pe, m, L, s):
    def transpose_y(t, c):
        pe.wait_ge(m.norm.chain, 3 * (L.norms + t) + 3)
        for d in range(DC):
            last = nc.tensor.transpose(m.ring[c][:, d * P:(d + 1) * P], m.y[:, c, d * P:(d + 1) * P], m.ident[:, :])
        last.then_inc(s.yT_in_psum, 1)

    def logits(t, c, first=False):
        pe.wait_ge(s.yT_ready, t + 1)
        if not first:
            pe.wait_ge(s.logits_ready, t)
        for d in range(DC):
            last = nc.tensor.matmul(m.ring[2][:, 0:E8], m.yT[:, c, d, :], L.router[:, d, :],
                                    start=d == 0, stop=d == DC - 1)
        last.then_inc(s.logits_in_psum, 1)

    pe.wait_ge(L.weights_loaded, 32)
    pe.wait_ge(L.before, NT * L.x_steps)
    transpose_y(0, 0)
    transpose_y(1, 1)
    logits(0, 0, True)
    with pe.Fori(0, NT // 2 - 1) as i:
        for c in range(2):
            transpose_y(i * 2 + 2 + c, c)
            logits(i * 2 + 1 + c, 1 - c)
    logits(NT - 1, 1)


def router_scalar(nc, act, m, L, s):
    with act.Fori(0, NT // 2) as i:
        for c in range(2):
            t = i * 2 + c
            act.wait_ge(s.yT_in_psum, t + 1)
            if L.keep_yT:
                nc.scalar.activation(m.yT_all[:, bass.ts(t, D)], m.ring[c][:, 0:D], ACT.Identity)
            nc.scalar.activation(m.yT[:, c, :, :], m.ring[c][:, 0:D], ACT.Identity).then_inc(s.yT_ready, 1)


def router_vector(nc, dve, m, L, s):
    def norm(t, c):
        dve.wait_ge(L.x_ready, L.x_steps * (t + 1))
        if L.stored is not None and not isinstance(t, int):
            dve.wait_ge(L.stored[c], (t - c) * 8)
        norm_vector(nc, dve, m, m.x[:, bass.ts(t, D)], m.y[:, c, :], L.norms + t)

    def logits(t):
        dve.wait_ge(s.logits_in_psum, t + 1)
        nc.vector.tensor_tensor(m.logits[:, bass.ts(t, E8)], m.ring[2][:, 0:E8], L.router_bias[:, :],
                                ALU.add).then_inc(s.logits_ready, 1)

    norm(0, 0)
    norm(1, 1)
    with dve.Fori(1, NT // 2) as i:
        for c in range(2):
            t = i * 2 + c
            dve.wait_ge(s.yT_in_psum, t - 1)
            norm(t, c)
            logits(t - 2)
    logits(NT - 2)
    logits(NT - 1)


def router_gpsimd(nc, pool, m, L, s):
    with pool.Fori(0, NT) as t:
        norm_gpsimd(nc, pool, m, L.norms + t)


MIX0 = ["route_chain", "exp_asked", "exp_done", "combine_ready", "h_in_psum", "gelu_done", "out_in_psum", "x_done"]


def mix0_route_vector(nc, dve, m, s):
    link = Link(dve, s.route_chain, 0)
    v = nc.vector
    grid = [P, NT, E8]
    logits = m.logits[:, :].rearrange("p (t e) -> p t e", e=E8)
    biased, hit, best0, best1 = (m.route[:, n, :].rearrange("p (t e) -> p t e", e=E8) for n in range(4))
    top, low, high = m.route_col[:, 0, :], m.route_col[:, 1, :], m.route_col[:, 2, :]
    dve.wait_ge(m.logits_ready, NT)
    link(v.tensor_tensor(biased, logits, bc(m.aux_bias[:, None, :], grid), ALU.add))
    for n, best in enumerate((best0, best1)):
        link(v.tensor_reduce(top, biased, AX_X, ALU.max))
        link(v.tensor_tensor(hit, biased, bc(top[:, :, None], grid), ALU.is_equal))
        link(v.tensor_tensor(hit, hit, bc(m.order[:, None, :], grid), ALU.mult))
        link(v.tensor_reduce(top, hit, AX_X, ALU.max))
        link(v.tensor_tensor(best, hit, bc(top[:, :, None], grid), ALU.is_equal))
        if n == 0:
            link(v.scalar_tensor_tensor(biased, best, -3.0e38, biased, ALU.mult, ALU.add))
    for best, value in ((best0, low), (best1, high)):
        link(v.tensor_tensor(hit, best, logits, ALU.mult))
        link(v.tensor_reduce(value, hit, AX_X, ALU.add))
    link(v.tensor_tensor(top, low, high, ALU.max))
    link(v.tensor_tensor(low, low, top, ALU.subtract))
    v.tensor_tensor(high, high, top, ALU.subtract).then_inc(s.exp_asked, 1)
    dve.wait_ge(s.exp_done, 1)
    link(v.tensor_tensor(top, low, high, ALU.add))
    link(v.reciprocal(top, top))
    link(v.tensor_tensor(low, low, top, ALU.mult))
    link(v.tensor_tensor(high, high, top, ALU.mult))
    link(v.tensor_tensor(best0, best0, bc(low[:, :, None], grid), ALU.mult))
    link(v.tensor_tensor(best1, best1, bc(high[:, :, None], grid), ALU.mult))
    v.tensor_tensor(m.combine[:, :].rearrange("p (t e) -> p t e", e=E8), best0, best1,
                    ALU.add).then_inc(s.combine_ready, 1)


def mix0_tensor(nc, pe, m, L, s):
    def hidden(t, e, first):
        n = t * E8 + e
        if not first or e >= 2:
            pe.wait_ge(s.gelu_done, n - 1)
        for f in range(DC):
            for d in range(DC):
                last = nc.tensor.matmul(m.ring[e % 2][:, f * P:(f + 1) * P], m.w1[:, e, d, f * P:(f + 1) * P],
                                        m.yT_all[:, bass.ts(t * DC + d, P)], start=d == 0, stop=d == DC - 1)
        last.then_inc(s.h_in_psum, 1)

    def out(t, e, first):
        n = t * E8 + e
        pe.wait_ge(s.gelu_done, n + 1)
        if not first or e >= 2:
            pe.wait_ge(s.x_done, n - 1)
        for f in range(DC):
            last = nc.tensor.matmul(m.scores[:, (e % 2) * 512:(e % 2) * 512 + D], m.hT[:, e % 2, f, :],
                                    m.w2[:, e, f, :], start=f == 0, stop=f == DC - 1)
        last.then_inc(s.out_in_psum, 1)

    def tile(t, first=False):
        for e in range(E8):
            hidden(t, e, first)
            if e > 0:
                out(t, e - 1, first)
            elif not first:
                out(t - 1, E8 - 1, False)

    pe.wait_ge(L.experts_loaded, 32)
    tile(0, True)
    with pe.Fori(1, NT) as t:
        tile(t)
    out(NT - 1, E8 - 1, False)


def mix0_scalar(nc, act, m, L, s):
    act.wait_ge(s.exp_asked, 1)
    nc.scalar.activation(m.route_col[:, 1:3, :], m.route_col[:, 1:3, :], ACT.Exp).then_inc(s.exp_done, 1)
    with act.Fori(0, NT) as t:
        for e in range(E8):
            act.wait_ge(s.h_in_psum, t * E8 + e + 1)
            nc.scalar.activation(m.hT[:, e % 2, :, :], m.ring[e % 2][:, 0:D], ACT.Gelu).then_inc(s.gelu_done, 1)


def mix0_vector(nc, dve, m, L, s):
    dve.wait_ge(s.combine_ready, 1)
    with dve.Fori(0, NT) as t:
        for e in range(E8):
            n = t * E8 + e
            dve.wait_ge(s.out_in_psum, n + 1)
            if e > 0:
                dve.wait_ge(s.x_done, n)
            x = m.x[:, bass.ts(t, D)]
            nc.vector.scalar_tensor_tensor(x, m.scores[:, (e % 2) * 512:(e % 2) * 512 + D],
                                           m.combine[:, bass.ds(n, 1)], x, ALU.mult, ALU.add).then_inc(s.x_done, 1)


CAP = N // E8
HALVES = CAP // P
F1 = 1024
FC1 = F1 // P
ROW = D + E8
TOP_PAIR = 28
SEARCH_STEPS = 5
SEARCH_LOOPS = (TOP_PAIR // 2 + 1) // SEARCH_STEPS
MIX1 = ["soft_chain", "exp_asked", "exp_done", "probs_ready", "cand_chain", "compare_ready", "count_in_psum",
        "pick_chain", "marks_ready", "ranks_in_psum", "slots_ready", "onehot_ready", "onehot_used", "index_ready",
        "y_stored0", "y_stored1", "probs_stored", "x_stored", "gathered0", "gathered1", "xinT_in_psum",
        "xinT_ready", "gate_ready",
        "h_in_psum", "gelu_done", "out_in_psum", "bias_done", "out_ready", "w1_loaded0", "w1_loaded1", "w2_loaded0",
        "w2_loaded1", "scattered"]


def mix1_softmax_vector(nc, dve, m, s):
    link = Link(dve, s.soft_chain, 0)
    v = nc.vector
    grid = [P, NT, E8]
    logits = m.logits[:, :].rearrange("p (t e) -> p t e", e=E8)
    probs = m.combine[:, :].rearrange("p (t e) -> p t e", e=E8)
    col = m.route_col[:, 0, :]
    dve.wait_ge(m.logits1_ready, NT)
    link(v.tensor_reduce(col, logits, AX_X, ALU.max))
    v.tensor_tensor(probs, logits, bc(col[:, :, None], grid), ALU.subtract).then_inc(s.exp_asked, 1)
    dve.wait_ge(s.exp_done, 1)
    link(v.tensor_reduce(col, probs, AX_X, ALU.add))
    link(v.reciprocal(col, col))
    v.tensor_tensor(probs, probs, bc(col[:, :, None], grid), ALU.mult).then_inc(s.probs_ready, 1)
    dve.wait_ge(s.probs_ready, 1)


def mix1_threshold_vector(nc, dve, m, s):
    v = nc.vector
    grid = [P, 3, NT, E8]
    probs = bc(m.combine[:, :].rearrange("p (o t e) -> p o t e", o=1, e=E8), grid)
    hit = m.hit3[:, :].rearrange("p (g t e) -> p g t e", g=3, e=E8)
    bits, cand, gain = (buf[:, :].rearrange("p (g e) -> p g e", g=3) for buf in (m.bits, m.cand, m.gain))
    with dve.Fori(0, SEARCH_LOOPS) as i:
        for k in range(SEARCH_STEPS):
            r = i * SEARCH_STEPS + k
            link = Link(dve, s.cand_chain, 6 * r)
            link(v.tensor_tensor(cand, bc(m.threshold[:, None, :], [P, 3, E8]), bits, ALU.bitwise_or))
            link(v.tensor_tensor(hit, probs, bc(cand[:, :, None, :].bitcast(F32), grid), ALU.is_ge))
            with nc.allow_low_precision(reason="counts up to NT are exact in bfloat16"):
                v.tensor_reduce(m.hits[:, :].rearrange("p (g e) -> p g e", g=3),
                                hit.rearrange("p g t e -> p g e t"), AX_X, ALU.add).then_inc(s.compare_ready, 1)
            dve.wait_ge(s.count_in_psum, r + 1)
            link(v.scalar_tensor_tensor(gain, m.ring[0][:, 0:3 * E8].rearrange("p (g e) -> p g e", g=3), float(CAP),
                                        bc(bits[:, 0:1, :], [P, 3, E8]), ALU.is_ge, ALU.mult))
            with nc.allow_low_precision(reason="a sum of equal powers of two is exact"):
                link(v.tensor_reduce(m.pair[:, :], gain.rearrange("p g e -> p e g"), AX_X, ALU.add))
            link(v.tensor_tensor(m.threshold[:, :], m.threshold[:, :], m.pair[:, :], ALU.bitwise_or))
            link(v.tensor_scalar(m.bits[:, :], m.bits[:, :], 0.25, None, ALU.mult))


def mix1_slots_vector(nc, dve, m, s):
    link = Link(dve, s.pick_chain, 0)
    v = nc.vector
    grid = [P, NT, E8]
    probs = m.combine[:, :].rearrange("p (t e) -> p t e", e=E8)
    above, equal, taken, place = (m.route[:, n, :] for n in range(4))
    level = bc(m.threshold[:, None, :].bitcast(F32), grid)
    cube = "p (t e) -> p t e"

    def before_tile(total):
        link(v.tensor_copy(m.scan0[:, 9 * E8:], total[:, 0:(NT - 1) * E8]))
        source, target = m.scan0, m.scan1
        for step in (1, 2, 4, 8):
            link(v.tensor_tensor(target[:, 8 * E8:], source[:, 8 * E8:], source[:, (8 - step) * E8:-step * E8],
                                 ALU.add))
            source, target = target, source
        return source[:, 8 * E8:]

    link(v.tensor_tensor(above.rearrange(cube, e=E8), probs, level, ALU.is_gt))
    link(v.tensor_tensor(equal.rearrange(cube, e=E8), probs, level, ALU.is_equal))
    link(v.tensor_copy(m.marks[:, 0, :], above))
    v.tensor_copy(m.marks[:, 1, :], equal).then_inc(s.marks_ready, 1)
    dve.wait_ge(s.ranks_in_psum, 1)
    total_above, total, within = (m.ring[0][:, n * P:(n + 1) * P] for n in range(3))
    link(v.tensor_reduce(m.need[:, :], total_above.rearrange("p (t e) -> p e t", e=E8), AX_X, ALU.add))
    link(v.tensor_scalar(m.need[:, :], m.need[:, :], -1.0, float(CAP), ALU.mult, ALU.add))
    link(v.tensor_tensor(place, within, before_tile(total), ALU.add))
    link(v.tensor_tensor(taken.rearrange(cube, e=E8), place.rearrange(cube, e=E8), bc(m.need[:, None, :], grid),
                         ALU.is_lt))
    link(v.tensor_tensor(taken, taken, equal, ALU.mult))
    link(v.tensor_tensor(taken, taken, above, ALU.add))
    v.tensor_copy(m.marks[:, 0, :], taken).then_inc(s.marks_ready, 1)
    dve.wait_ge(s.ranks_in_psum, 2)
    link(v.tensor_tensor(place, within, before_tile(total), ALU.add))
    link(v.scalar_tensor_tensor(place, place, -1000.0, taken, ALU.add, ALU.mult))
    v.tensor_scalar(m.slot[:, :], place, 1000.0, None, ALU.add).then_inc(s.slots_ready, 1)
    dve.wait_ge(s.slots_ready, 1)


def index_bank(m, half):
    return m.scores[:, (2 + half) * 512:(3 + half) * 512]


def mix1_index_vector(nc, dve, m, s, e, first=False):
    for t in range(NT):
        if not first:
            dve.wait_ge(s.onehot_used, e * NT + t - NT + 1)
        nc.vector.tensor_scalar(m.onehot[:, t, :], m.slots_row[:, :], m.slot[:, bass.ds(e + t * E8, 1)], None,
                                ALU.is_equal).then_inc(s.onehot_ready, 1)
    dve.wait_ge(s.onehot_used, e * NT + NT)
    for half in range(HALVES):
        with nc.allow_low_precision(reason="token indices are whole numbers"):
            last = nc.vector.tensor_reduce(m.index[:, bass.ds(e * HALVES + half, 1)],
                                           index_bank(m, half)[:, 0:2], AX_X, ALU.add)
    last.then_inc(s.index_ready, 1)


def mix1_sync(nc, sp, m, L, s, out):
    def weights(e, c):
        sp.dma_start(m.w1_slot[:, c, :, :], m.mix1_w1[bass.ds(e, 1), :, :, :].rearrange("o p c f -> p (o c) f")) \
            .then_inc([s.w1_loaded0, s.w1_loaded1][c], 16)
        sp.dma_start(m.w2_slot[:, c, :, :], m.mix1_w2[bass.ds(e, 1), :, :, :].rearrange("o p f d -> p (o f) d")) \
            .then_inc([s.w2_loaded0, s.w2_loaded1][c], 16)

    sp.wait_ge(L.mix0_done, NT * E8)
    weights(0, 0)
    weights(1, 1)
    for c, sem in enumerate((s.y_stored0, s.y_stored1)):
        sp.wait_ge(m.norm.chain, 3 * (L.norms + c) + 3)
        sp.dma_start(m.y_rows[c * P:(c + 1) * P, 0:D], m.y[:, c, :]).then_inc(sem, 16)
    with sp.Fori(1, NT // 2) as i:
        for c, sem in enumerate((s.y_stored0, s.y_stored1)):
            t = i * 2 + c
            sp.wait_ge(m.norm.chain, 3 * (L.norms + t) + 3)
            sp.dma_start(m.y_rows[bass.ts(t, P), 0:D], m.y[:, c, :]).then_inc(sem, 16)
    sp.dma_start(out.rearrange("(t p) d -> p t d", p=P),
                 m.x[:, :].rearrange("p (t d) -> p t d", d=D)).then_inc(s.x_stored, 16)
    sp.wait_ge(s.probs_ready, 1)
    sp.dma_start(m.y_rows[:, D:ROW].rearrange("(t p) e -> p t e", p=P),
                 m.combine[:, :].rearrange("p (t e) -> p t e", e=E8)).then_inc(s.probs_stored, 16)
    with sp.Fori(1, E8 // 2) as i:
        for c in range(2):
            sp.wait_ge(s.out_in_psum, (i * 2 + c) * HALVES - HALVES)
            weights(i * 2 + c, c)
    sp.wait_ge(s.scattered, 16 * E8 * HALVES)


def mix1_gpsimd(nc, pool, m, s, out):
    gathered = [s.gathered0, s.gathered1]

    def gather(e):
        c = e % 2
        pool.wait_ge(s.index_ready, e + 1)
        if e >= 2:
            pool.wait_ge(s.gate_ready, e - 1)
        for half in range(HALVES):
            n = e * HALVES + half
            pool.indirect_dma_start(m.xin[:, c, half, :], None, m.y_rows,
                                    bass.IndirectOffsetOnAxis(m.index[:, n:n + 1], 0)).then_inc(gathered[c], 16)

    def scatter(e):
        for half in range(HALVES):
            n = e * HALVES + half
            pool.wait_ge(s.out_ready, n + 1)
            if n:
                pool.wait_ge(s.scattered, 16 * n)
            pool.indirect_dma_start(out, bass.IndirectOffsetOnAxis(m.index[:, n:n + 1], 0),
                                    m.out_rows[:, e % 2, half, :], None, compute_op=ALU.add).then_inc(s.scattered, 16)

    pool.wait_ge(s.y_stored0, 16 * (NT // 2))
    pool.wait_ge(s.y_stored1, 16 * (NT // 2))
    pool.wait_ge(s.probs_stored, 16)
    gather(0)
    gather(1)
    pool.wait_ge(s.x_stored, 16)
    for e in range(E8):
        if e + 2 < E8:
            gather(e + 2)
        scatter(e)


def mix1_tensor(nc, pe, m, s):
    gathered = [s.gathered0, s.gathered1]
    w1_loaded, w2_loaded = [s.w1_loaded0, s.w1_loaded1], [s.w2_loaded0, s.w2_loaded1]

    with pe.Fori(0, SEARCH_LOOPS) as i:
        for k in range(SEARCH_STEPS):
            pe.wait_ge(s.compare_ready, i * SEARCH_STEPS + k + 1)
            nc.tensor.matmul(m.ring[0][:, 0:3 * E8], m.ones[:, :], m.hits[:, :], start=True,
                             stop=True).then_inc(s.count_in_psum, 1)
    for n in range(2):
        pe.wait_ge(s.marks_ready, n + 1)
        for k, (weight, marks) in enumerate(((m.ones, 0), (m.ones, 1 - n), (m.earlier, 1 - n))):
            last = nc.tensor.matmul(m.ring[0][:, k * P:(k + 1) * P], weight[:, :], m.marks[:, marks, :],
                                    start=True, stop=True)
        last.then_inc(s.ranks_in_psum, 1)

    def index(e, first=False):
        if not first:
            pe.wait_ge(s.index_ready, e)
        for t in range(NT):
            pe.wait_ge(s.onehot_ready, e * NT + t + 1)
            for half in range(HALVES):
                last = nc.tensor.matmul(index_bank(m, half)[:, 0:2], m.onehot[:, t, half * P:(half + 1) * P],
                                        m.token[:, t, :], start=t == 0, stop=t == NT - 1)
            last.then_inc(s.onehot_used, 1)

    def transpose_rows(e, c):
        pe.wait_ge(gathered[c], (e - c) * 16 + 32)
        for d in range(DC):
            for half in range(HALVES):
                at = d * CAP + half * P
                last = nc.tensor.transpose(m.ring[0][:, at:at + P], m.xin[:, c, half, d * P:(d + 1) * P],
                                           m.ident[:, :])
        last.then_inc(s.xinT_in_psum, 1)

    def hidden(e, c, first=False):
        pe.wait_ge(w1_loaded[c], (e - c) * 8 + 16)
        pe.wait_ge(s.xinT_ready, e + 1)
        for f in range(FC1):
            n = e * FC1 + f
            if not first or f >= 2:
                pe.wait_ge(s.gelu_done, n - 1)
            for d in range(DC):
                last = nc.tensor.matmul(m.ring[1 + f % 2][:, 0:CAP], m.w1_slot[:, c, d, f * P:(f + 1) * P],
                                        m.xinT[:, d, :], start=d == 0, stop=d == DC - 1)
            last.then_inc(s.h_in_psum, 1)

    def out_rows(e, c, first=False):
        pe.wait_ge(w2_loaded[c], (e - c) * 8 + 16)
        for half in range(HALVES):
            if not first:
                pe.wait_ge(s.out_ready, (e - 1) * HALVES + half + 1)
            for f in range(FC1):
                if half == 0:
                    pe.wait_ge(s.gelu_done, e * FC1 + f + 1)
                last = nc.tensor.matmul(m.scores[:, half * 512:half * 512 + D], m.h1T[:, f, half * P:(half + 1) * P],
                                        m.w2_slot[:, c, f, :], start=f == 0, stop=f == FC1 - 1)
            last.then_inc(s.out_in_psum, 1)

    def expert(e, c, indices=True, first=False):
        if indices:
            index(e + 3)
        hidden(e, c, first)
        if not isinstance(e, int) or e < E8 - 1:
            transpose_rows(e + 1, 1 - c)
        out_rows(e, c, first)

    index(0, True)
    index(1)
    index(2)
    transpose_rows(0, 0)
    expert(0, 0, first=True)
    with pe.Fori(0, 2) as i:
        for c in range(2):
            expert(i * 2 + 1 + c, 1 - c)
    for e in range(5, E8):
        expert(e, e % 2, indices=False)


def mix1_scalar(nc, act, m, s):
    act.wait_ge(s.exp_asked, 1)
    nc.scalar.activation(m.combine[:, :], m.combine[:, :], ACT.Exp).then_inc(s.exp_done, 1)

    def rows(e, c):
        act.wait_ge(s.xinT_in_psum, e + 1)
        nc.scalar.activation(m.xinT[:, :, :], m.ring[0][:, :], ACT.Identity).then_inc(s.xinT_ready, 1)
        if not isinstance(e, int) or e >= 2:
            act.wait_ge(s.out_ready, (e - 1) * HALVES)
        nc.scalar.activation(m.gate[:, c, :], m.xin[:, c, :, bass.ds(e + D, 1)],
                             ACT.Identity).then_inc(s.gate_ready, 1)

    def hidden(e):
        for f in range(FC1):
            act.wait_ge(s.h_in_psum, e * FC1 + f + 1)
            nc.scalar.activation(m.h1T[:, f, :], m.ring[1 + f % 2][:, 0:CAP], ACT.Gelu_apprx_tanh,
                                 bias=m.b1[:, bass.ds(e * FC1 + f, 1)]).then_inc(s.gelu_done, 1)

    rows(0, 0)
    hidden(0)
    rows(1, 1)
    with act.Fori(0, E8 // 2 - 1) as i:
        for c in range(2):
            e = i * 2 + 1 + c
            hidden(e)
            rows(e + 1, c)
    hidden(E8 - 1)


def mix1_vector(nc, dve, m, s):
    def expert(e, c, first=False):
        for half in range(HALVES):
            n = e * HALVES + half
            link = Link(dve, s.bias_done, n)
            if not first:
                dve.wait_ge(s.scattered, 16 * n - 48)
            dve.wait_ge(s.out_in_psum, n + 1)
            link(nc.vector.tensor_tensor(m.out_rows[:, c, half, :], m.scores[:, half * 512:half * 512 + D],
                                         m.b2[:, bass.ts(e, D)], ALU.add))
            nc.vector.tensor_scalar(m.out_rows[:, c, half, :], m.out_rows[:, c, half, :],
                                    m.gate[:, c, half:half + 1], None, ALU.mult).then_inc(s.out_ready, 1)

    mix1_index_vector(nc, dve, m, s, 0, True)
    with dve.Fori(1, 4) as e:
        mix1_index_vector(nc, dve, m, s, e)
    for e in range(4):
        mix1_index_vector(nc, dve, m, s, e + 4)
        dve.wait_ge(s.gate_ready, e + 1)
        expert(e, e % 2, e < 2)
    with dve.Fori(2, E8 // 2) as i:
        for c in range(2):
            dve.wait_ge(s.gate_ready, i * 2 + c + 1)
            expert(i * 2 + c, c)
COL_BIAS = ["c0q", "c0k", "c0v", "c1q", "c1k", "c1v", "s1q", "s1k", "s1v", "zero"]
ROW_BIAS = ["c0o", "s0o", "c1o", "s1o", "gamma", "beta"]
N_COLS = DC * len(COL_BIAS) + FC1 * E8
FIRST_SHAPES = P + P + E8 + 2
LAYERS = ["c0", "s0", "c1", "s1"]


def perceiver(nc, x, ctxT, pad, src_mask, proj, cols, rows, small, shapes, mix0_w1, mix0_w2, mix0_router,
              mix1_w1, mix1_w2, mix1_router, mix1_b2, out):
    y_rows = nc.dram_tensor("y_rows", [N, ROW], F32, kind="Internal").ap()
    with ExitStack() as ctx:
        def sb(name, shape, dt=F32):
            return ctx.enter_context(nc.sbuf_tensor(f"sb_{name}", [P, *shape], dt))

        def by_name(stage, names):
            return {n: ctx.enter_context(nc.semaphore(f"{stage}_{n}")) for n in names}

        def sems(stage, names):
            return Named(**by_name(stage, names))

        m = Named(
            x=sb("x", [NT * D]), y=sb("y", [2, D]), z=sb("z", [2, D]), yT=sb("yT", [2, DC, P]),
            stats=sb("stats", [6]), moments=sb("moments", [2]), var_eps=sb("var_eps", [1]), rstd=sb("rstd", [1]),
            carrier=sb("carrier", [5]), drop=sb("drop", [2, S2]), big=sb("big", [1]),
            table=sb("table", [1]), minus_half=sb("minus_half", [1]), q=sb("q", [DC, P]),
            qbd=sb("qbd", [BT, NP, P]), K=sb("K", [2, DC, S2]),
            V=sb("V", [2, KT, D]), probs=sb("probs", [2, NP, S2]), pT=sb("pT", [4, 2, KT, P]),
            pT_blocks=sb("pT_blocks", [2, PG, BT, P]), contextT=sb("contextT", [DC, P]), half=sb("half", [DC, S]),
            halves=sb("halves", [DC, BT, S]), neg_max=sb("neg_max", [2, NP]), row_sum=sb("row_sum", [2, NP]),
            row_max=sb("row_max", [NP]), inv_sum=sb("inv_sum", [NP]), tile_max=sb("tile_max", [NP, BT]),
            tile_sum=sb("tile_sum", [NP * BT]), tile_inv=sb("tile_inv", [NP * BT]), ctxT=sb("ctxT", [2, DC, S2]),
            pad=sb("pad", [2, S2], I32), keep=sb("keep", [2, S2]), add_mask=sb("add_mask", [2, S2]),
            mask_part=sb("mask_part", [S2]), src_mask=sb("src_mask", [S2]), proj=sb("proj", [16, DC, D]),
            cols=sb("cols", [N_COLS]), cols4=sb("cols4", [DC * len(COL_BIAS)]), rows=sb("rows", [len(ROW_BIAS), D]),
            s0_row=sb("s0_row", [D]), shapes=sb("shapes", [P + P + E8 + 2 + 2 * S + CAP + 2 * NT]),
            yT_all=sb("yT_all", [NT * D]), router0=sb("router0", [DC, E8]), router1=sb("router1", [DC, E8]),
            small=sb("small", [2, E8]), zero_bias=sb("zero_bias", [E8]), logits=sb("logits", [NT * E8]),
            route=sb("route", [4, NT * E8]), route_col=sb("route_col", [3, NT]), combine=sb("combine", [NT * E8]),
            w1=sb("w1", [E8, DC, D]), w2=sb("w2", [E8, DC, D]), hT=sb("hT", [2, DC, P]),
            threshold=sb("threshold", [E8], I32), bits=sb("bits", [3 * E8], I32), cand=sb("cand", [3 * E8], I32),
            gain=sb("gain", [3 * E8]), pair=sb("pair", [E8], I32),
            hits=sb("hits", [3 * E8], BF16), need=sb("need", [E8]),
            marks=sb("marks", [2, NT * E8], BF16), scan0=sb("scan0", [(8 + NT) * E8]),
            scan1=sb("scan1", [(8 + NT) * E8]), slot=sb("slot", [NT * E8]),
            slots_row=sb("slots_row", [CAP], BF16), token=sb("token", [NT, 2], BF16), ones=sb("ones", [P], BF16),
            earlier=sb("earlier", [P], BF16), gate=sb("gate", [2, HALVES]), index=sb("index", [E8 * HALVES], I32),
            xin=sb("xin", [2, HALVES, ROW]), b2=sb("b2", [E8 * D]),
        )
        m.h1T = m.yT_all[:, 0:FC1 * CAP].rearrange("p (f k) -> p f k", k=CAP)
        m.xinT = m.yT_all[:, FC1 * CAP:(FC1 + DC) * CAP].rearrange("p (d k) -> p d k", k=CAP)
        m.out_rows = m.yT_all[:, (FC1 + DC) * CAP:(FC1 + DC + 4) * CAP].rearrange(
            "p (c h d) -> p c h d", c=2, d=D)
        m.w1_slot = m.w1[:, :, :, :].rearrange("p (c g) d f -> p c (g d f)", c=2).rearrange(
            "p c (d f) -> p c d f", d=DC)
        m.w2_slot = m.w2[:, :, :, :].rearrange("p (c g) d f -> p c (g d f)", c=2).rearrange(
            "p c (f d) -> p c f d", f=FC1)
        m.onehot = m.probs[:, 0, :, :].rearrange("p n k -> p (n k)").bitcast(BF16).rearrange("p (t k) -> p t k", k=CAP)
        m.hit3 = m.probs[:, 1, 0:2, :].rearrange("p n k -> p (n k)")[:, 0:3 * NT * E8]
        m.y_rows, m.mix1_w1, m.mix1_w2 = y_rows, mix1_w1, mix1_w2
        m.b1 = m.cols[:, DC * len(COL_BIAS):]
        m.ring = [ctx.enter_context(nc.psum_tensor(f"ring{n}", [P, 512], F32)) for n in range(3)]
        m.context = ctx.enter_context(nc.psum_tensor("context", [P, 512], F32))
        m.scores = ctx.enter_context(nc.psum_tensor("scores", [P, 4 * 512], F32))
        m.ctxT_dram, m.pad_dram = ctxT.rearrange("(c p) n -> p c n", p=P), pad
        at = [0]

        def shape_part(width):
            at[0] += width
            return m.shapes[:, at[0] - width:at[0]]

        m.ident, m.before, m.order = shape_part(P), shape_part(P), shape_part(E8)
        m.even_head, m.odd_head = shape_part(1), shape_part(1)
        m.causal, m.causal_add = shape_part(S), shape_part(S)
        m.slots_row_f, m.token_f = shape_part(CAP), shape_part(2 * NT)
        m.head = sb("head", [E8])
        m.gamma = m.rows[:, ROW_BIAS.index("gamma"), :]
        m.aux_bias = m.small[:, 0, :]

        load = sems("load", ["x_first", "x_rest", "first_consts", "rows", "consts", "proj_query", "proj0", "proj1", "proj2", "proj3",
                             "experts0", "routers", "consts_ready"])

        m.consts_ready = load.consts_ready

        def layer(n, x_ready, x_steps, before, norms, **more):
            name = LAYERS[n]
            wq, wk, wv, wo = (m.proj[:, 4 * n + k, :, :] for k in range(4))

            def col(kind, of=m.cols):
                i = COL_BIAS.index(name + kind if name + kind in COL_BIAS else "zero") * DC
                return of[:, i:i + DC]

            return Named(wq=wq, wk=wk, wv=wv, wo=wo, bq=col("q", m.cols4), bk=col("k"), bv=col("v"),
                         bo=m.s0_row[:, :] if n == 1 else m.rows[:, ROW_BIAS.index(name + "o"), :],
                         weights_loaded=[load.proj0, load.proj1, load.proj2, load.proj3][n],
                         x_ready=x_ready, x_steps=x_steps, before=before, masked=n == 2, causal=n == 3,
                         norms=norms, tile_norms=2 if n == 1 else 1, first=NT if n == 3 else 0, **more)

        m.norm = sems("norm", NORM)
        self_sems = by_name("self", SELF)
        c0, r0, m0 = sems("c0", CROSS), sems("r0", ROUTER), sems("m0", MIX0)
        c1, r1, m1 = sems("c1", CROSS + MASKED), sems("r1", ROUTER), sems("m1", MIX1)
        s0 = Named(**self_sems, **by_name("s0", ["x_done", "soft_chain", "z_chain"]))
        s1 = Named(**self_sems, **by_name("s1", ["x_done", "soft_chain", "shifted"]))
        m.logits1_ready = r1.logits_ready
        m.logits_ready = r0.logits_ready
        C0 = layer(0, None, 1, None, 0, x_first=load.x_first, x_rest=load.x_rest, rows=load.rows,
                   proj_query=load.proj_query,
                   ctx_free=None)
        S0 = layer(1, c0.x_done, 1, c0.x_done, NT)
        R0 = Named(x_steps=1, norms=3 * NT, router=m.router0, router_bias=m.zero_bias, x_ready=s0.x_done,
                   before=s0.x_done, weights_loaded=load.routers, keep_yT=True, stored=None)
        M0 = Named(experts_loaded=load.experts0)
        C1 = layer(2, m0.x_done, E8, m0.x_done, 4 * NT, rows=None, proj_query=None, ctx_free=c0.v_in_psum)
        S1 = layer(3, c1.x_done, 1, c1.x_done, 5 * NT)
        R1 = Named(x_steps=1, norms=6 * NT, router=m.router1, router_bias=m.small[:, 1, :], x_ready=s1.x_done,
                   before=s1.x_done, weights_loaded=load.routers, keep_yT=False, stored=(m1.y_stored0, m1.y_stored1))
        M1 = Named(mix0_done=m0.x_done, norms=6 * NT)

        block = ctx.enter_context(nc.Block())

        @block.sync
        def _(sp):
            sp.dma_start(m.x[:, 0:D], x[0:P, :]).then_inc(load.x_first, 16)
            sp.dma_start(m.shapes[:, 0:FIRST_SHAPES], shapes[:, 0:FIRST_SHAPES]).then_inc(load.first_consts, 16)
            sp.dma_start(m.cols[:, :], cols).then_inc(load.first_consts, 16)
            sp.dma_start(m.head[:, :], shapes[:, m.shapes.shape[1]:]).then_inc(load.first_consts, 16)
            sp.dma_start(m.proj[:, 0:1, :, :], proj[:, 0:1, :, :]).then_inc(load.proj_query, 16)
            sp.dma_start(m.proj[:, 1:4, :, :], proj[:, 1:4, :, :]).then_inc(load.proj0, 16)

            def x_and_bias():
                sp.dma_start(m.rows[:, :, :], bc(rows[None, :, :], [P, len(ROW_BIAS), D])).then_inc(load.rows, 16)
                sp.dma_start(m.x[:, D:].rearrange("p (t d) -> p t d", d=D),
                             x[P:, :].rearrange("(t p) d -> p t d", p=P)).then_inc(load.x_rest, 16)

            def later_loads():
                for n, sem in ((1, load.proj1), (2, load.proj2), (3, load.proj3)):
                    sp.dma_start(m.proj[:, 4 * n:4 * n + 4, :, :], proj[:, 4 * n:4 * n + 4, :, :]).then_inc(sem, 16)
                sp.dma_start(m.shapes[:, FIRST_SHAPES:], shapes[:, FIRST_SHAPES:m.shapes.shape[1]]) \
                    .then_inc(load.consts, 16)
                sp.dma_start(m.small[:, :, :], bc(small[None, :, :], [P, 2, E8])).then_inc(load.consts, 16)
                for a in range(2):
                    sp.dma_start(m.src_mask[a * S:(a + 1) * S, :], src_mask).then_inc(load.consts, 16)
                sp.dma_start(m.router0[:, :, :], mix0_router).then_inc(load.routers, 16)
                sp.dma_start(m.router1[:, :, :], mix1_router).then_inc(load.routers, 16)
                sp.dma_start(m.w1[:, :, :, :], mix0_w1).then_inc(load.experts0, 16)
                sp.dma_start(m.w2[:, :, :, :], mix0_w2).then_inc(load.experts0, 16)
                sp.dma_start(m.b2[:, :], bc(mix1_b2.rearrange("(o e) d -> o (e d)", o=1), [P, E8 * D])) \
                    .then_inc(load.consts, 16)

            cross_sync(nc, sp, m, C0, c0, x_and_bias, later_loads)
            cross_sync(nc, sp, m, C1, c1)
            mix1_sync(nc, sp, m, M1, m1, out)

        @block.tensor
        def _(pe):
            pe.wait_ge(load.consts_ready, 2)
            cross_tensor(nc, pe, m, C0, c0)
            self_tensor(nc, pe, m, S0, s0)
            router_tensor(nc, pe, m, R0, r0)
            mix0_tensor(nc, pe, m, M0, m0)
            cross_tensor(nc, pe, m, C1, c1)
            self_tensor(nc, pe, m, S1, s1)
            router_tensor(nc, pe, m, R1, r1)
            mix1_tensor(nc, pe, m, m1)

        @block.scalar
        def _(act):
            act.wait_ge(load.consts_ready, 1)
            nc.scalar.activation(m.table[:, :], m.zero_bias[:, 0:1], ACT.Exp)
            act.wait_ge(load.consts_ready, 2)
            cross_scalar(nc, act, m, C0, c0)
            self_scalar(nc, act, m, S0, s0)
            router_scalar(nc, act, m, R0, r0)
            mix0_scalar(nc, act, m, M0, m0)
            cross_scalar(nc, act, m, C1, c1)
            self_scalar(nc, act, m, S1, s1)
            router_scalar(nc, act, m, R1, r1)
            mix1_scalar(nc, act, m, m1)

        @block.vector
        def _(dve):
            nc.vector.memset(m.zero_bias[:, :], 0.0).then_inc(load.consts_ready, 1)
            nc.vector.memset(m.minus_half[:, :], -0.5)
            nc.vector.memset(m.big[:, :], -NEG_PAD)
            nc.vector.memset(m.pT_blocks[:, :, :, :, :], 0.0)
            nc.vector.memset(m.threshold[:, :], 0)
            for g in range(3):
                nc.vector.memset(m.bits[:, g * E8:(g + 1) * E8], (g + 1) << TOP_PAIR)
            nc.vector.memset(m.scan0[:, :], 0.0)
            nc.vector.memset(m.scan1[:, :], 0.0)
            nc.vector.memset(m.ones[:, :], 1.0)
            dve.wait_ge(load.first_consts, 16 * 3)
            nc.vector.tensor_scalar(m.cols4[:, :], m.cols[:, 0:DC * len(COL_BIAS)], HD ** -0.5, None,
                                    ALU.mult).then_inc(load.consts_ready, 1)
            dve.wait_ge(load.consts_ready, 2)
            cross_vector(nc, dve, m, C0, c0)
            dve.wait_ge(load.consts, 16 * 5)
            nc.vector.tensor_copy(m.earlier[:, :], m.before)
            nc.vector.tensor_copy(m.slots_row[:, :], m.slots_row_f)
            nc.vector.tensor_copy(m.token[:, :, :], m.token_f)
            nc.vector.tensor_tensor(m.s0_row[:, :], m.rows[:, ROW_BIAS.index("s0o"), :],
                                    m.rows[:, ROW_BIAS.index("beta"), :], ALU.add).then_inc(load.consts_ready, 1)
            dve.wait_ge(load.consts_ready, 3)
            self_vector(nc, dve, m, S0, s0)
            router_vector(nc, dve, m, R0, r0)
            mix0_route_vector(nc, dve, m, m0)
            mix0_vector(nc, dve, m, M0, m0)
            cross_vector(nc, dve, m, C1, c1)
            self_vector(nc, dve, m, S1, s1)
            router_vector(nc, dve, m, R1, r1)
            mix1_softmax_vector(nc, dve, m, m1)
            mix1_threshold_vector(nc, dve, m, m1)
            mix1_slots_vector(nc, dve, m, m1)
            mix1_vector(nc, dve, m, m1)

        @block.gpsimd
        def _(pool):
            pool.wait_ge(load.consts_ready, 2)
            cross_gpsimd(nc, pool, m, C0, c0)
            pool.wait_ge(load.consts_ready, 3)
            self_gpsimd(nc, pool, m, S0, s0)
            router_gpsimd(nc, pool, m, R0, r0)
            cross_gpsimd(nc, pool, m, C1, c1)
            self_gpsimd(nc, pool, m, S1, s1)
            router_gpsimd(nc, pool, m, R1, r1)
            mix1_gpsimd(nc, pool, m, m1, out)


def _constants(np):
    p = np.arange(P)
    q, k = np.arange(P)[:, None] % S, np.arange(S)[None, :]
    causal = (k <= q).astype(np.float32)
    return np.concatenate([
        np.eye(P, dtype=np.float32),
        (p[:, None] < p[None, :]).astype(np.float32),
        np.tile(E8 - np.arange(E8, dtype=np.float32), (P, 1)),
        ((p // HD) % 2 == 0).astype(np.float32)[:, None],
        ((p // HD) % 2 == 1).astype(np.float32)[:, None],
        causal,
        np.where(causal == 0, np.float32(NEG_CAUSAL), np.float32(0)),
        np.tile(np.arange(CAP, dtype=np.float32), (P, 1)),
        np.stack(np.broadcast_arrays(P * np.arange(NT)[None, :], p[:, None]), axis=2).reshape(P, 2 * NT),
        (p[:, None] // HD == np.arange(E8)[None, :]).astype(np.float32),
    ], axis=1).astype(np.float32)


def layout(np, i):
    def chunks(w):
        return np.ascontiguousarray(w.reshape(-1, P, w.shape[-1]).transpose(1, 0, 2))

    def col(v):
        return v.reshape(-1, P).T

    qkv = i["L0_attn_W_qkv"]
    proj = [i["L0_xattn_w_q"].T, i["L0_xattn_w_k"].T, i["L0_xattn_w_v"].T, i["L0_xattn_w_o"].T,
            qkv[0:D].T, qkv[D:2 * D].T, qkv[2 * D:].T, i["L0_attn_W_proj"].T,
            i["L1_xattn_Wq"].T, i["L1_xattn_Wk"].T, i["L1_xattn_Wv"].T, i["L1_xattn_Wo"].T,
            i["L1_attn_Wq"], i["L1_attn_Wk"], i["L1_attn_Wv"], i["L1_attn_Wo"]]
    biases = dict(c0q=i["L0_xattn_b_q"], c0k=i["L0_xattn_b_k"], c0v=i["L0_xattn_b_v"], c1q=i["L1_xattn_bq"],
                  c1k=i["L1_xattn_bk"], c1v=i["L1_xattn_bv"], s1q=i["L1_attn_bq"], s1k=i["L1_attn_bk"],
                  s1v=i["L1_attn_bv"], zero=np.zeros(D, np.float32))
    rows = dict(c0o=i["L0_xattn_b_o"], s0o=i["L0_attn_b_proj"], c1o=i["L1_xattn_bo"], s1o=i["L1_attn_bo"],
                gamma=i["L0_attn_ln_gamma"], beta=i["L0_attn_ln_beta"])
    return dict(
        x=i["x"].reshape(N, D),
        ctxT=np.ascontiguousarray(i["ctx_1024"].reshape(B * S2, D).T),
        pad=i["mask_BxS2_ik0"],
        src_mask=i["mask_1x1xSxS2_ff0"].reshape(S, S2),
        proj=np.ascontiguousarray(np.stack([chunks(w) for w in proj], axis=1)),
        cols=np.ascontiguousarray(np.concatenate(
            [col(biases[n]) for n in COL_BIAS] + [col(i["L1_ffn_b1"].reshape(-1))], axis=1)),
        rows=np.stack([rows[n] for n in ROW_BIAS]),
        small=np.stack([i["L0_ffn_auxfree_bias"], i["L1_ffn_bs"]]),
        shapes=_constants(np),
        mix0_w1=np.ascontiguousarray(i["L0_ffn_w1"].transpose(0, 2, 1).reshape(E8, DC, P, D).transpose(2, 0, 1, 3)),
        mix0_w2=np.ascontiguousarray(i["L0_ffn_w2"].transpose(0, 2, 1).reshape(E8, DC, P, D).transpose(2, 0, 1, 3)),
        mix0_router=chunks(i["L0_ffn_router_w"].T),
        mix1_w1=np.ascontiguousarray(i["L1_ffn_W1"].reshape(E8, DC, P, F1).transpose(0, 2, 1, 3)),
        mix1_w2=np.ascontiguousarray(i["L1_ffn_W2"].reshape(E8, FC1, P, D).transpose(0, 2, 1, 3)),
        mix1_router=chunks(i["L1_ffn_Ws"]),
        mix1_b2=i["L1_ffn_b2"],
    )


def kernel(**inputs):
    import numpy as np
    import concourse.bacc as bacc
    from concourse.bass_utils import run_bass_kernel_spmd

    nc = bacc.Bacc("TRN2", target_bir_lowering=False, num_devices=1)
    arrays = layout(np, {k: np.asarray(v) for k, v in inputs.items()})
    args = [nc.dram_tensor(f"in_{n}", a.shape, mybir.dt.from_np(a.dtype), kind="ExternalInput").ap()
            for n, a in arrays.items()]
    out = nc.dram_tensor("out_x", [N, D], F32, kind="ExternalOutput").ap()
    perceiver(nc, *args, out)
    r = run_bass_kernel_spmd(nc, [{f"in_{n}": a for n, a in arrays.items()}], core_ids=[0])
    return r.results[0]["out_x"].reshape(B, S, D)
```

```python
from contextlib import ExitStack

import concourse.bass as bass
from concourse import mybir

F32 = mybir.dt.float32
I32 = mybir.dt.int32
BF16 = mybir.dt.bfloat16
ALU = mybir.AluOpType
ACT = mybir.ActivationFunctionType
AX_X = mybir.AxisListType.X

P = 128
D = 256
DC = D // P
H = 16
HD = D // H
B = 32
S = 64
S2 = 256
KT = S2 // P
N = B * S
NT = N // P
BT = P // S
NP = H // 2
PG = NP // DC
E8 = 8
EPS = 1e-5
NEG_PAD = -1.0e9
NEG_CAUSAL = -1.0e4


class Link:

    def __init__(self, eng, sem, base):
        self.eng, self.sem, self.count = eng, sem, base

    def count_on(self, ins):
        ins.then_inc(self.sem, 1)
        self.count = self.count + 1

    def __call__(self, ins):
        self.count_on(ins)
        self.eng.wait_ge(self.sem, self.count)


class Named(dict):

    def __getattr__(self, name):
        return self[name]

    def __setattr__(self, name, value):
        self[name] = value


def bc(ap, shape):
    return ap.broadcast_to(shape)


NORM = ["chain", "stats_chain", "rstd_ready", "y_ready", "z_ready"]


def stats_vector(nc, dve, m, chain, n, tile, moments):
    link = Link(dve, chain, 3 * n)
    nc.vector.memset(m.carrier[:, 5:6], 0.0)
    link(nc.vector.bn_stats(m.stats[:, :], tile))
    nc.vector.memset(m.carrier[:, 4:5], 0.0)
    link(nc.vector.bn_aggr(m.mean_var[:, :], m.stats[:, :]))
    nc.vector.tensor_tensor(moments, m.mean_var[:, :], m.zero_eps[:, :], ALU.add).then_inc(chain, 1)


def tile_stats_vector(nc, dve, m, n, t):
    stats_vector(nc, dve, m, m.norm.stats_chain, n, m.x[:, bass.ts(t, D)], m.moments[:, bass.ts(t, 2)])


def rstd_gpsimd(nc, pool, m, stats, first, end):
    both = m.moments[:, :].rearrange("p (t k) -> p t k", k=2)
    pool.wait_ge(m.norm.stats_chain, 3 * (stats - NT + end))
    nc.gpsimd.tensor_tensor(m.rstd[:, first:end], both[:, first:end, 1], bc(m.minus_half[:, :], [P, end - first]),
                            ALU.pow).then_inc(m.norm.rstd_ready, 1)


def y_vector(nc, dve, m, y, t, L):
    if L.rstd_at is None:
        dve.wait_ge(m.norm.rstd_ready, t + 1)
    else:
        dve.wait_ge(m.norm.rstd_ready, L.rstd_at if isinstance(t, int) and t < 2 else L.rstd_rest)
    nc.vector.tensor_scalar(y, m.x[:, bass.ts(t, D)], m.moments[:, bass.ds(t * 2, 1)], m.rstd[:, bass.ds(t, 1)],
                            ALU.subtract, ALU.mult).then_inc(m.norm.y_ready, 1)


def start_vector(nc, dve, m, L):
    for t in range(L.first_norms):
        y_vector(nc, dve, m, m.y[:, t, :], t, L)


CROSS = ["yT_in_psum", "yT_ready", "q_in_psum", "q_ready", "qbd_ready", "k_in_psum", "k_ready", "v_in_psum",
         "v_ready", "scores_in_psum", "max_ready", "exp_done", "probs_ready", "pT_in_psum", "pT_outer_ready",
         "pT_inner_ready", "context_in_psum", "context_ready", "out_in_psum", "x_done", "bias_added",
         "context_chain", "recip_chain", "ctx_loaded0", "ctx_loaded1"]
MASKED = ["pad_loaded0", "pad_loaded1", "keep_ready", "mask_part_ready", "mask_ready", "scores_taken"]
P_SLOT = [2, 0, 1, 2]


def cross_sync(nc, sp, m, L, s, next_to_load=None, more_loads=None):
    ctx_loaded = [s.ctx_loaded0, s.ctx_loaded1]
    pad_loaded = [s.pad_loaded0, s.pad_loaded1] if L.masked else None

    def load_pad(b, c):
        sp.dma_start(m.pad[:, c, :], bc(m.pad_dram[bass.ts(b, 1), :], [P, S2])).then_inc(pad_loaded[c], 16)

    def load_context(b, c):
        sp.dma_start(m.ctxT[:, c, :, :], m.ctxT_dram[:, :, bass.ts(b, S2)]).then_inc(ctx_loaded[c], 16)

    def next_loads(t):
        for c in range(BT):
            b = t * BT + c
            if L.masked:
                sp.wait_ge(s.keep_ready, b - 1)
                load_pad(b, c)
            sp.wait_ge(s.v_in_psum, b - 1)
            load_context(b, c)

    if L.ctx_free is not None:
        sp.wait_ge(L.ctx_free, B)
    for c in range(BT):
        load_context(c, c)
        if L.masked:
            load_pad(c, c)
    if next_to_load is not None:
        next_to_load()
    if more_loads is not None:
        next_loads(1)
        more_loads()
        next_loads(2)
    with sp.Fori(1 if more_loads is None else 3, NT) as t:
        next_loads(t)


def cross_tensor(nc, pe, m, L, s):
    ctx_loaded = [s.ctx_loaded0, s.ctx_loaded1]
    pT_ready = [s.pT_outer_ready, s.pT_inner_ready]

    def transpose_y(t):
        pe.wait_ge(m.norm.y_ready, L.ys + t + 1)
        for d in range(DC):
            last = nc.tensor.transpose(m.ring[0][:, d * P:(d + 1) * P], m.y[:, 0, d * P:(d + 1) * P], m.ident[:, :])
        last.then_inc(s.yT_in_psum, 1)

    def query(t):
        pe.wait_ge(s.yT_ready, t + 1)
        for g in range(DC):
            for d in range(DC):
                last = nc.tensor.matmul(m.ring[2][:, g * P:(g + 1) * P], L.wq[:, d, g * P:(g + 1) * P],
                                        m.yT[:, 0, d, :], start=d == 0, stop=d == DC - 1)
        last.then_inc(s.q_in_psum, 1)

    def key(b, c):
        pe.wait_ge(ctx_loaded[c], (b - c) * 8 + 16)
        for g in range(DC):
            for d in range(DC):
                last = nc.tensor.matmul(m.ring[0][:, g * S2:(g + 1) * S2], L.wk[:, d, g * P:(g + 1) * P],
                                        m.ctxT[:, c, d, :], start=d == 0, stop=d == DC - 1)
        last.then_inc(s.k_in_psum, 1)

    def value(b, c):
        for k in range(KT):
            for d in range(DC):
                last = nc.tensor.matmul(m.ring[1][:, k * D:(k + 1) * D], m.ctxT[:, c, d, k * P:(k + 1) * P],
                                        L.wv[:, d, :], start=d == 0, stop=d == DC - 1)
        last.then_inc(s.v_in_psum, 1)

    def scores(b, c, first=False):
        pe.wait_ge(s.k_ready, b + 1)
        pe.wait_ge(s.qbd_ready, b + 1)
        for p in range(NP):
            if p % 2 == 0 and not first:
                pe.wait_ge(s.scores_taken if L.masked else s.exp_done, b * NP - NP + p + 2)
            last = nc.tensor.matmul(m.scores[:, p * S2:(p + 1) * S2], m.qbd[:, c, p, :], m.K[:, c, p // PG, :],
                                    start=True, stop=True)
            if p % 2 == 1:
                last.then_inc(s.scores_in_psum, 1)

    def turn(b, c, r):
        pe.wait_ge(s.probs_ready, b * NP + 2 * r + 2)
        for j in range(2):
            for k in range(KT):
                n = j * KT + k
                last = nc.tensor.transpose(m.ring[P_SLOT[r]][:, n * P:(n + 1) * P],
                                           m.probs[:, c, 2 * r + j, k * P:(k + 1) * P], m.ident[:, :])
        last.then_inc(s.pT_in_psum, 1)

    def product(b, c, r):
        pe.wait_ge(pT_ready[1 if r in (1, 2) else 0], b * 2 + r // 2 + 1)
        for p in (2 * r, 2 * r + 1):
            row, g = 32 * (p % PG), p // PG
            for k in range(KT):
                last = nc.tensor.matmul(m.context[row:row + 32, g * P:(g + 1) * P], m.V[:, c, k, 32 * p:32 * p + 32],
                                        m.pT[:, r, p % 2, k, :], start=k == 0, stop=k == KT - 1)
        if r == 3:
            last.then_inc(s.context_in_psum, 1)

    def context(b, c, slot2=None, slot0=None, slot1=None, first=False):
        if slot2:
            pe.wait_ge(*slot2)
        turn(b, c, 0)
        if slot0:
            pe.wait_ge(*slot0)
        turn(b, c, 1)
        if slot1:
            pe.wait_ge(*slot1)
        turn(b, c, 2)
        if not first:
            pe.wait_ge(s.context_ready, b)
        product(b, c, 0)
        turn(b, c, 3)
        product(b, c, 1)
        product(b, c, 2)
        product(b, c, 3)

    def output(t):
        pe.wait_ge(s.context_ready, t * BT + BT)
        for g in range(DC):
            last = nc.tensor.matmul(m.ring[1][:, 0:D], m.contextT[:, g, :], L.wo[:, g, :],
                                    start=g == 0, stop=g == DC - 1)
        last.then_inc(s.out_in_psum, 1)

    def tile(t, first=False, last=False):
        b = t * BT
        scores(b, 0, first)
        key(b + 1, 1)
        value(b, 0)
        if not first:
            context(b - 1, 1, slot0=(s.k_ready, b + 2), slot1=(s.v_ready, b + 1))
        scores(b + 1, 1)
        if not last:
            transpose_y(t + 1)
        if not first:
            output(t - 1)
        if not last:
            query(t + 1)
            key(b + 2, 0)
        pe.wait_ge(*((s.v_ready, 1) if first else (s.x_done, t)))
        value(b + 1, 1)
        if not last:
            context(b, 0, (s.q_ready, t + 2), (s.k_ready, b + 3), (s.v_ready, b + 2), first)
        else:
            context(b, 0, slot1=(s.v_ready, b + 2))

    transpose_y(0)
    pe.wait_ge(L.weights_loaded if L.proj_query is None else L.proj_query, 16)
    query(0)
    pe.wait_ge(L.weights_loaded, 16)
    key(0, 0)
    if L.before is not None:
        pe.wait_ge(L.before, NT * L.x_steps)
    tile(0, first=True)
    with pe.Fori(0, NT // 2 - 1) as i:
        for c in range(2):
            tile(i * 2 + 1 + c)
    tile(NT - 1, last=True)
    context(B - 1, 1)
    output(NT - 1)


def cross_scalar(nc, act, m, L, s):
    def yT(t):
        act.wait_ge(s.yT_in_psum, t + 1)
        nc.scalar.activation(m.yT[:, 0, :, :], m.ring[0][:, 0:D], ACT.Identity).then_inc(s.yT_ready, 1)

    def query(t):
        act.wait_ge(s.q_in_psum, t + 1)
        for g in range(DC):
            last = nc.scalar.activation(m.q[:, g, :], m.ring[2][:, g * P:(g + 1) * P], ACT.Identity,
                                        bias=L.bq[:, g:g + 1], scale=HD ** -0.5)
        last.then_inc(s.q_ready, 1)

    def key(b, c):
        if L.masked:
            return
        act.wait_ge(s.k_in_psum, b + 1)
        for g in range(DC):
            last = nc.scalar.activation(m.K[:, c, g, :], m.ring[0][:, g * S2:(g + 1) * S2], ACT.Identity,
                                        bias=L.bk[:, g:g + 1])
        last.then_inc(s.k_ready, 1)

    def exps(b, c, pairs):
        for p in pairs:
            if L.masked:
                if p % 4 == 0:
                    act.wait_ge(s.max_ready, b * 2 + p // 4 + 1)
                source = m.probs[:, c, p, :]
            else:
                if p % 2 == 0:
                    act.wait_ge(s.max_ready, b * 4 + p // 2 + 1)
                source = m.scores[:, p * S2:(p + 1) * S2]
            nc.scalar.activation(m.probs[:, c, p, :], source, ACT.Exp, bias=m.neg_max[:, c, p:p + 1],
                                 accum_out=m.row_sum[:, c, p:p + 1]).then_inc(s.exp_done, 1)

    def outer_turn(b, r):
        act.wait_ge(s.pT_in_psum, b * 4 + r + 1)
        nc.scalar.activation(m.pT[:, r, :, :, :], m.ring[P_SLOT[r]][:, :], ACT.Identity).then_inc(s.pT_outer_ready, 1)

    def tile(t, first=False, last=False):
        b = t * BT
        exps(b, 0, range(NP))
        key(b + 1, 1)
        if not first:
            outer_turn(b - 1, 0)
            outer_turn(b - 1, 3)
        if not last:
            yT(t + 1)
        exps(b + 1, 1, range(NP // 2))
        if not last:
            query(t + 1)
        exps(b + 1, 1, range(NP // 2, NP))
        if not last:
            key(b + 2, 0)
        outer_turn(b, 0)
        outer_turn(b, 3)

    yT(0)
    query(0)
    key(0, 0)
    tile(0, first=True)
    with act.Fori(0, NT // 2 - 1) as i:
        for c in range(2):
            tile(i * 2 + 1 + c)
    tile(NT - 1, last=True)
    outer_turn(B - 1, 0)
    outer_turn(B - 1, 3)


def cross_vector(nc, dve, m, L, s, following):
    def norm_stats(t, first=False):
        if L.rstd_at is None:
            dve.wait_ge(L.x_first if first else L.x_rest, 16)
            stats_vector(nc, dve, m, m.norm.chain, t, m.x[:, bass.ts(t, D)], m.moments[:, bass.ts(t, 2)])

    def norm_out(t, first=False):
        if not first:
            dve.wait_ge(s.yT_in_psum, t)
        y_vector(nc, dve, m, m.y[:, 0, :], t, L)

    def stats(t):
        dve.wait_ge(s.x_done, t + 1)
        tile_stats_vector(nc, dve, m, L.stats + t, t)

    def keep(b, c):
        dve.wait_ge([s.pad_loaded0, s.pad_loaded1][c], (b - c) * 8 + 16)
        nc.vector.tensor_scalar(m.keep[:, c, :], m.pad[:, c, :], 0.0, None, ALU.not_equal)
        nc.vector.tensor_scalar(m.drop[:, c, :], m.pad[:, c, :], 0.0, -1.0, ALU.not_equal,
                                ALU.add).then_inc(s.keep_ready, 1)

    def key(b, c):
        dve.wait_ge(s.k_in_psum, b + 1)
        dve.wait_ge(s.keep_ready, b + 1)
        for g in range(DC):
            last = nc.vector.scalar_tensor_tensor(m.K[:, c, g, :], m.ring[0][:, g * S2:(g + 1) * S2],
                                                  L.bk[:, g:g + 1], m.keep[:, c, :], ALU.add, ALU.mult)
        last.then_inc(s.k_ready, 1)

    def maxima(b, c):
        if not L.masked:
            for k in range(NP // 2):
                dve.wait_ge(s.scores_in_psum, b * 4 + k + 1)
                bank = m.scores[:, 2 * k * S2:(2 * k + 2) * S2].rearrange("p (j k) -> p j k", j=2)
                nc.vector.tensor_reduce(m.neg_max[:, c, 2 * k:2 * k + 2], bank, AX_X, ALU.max,
                                        negate=True).then_inc(s.max_ready, 1)
            return
        dve.wait_ge(s.mask_ready, b + 1)
        for p in range(NP):
            if p % 2 == 0:
                dve.wait_ge(s.scores_in_psum, b * 4 + p // 2 + 1)
                nc.vector.memset(m.carrier[:, p // 2:p // 2 + 1], 0.0)
            nc.vector.tensor_tensor_reduce(out=m.probs[:, c, p, :], in0=m.scores[:, p * S2:(p + 1) * S2],
                                           in1=m.add_mask[:, c, :], scale=1.0, scalar=-3.0e38, op0=ALU.add,
                                           op1=ALU.max, accum_out=m.row_max[:, p:p + 1]).then_inc(s.scores_taken, 1)
            if p % 4 == 3:
                dve.wait_ge(s.scores_taken, b * NP + p + 1)
                nc.vector.tensor_scalar(m.neg_max[:, c, p - 3:p + 1], m.row_max[:, p - 3:p + 1], -1.0, None,
                                        ALU.mult).then_inc(s.max_ready, 1)

    def value(b, c):
        dve.wait_ge(s.v_in_psum, b + 1)
        nc.vector.tensor_copy(m.V[:, c, :, :], m.ring[1][:, :]).then_inc(s.v_ready, 1)

    def inner_turn(b, r):
        dve.wait_ge(s.pT_in_psum, b * 4 + r + 1)
        nc.vector.tensor_copy(m.pT[:, r, :, :, :], m.ring[P_SLOT[r]][:, :]).then_inc(s.pT_inner_ready, 1)

    def context(b, c):
        link = Link(dve, s.context_chain, b)
        dve.wait_ge(s.context_in_psum, b + 1)
        for g in range(DC):
            part = nc.vector.tensor_scalar(m.half[:, g, :], m.context[:, g * P:g * P + S], m.even_head[:, :],
                                           L.bv[:, g:g + 1], ALU.mult, ALU.add)
        link(part)
        both = m.context[:, 0:D].rearrange("p (g a q) -> p g a q", g=DC, a=2)
        nc.vector.scalar_tensor_tensor(m.contextT[:, :, c * S:(c + 1) * S], both[:, :, 1, :], m.odd_head[:, :],
                                       m.half[:, 0:DC, :], ALU.mult, ALU.add).then_inc(s.context_ready, 1)

    def normalise(b, c):
        dve.wait_ge(s.exp_done, b * NP + NP)
        Link(dve, s.recip_chain, b)(nc.vector.reciprocal(m.inv_sum[:, :], m.row_sum[:, c, :]))
        for p in range(NP):
            nc.vector.tensor_scalar(m.probs[:, c, p, :], m.probs[:, c, p, :], m.inv_sum[:, p:p + 1], None,
                                    ALU.mult).then_inc(s.probs_ready, 1)

    def output(t):
        dve.wait_ge(s.out_in_psum, t + 1)
        dve.wait_ge(s.bias_added, t + 1)
        x = m.x[:, bass.ts(t, D)]
        nc.vector.tensor_tensor(x, m.ring[1][:, 0:D], x, ALU.add).then_inc(s.x_done, 1)

    def tile(t, first=False, last=False):
        b = t * BT
        maxima(b, 0)
        if not first:
            normalise(b - 1, 1)
        if L.masked:
            key(b + 1, 1)
        value(b, 0)
        if not first:
            inner_turn(b - 1, 1)
            inner_turn(b - 1, 2)
        if L.masked and not last:
            keep(b + 2, 0)
        if not last:
            norm_stats(t + 1)
        if not first:
            context(b - 1, 1)
        if not last:
            norm_out(t + 1)
        maxima(b + 1, 1)
        if not first:
            output(t - 1)
        normalise(b, 0)
        if L.masked and not last:
            key(b + 2, 0)
        value(b + 1, 1)
        inner_turn(b, 1)
        inner_turn(b, 2)
        if L.masked and not last:
            keep(b + 3, 1)
        if not first:
            stats(t - 1)
        context(b, 0)

    norm_stats(0, first=True)
    if L.rstd_at is None:
        norm_out(0, first=True)
    if L.masked:
        keep(0, 0)
        keep(1, 1)
        key(0, 0)
    tile(0, first=True)
    with dve.Fori(0, NT // 2 - 1) as i:
        for c in range(2):
            tile(i * 2 + 1 + c)
    tile(NT - 1, last=True)
    normalise(B - 1, 1)
    dve.wait_ge(s.yT_in_psum, NT)
    start_vector(nc, dve, m, following)
    inner_turn(B - 1, 1)
    inner_turn(B - 1, 2)
    context(B - 1, 1)
    output(NT - 1)
    stats(NT - 1)


def cross_gpsimd(nc, pool, m, L, s):
    def mask(b, c, first=False):
        if not first:
            pool.wait_ge(s.mask_ready, b)
        pool.wait_ge(s.keep_ready, b + 1)
        nc.gpsimd.tensor_tensor(m.mask_part[:, :], m.drop[:, c, :], bc(m.big[:, 0:1], [P, S2]),
                                ALU.mult).then_inc(s.mask_part_ready, 1)
        pool.wait_ge(s.mask_part_ready, b + 1)
        nc.gpsimd.tensor_tensor(m.add_mask[:, c, :], m.mask_part[:, :], m.src_mask[:, :],
                                ALU.add).then_inc(s.mask_ready, 1)

    def bias(t):
        pool.wait_ge(m.norm.y_ready, L.ys + t + 1)
        x = m.x[:, bass.ts(t, D)]
        nc.gpsimd.tensor_tensor(x, x, L.bo[:, :], ALU.add).then_inc(s.bias_added, 1)

    def spread(t):
        pool.wait_ge(s.q_ready, t + 1)
        for c in range(BT):
            for g in range(DC):
                q = m.q[:, g:g + 1, c * S:(c + 1) * S]
                last = nc.gpsimd.tensor_tensor(
                    m.qbd[:, c, g * PG:(g + 1) * PG, :].rearrange("p j (a q) -> p (j a) q", a=2),
                    bc(q, [P, H // DC, S]), bc(m.head[:, :, None], [P, H // DC, S]), ALU.mult)
            last.then_inc(s.qbd_ready, 1)

    def rstd(t):
        if L.rstd_at is None:
            pool.wait_ge(m.norm.chain, 3 * t + 3)
            nc.gpsimd.tensor_tensor(m.rstd[:, bass.ds(t, 1)], m.moments[:, bass.ds(t * 2 + 1, 1)], m.minus_half[:, :],
                                    ALU.pow).then_inc(m.norm.rstd_ready, 1)

    def tile(t, last=False):
        if L.masked:
            mask(t * BT + 1, 1)
        if not last:
            rstd(t + 1)
            bias(t + 1)
            if L.masked:
                mask(t * BT + 2, 0)
            spread(t + 1)

    if L.rstd_at is None:
        rstd(0)
    else:
        rstd_gpsimd(nc, pool, m, L.stats_before, 0, 2)
    if L.masked:
        bias(0)
        mask(0, 0, True)
    spread(0)
    if L.rstd_at is not None:
        rstd_gpsimd(nc, pool, m, L.stats_before, 2, NT)
    if L.rows is not None:
        pool.wait_ge(L.rows, 16)
        bias(0)
    with pool.Fori(0, NT - 1) as t:
        tile(t)
    if L.masked:
        tile(NT - 1, last=True)
T_SLOT = [2, 0]
SELF = ["yT_in_psum", "yT_ready", "q_in_psum", "q_ready", "qbd_ready", "k_in_psum", "k_ready", "v_in_psum",
        "v_ready", "scores_in_psum", "scores_taken", "exp_done", "inv_ready", "probs_ready", "pT_in_psum",
        "pT_low_ready", "pT_high_ready", "context_in_psum", "context_ready", "out_in_psum", "bias_added",
        "context_chain", "sum_chain"]


def self_tensor(nc, pe, m, L, s):
    def transpose_y(t, c):
        pe.wait_ge(m.norm.y_ready, L.ys + t + 1)
        for d in range(DC):
            last = nc.tensor.transpose(m.ring[0][:, d * P:(d + 1) * P], m.y[:, c, d * P:(d + 1) * P], m.ident[:, :])
        last.then_inc(s.yT_in_psum, 1)

    def query(t, c):
        for g in range(DC):
            for d in range(DC):
                last = nc.tensor.matmul(m.ring[1][:, g * P:(g + 1) * P], L.wq[:, d, g * P:(g + 1) * P],
                                        m.yT[:, c, d, :], start=d == 0, stop=d == DC - 1)
        last.then_inc(s.q_in_psum, 1)

    def key(t, c):
        for g in range(DC):
            for d in range(DC):
                last = nc.tensor.matmul(m.ring[2][:, g * P:(g + 1) * P], L.wk[:, d, g * P:(g + 1) * P],
                                        m.yT[:, c, d, :], start=d == 0, stop=d == DC - 1)
        last.then_inc(s.k_in_psum, 1)

    def value(t, c):
        for d in range(DC):
            last = nc.tensor.matmul(m.ring[0][:, 0:D], m.yT[:, c, d, :], L.wv[:, d, :],
                                    start=d == 0, stop=d == DC - 1)
        last.then_inc(s.v_in_psum, 1)

    def scores(t, c, first=False):
        pe.wait_ge(s.k_ready, L.first + t + 1)
        pe.wait_ge(s.qbd_ready, (L.first + t) * BT + c + 1)
        if not first:
            pe.wait_ge(s.scores_taken, (L.first + t) * BT + c - 1)
        for p in range(NP):
            n = c * NP + p
            last = nc.tensor.matmul(m.scores[:, n * P:(n + 1) * P], m.qbd[:, c, p, :],
                                    m.K[:, 0, p // PG, 0:P], start=True, stop=True)
        last.then_inc(s.scores_in_psum, 1)

    def turn(t, c, r):
        for j in range(PG):
            last = nc.tensor.transpose(m.ring[T_SLOT[r]][:, j * P:(j + 1) * P],
                                       m.probs[:, c, (r * PG + j) // 2, (j % 2) * P:(j % 2 + 1) * P], m.ident[:, :])
        last.then_inc(s.pT_in_psum, 1)

    def product(t, c, r):
        pe.wait_ge(s.pT_low_ready, 2 * (L.first + t) + r + 1)
        pe.wait_ge(s.pT_high_ready, 2 * (L.first + t) + r + 1)
        for j in range(PG):
            last = nc.tensor.matmul(m.context[32 * j:32 * j + 32, r * D:(r + 1) * D],
                                    m.V[:, c, 0, 32 * (r * PG + j):32 * (r * PG + j) + 32],
                                    m.pT_blocks[:, r, j, :, :], start=True, stop=True)
        if r == 1:
            last.then_inc(s.context_in_psum, 1)

    def output(t):
        pe.wait_ge(s.context_ready, L.first + t + 1)
        for g in range(DC):
            last = nc.tensor.matmul(m.ring[1][:, 0:D], m.contextT[:, g, :], L.wo[:, g, :],
                                    start=g == 0, stop=g == DC - 1)
        last.then_inc(s.out_in_psum, 1)

    def tile(t, c, stage=None):
        scores(t, 0, stage == 0)
        if stage not in (0, 1):
            output(t - 2)
        scores(t, 1, stage == 0)
        if stage != "last":
            if stage != 0:
                pe.wait_ge(s.v_ready, L.first + t)
            transpose_y(t + 1, 1 - c)
        if stage != 0:
            pe.wait_ge(s.probs_ready, L.first + t)
            turn(t - 1, 1 - c, 0)
        if stage != "last":
            pe.wait_ge(s.yT_ready, L.first + t + 2)
            if stage not in (0, 1):
                pe.wait_ge(s.x_done, t - 1)
            query(t + 1, 1 - c)
        if stage != 0:
            if stage == "last":
                pe.wait_ge(s.v_ready, L.first + t)
            turn(t - 1, 1 - c, 1)
            if stage != 1:
                pe.wait_ge(s.context_ready, L.first + t - 1)
            product(t - 1, 1 - c, 0)
        if stage != "last":
            key(t + 1, 1 - c)
        if stage != 0:
            product(t - 1, 1 - c, 1)
        value(t, c)

    transpose_y(0, 0)
    pe.wait_ge(L.before, NT * L.x_steps)
    pe.wait_ge(L.weights_loaded, 16)
    pe.wait_ge(s.yT_ready, L.first + 1)
    query(0, 0)
    key(0, 0)
    tile(0, 0, 0)
    tile(1, 1, 1)
    with pe.Fori(1, NT // 2 - 1) as i:
        for c in range(2):
            tile(i * 2 + c, c)
    tile(NT - 2, 0)
    tile(NT - 1, 1, "last")
    output(NT - 2)
    pe.wait_ge(s.probs_ready, L.first + NT)
    turn(NT - 1, 1, 0)
    pe.wait_ge(s.v_ready, L.first + NT)
    turn(NT - 1, 1, 1)
    pe.wait_ge(s.context_ready, L.first + NT - 1)
    product(NT - 1, 1, 0)
    product(NT - 1, 1, 1)
    pe.wait_ge(s.x_done, NT - 1)
    output(NT - 1)


def self_scalar(nc, act, m, L, s):
    def yT(t, c):
        act.wait_ge(s.yT_in_psum, L.first + t + 1)
        nc.scalar.activation(m.yT[:, c, :, :], m.ring[0][:, 0:D], ACT.Identity).then_inc(s.yT_ready, 1)

    def query(t):
        act.wait_ge(s.q_in_psum, L.first + t + 1)
        for g in range(DC):
            last = nc.scalar.activation(m.q[:, g, :], m.ring[1][:, g * P:(g + 1) * P], ACT.Identity,
                                        bias=L.bq[:, g:g + 1], scale=HD ** -0.5)
        last.then_inc(s.q_ready, 1)

    def key(t):
        act.wait_ge(s.k_in_psum, L.first + t + 1)
        for g in range(DC):
            last = nc.scalar.activation(m.K[:, 0, g, 0:P], m.ring[2][:, g * P:(g + 1) * P], ACT.Identity,
                                        bias=L.bk[:, g:g + 1])
        last.then_inc(s.k_ready, 1)

    def value(t, c):
        act.wait_ge(s.v_in_psum, L.first + t + 1)
        nc.scalar.activation(m.V[:, c, 0, :], m.ring[0][:, 0:D], ACT.Identity).then_inc(s.v_ready, 1)

    def exps(t, c):
        if L.causal:
            act.wait_ge(s.shifted, t * BT + BT)
        else:
            act.wait_ge(s.scores_taken, (L.first + t) * BT + BT)
        nc.scalar.activation(m.probs[:, c, 0:PG, :], m.probs[:, c, 0:PG, :], ACT.Exp).then_inc(s.exp_done, 1)

    def low(t, r):
        act.wait_ge(s.pT_in_psum, 2 * (L.first + t) + r + 1)
        nc.scalar.activation(m.pT_blocks[0:S, r, :, 0, :],
                             m.ring[T_SLOT[r]][0:S, :].rearrange("p (j q) -> p j q", j=PG),
                             ACT.Identity).then_inc(s.pT_low_ready, 1)

    def tile(t, c, stage=None):
        if stage != "last":
            yT(t + 1, 1 - c)
        if stage != 0:
            low(t - 1, 0)
        if stage != "last":
            query(t + 1)
        if stage != 0:
            low(t - 1, 1)
        if L.causal and stage != "last":
            key(t + 1)
        exps(t, c)
        if not L.causal and stage != "last":
            key(t + 1)
        value(t, c)

    yT(0, 0)
    query(0)
    key(0)
    tile(0, 0, 0)
    with act.Fori(0, NT // 2 - 1) as i:
        for c in range(2):
            tile(i * 2 + 1 + c, 1 - c)
    tile(NT - 1, 1, "last")
    low(NT - 1, 0)
    low(NT - 1, 1)


def self_vector(nc, dve, m, L, s, following):
    def norm(t, c):
        if not isinstance(t, int) or t >= 2:
            y_vector(nc, dve, m, m.y[:, c, :], t, L)
        if L.normed:
            dve.wait_ge(m.norm.y_ready, L.ys + t + 1)
            stats_vector(nc, dve, m, m.norm.chain, NT + t, m.y[:, c, :], m.z_moments[:, :])

    def norm_out(t, c):
        if L.normed:
            dve.wait_ge(m.norm.rstd_ready, L.rstd_at + t + (1 if isinstance(t, int) and t < 2 else 2))
            nc.vector.tensor_scalar(m.z[:, c, :], m.y[:, c, :], m.z_moments[:, 0:1], m.z_rstd[:, :], ALU.subtract,
                                    ALU.mult).then_inc(m.norm.z_ready, 1)

    def stats(t):
        dve.wait_ge(s.x_done, t + 1)
        tile_stats_vector(nc, dve, m, L.stats + t, t)

    def block(c):
        part = m.scores[:, c * NP * P:(c + 1) * NP * P].rearrange("p (n k) -> p n k", k=P)
        return part[:, :, c * S:(c + 1) * S]

    def shifted(c):
        return m.probs[:, c, 0:PG, :].rearrange("p a k -> p (a k)").rearrange("p (n b k) -> p n b k", b=BT, k=S)

    def keep_causal(t, c, b):
        dve.wait_ge(s.scores_in_psum, (L.first + t) * BT + b + 1)
        nc.vector.tensor_tensor(shifted(c)[:, :, b, :], block(b), bc(m.causal[:, None, :], [P, NP, S]),
                                ALU.mult).then_inc(s.scores_taken, 1)

    def shift(t, c, b):
        if L.causal:
            dve.wait_ge(s.causal_ready, t * BT + b + 1)
            source = shifted(c)[:, :, b, :]
        else:
            dve.wait_ge(s.scores_in_psum, (L.first + t) * BT + b + 1)
            source = block(b)
        link = Link(dve, s.soft_chain, t * BT + b)
        link(nc.vector.tensor_reduce(m.tile_max[:, :, b], source, AX_X, ALU.max))
        nc.vector.tensor_tensor(shifted(c)[:, :, b, :], source, bc(m.tile_max[:, :, b:b + 1], [P, NP, S]),
                                ALU.subtract).then_inc(s.shifted if L.causal else s.scores_taken, 1)

    def sums(t, c):
        dve.wait_ge(s.exp_done, L.first + t + 1)
        link = Link(dve, s.sum_chain, L.first + t)
        rows = m.probs[:, c, 0:PG, :].rearrange("p a k -> p (a k)").rearrange("p (n k) -> p n k", k=S)
        link(nc.vector.tensor_reduce(m.tile_sum[:, :], rows, AX_X, ALU.add))
        nc.vector.reciprocal(m.tile_inv[:, :], m.tile_sum[:, :]).then_inc(s.inv_ready, 1)

    def high(t, r):
        dve.wait_ge(s.pT_in_psum, 2 * (L.first + t) + r + 1)
        nc.vector.tensor_copy(m.pT_blocks[S:P, r, :, 1, :],
                              m.ring[T_SLOT[r]][S:P, :].rearrange("p (j q) -> p j q", j=PG)) \
            .then_inc(s.pT_high_ready, 1)

    def context(t):
        link = Link(dve, s.context_chain, L.first + t)
        dve.wait_ge(s.context_in_psum, L.first + t + 1)
        for g in range(DC):
            both = m.context[:, g * D:(g + 1) * D].rearrange("p (b a q) -> p b a q", b=BT, a=2)
            part = nc.vector.tensor_scalar(m.halves[:, g, :, :], both[:, :, 0, :], m.even_head[:, :],
                                           L.bv[:, g:g + 1], ALU.mult, ALU.add)
        link(part)
        for g in range(DC):
            both = m.context[:, g * D:(g + 1) * D].rearrange("p (b a q) -> p b a q", b=BT, a=2)
            last = nc.vector.scalar_tensor_tensor(
                m.contextT[:, g, :].rearrange("p (b q) -> p b q", b=BT), both[:, :, 1, :], m.odd_head[:, :],
                m.halves[:, g, :, :], ALU.mult, ALU.add)
        last.then_inc(s.context_ready, 1)

    def output(t):
        dve.wait_ge(s.out_in_psum, L.first + t + 1)
        dve.wait_ge(s.bias_added, L.first + t + 1)
        x = m.x[:, bass.ts(t, D)]
        nc.vector.tensor_tensor(x, m.ring[1][:, 0:D], x, ALU.add).then_inc(s.x_done, 1)

    def tile(t, c, stage=None):
        last = stage in ("last", "last but one")
        if L.causal:
            keep_causal(t, c, 0)
        else:
            shift(t, c, 0)
        if stage not in (0, 1):
            output(t - 2)
        if L.causal:
            keep_causal(t, c, 1)
        else:
            shift(t, c, 1)
        if stage != 0:
            high(t - 1, 0)
        if L.causal:
            shift(t, c, 0)
        if stage != 0:
            high(t - 1, 1)
        if L.causal:
            shift(t, c, 1)
        if stage == 0 and L.normed:
            norm_out(1, 1)
        if not last:
            dve.wait_ge(s.yT_in_psum, L.first + t + 1)
            norm(t + 2, c)
        if stage != 0:
            context(t - 1)
        sums(t, c)
        if not last:
            if L.normed:
                dve.wait_ge(s.bias_added, L.first + t + 1)
            norm_out(t + 2, c)
        if stage not in (0, 1):
            stats(t - 2)

    norm(0, 0)
    norm_out(0, 0)
    norm(1, 1)
    if not L.normed:
        norm_out(1, 1)
    tile(0, 0, 0)
    tile(1, 1, 1)
    with dve.Fori(1, NT // 2 - 1) as i:
        for c in range(2):
            tile(i * 2 + c, c)
    tile(NT - 2, 0, "last but one")
    tile(NT - 1, 1, "last")
    output(NT - 2)
    stats(NT - 2)
    dve.wait_ge(s.yT_in_psum, L.first + NT)
    start_vector(nc, dve, m, following)
    high(NT - 1, 0)
    high(NT - 1, 1)
    context(NT - 1)
    output(NT - 1)
    stats(NT - 1)


def self_gpsimd(nc, pool, m, L, s):
    def rstd(t):
        if L.normed:
            pool.wait_ge(m.norm.chain, 3 * (NT + t) + 3)
            nc.gpsimd.tensor_tensor(m.z_rstd[:, :], m.z_moments[:, 1:2], m.minus_half[:, :],
                                    ALU.pow).then_inc(m.norm.rstd_ready, 1)

    def bias(t, c):
        if L.normed:
            pool.wait_ge(m.norm.z_ready, t + 1)
        else:
            pool.wait_ge(m.norm.y_ready, L.ys + t + 1)
        x = m.x[:, bass.ts(t, D)]
        if L.normed:
            link = Link(pool, s.z_chain, 2 * t)
            link(nc.gpsimd.tensor_tensor(m.z[:, c, :], m.z[:, c, :], m.gamma[:, :], ALU.mult))
            link(nc.gpsimd.tensor_tensor(m.z[:, c, :], m.z[:, c, :], L.bo[:, :], ALU.add))
            nc.gpsimd.tensor_tensor(x, x, m.z[:, c, :], ALU.add).then_inc(s.bias_added, 1)
        else:
            nc.gpsimd.tensor_tensor(x, x, L.bo[:, :], ALU.add).then_inc(s.bias_added, 1)

    def spread(t):
        pool.wait_ge(s.q_ready, L.first + t + 1)
        for c in range(BT):
            for g in range(DC):
                q = m.q[:, g:g + 1, c * S:(c + 1) * S]
                last = nc.gpsimd.tensor_tensor(
                    m.qbd[:, c, g * PG:(g + 1) * PG, :].rearrange("p j (a q) -> p (j a) q", a=2),
                    bc(q, [P, H // DC, S]), bc(m.head[:, :, None], [P, H // DC, S]), ALU.mult)
            last.then_inc(s.qbd_ready, 1)

    def normalise(t, c):
        pool.wait_ge(s.inv_ready, L.first + t + 1)
        rows = m.probs[:, c, 0:PG, :].rearrange("p a k -> p (a k)").rearrange("p (n k) -> p n k", k=S)
        nc.gpsimd.tensor_tensor(rows, rows, bc(m.tile_inv[:, :, None], [P, NP * BT, S]),
                                ALU.mult).then_inc(s.probs_ready, 1)

    def causal_add(t, c, b):
        pool.wait_ge(s.scores_taken, (L.first + t) * BT + b + 1)
        part = m.probs[:, c, 0:PG, :].rearrange("p a k -> p (a k)").rearrange("p (n b k) -> p n b k", b=BT, k=S)
        nc.gpsimd.tensor_tensor(part[:, :, b, :], part[:, :, b, :], bc(m.causal_add[:, None, :], [P, NP, S]),
                                ALU.add).then_inc(s.causal_ready, 1)

    def tile(t, c, stage=None):
        if L.causal:
            causal_add(t, c, 0)
            causal_add(t, c, 1)
            if stage != "last":
                bias(t + 1, 1 - c)
        if stage != "last":
            spread(t + 1)
        if stage not in ("last", "last but one"):
            rstd(t + 2)
        normalise(t, c)
        if not L.causal and stage not in ("last", "last but one"):
            bias(t + 2, c)

    rstd_gpsimd(nc, pool, m, L.stats_before, 0, 2)
    if L.normed:
        rstd(0)
        spread(0)
        rstd(1)
        rstd_gpsimd(nc, pool, m, L.stats_before, 2, NT)
        pool.wait_ge(m.consts_ready, 3)
    else:
        rstd_gpsimd(nc, pool, m, L.stats_before, 2, NT)
        spread(0)
    bias(0, 0)
    if not L.causal:
        bias(1, 1)
    with pool.Fori(0, NT // 2 - 1) as i:
        for c in range(2):
            tile(i * 2 + c, c)
    tile(NT - 2, 0, "last but one")
    tile(NT - 1, 1, "last")
ROUTER = ["yT_in_psum", "yT_ready", "logitsT_in_psum", "logitsT_ready", "logits_in_psum", "logits_ready"]
GT = 4
NG = NT // GT


def y_slot(m, c):
    return (m.y if c < 2 else m.z)[:, c % 2, :]


def router_tensor(nc, pe, m, L, s):
    tiles, groups = L.round * NT, L.round * NG

    def transpose_y(t, c):
        pe.wait_ge(m.norm.y_ready, L.ys + t + 1)
        if not isinstance(t, int) or t >= 2:
            pe.wait_ge(s.yT_ready, tiles + t - 1)
        for d in range(DC):
            last = nc.tensor.transpose(m.ring[c % 2][:, d * P:(d + 1) * P], y_slot(m, c)[:, d * P:(d + 1) * P],
                                       m.ident[:, :])
        last.then_inc(s.yT_in_psum, 1)

    def logits(g, first=False):
        pe.wait_ge(s.yT_ready, tiles + (g + 1) * GT)
        if not first:
            pe.wait_ge(s.logitsT_ready, groups + g)
        yT = m.yT_all[:, bass.ts(g, GT * D)].rearrange("p (t d k) -> p t d k", t=GT, d=DC)
        for d in range(DC):
            last = nc.tensor.matmul(m.ring[2][0:E8, :], L.router[:, d, :], yT[:, :, d, :],
                                    start=d == 0, stop=d == DC - 1)
        last.then_inc(s.logitsT_in_psum, 1)

    def group(g):
        transpose_y(g * GT, 0)
        transpose_y(g * GT + 1, 1)
        logits(g - 1, isinstance(g, int))
        transpose_y(g * GT + 2, 2)
        transpose_y(g * GT + 3, 3)

    pe.wait_ge(L.weights_loaded, 32)
    transpose_y(0, 0)
    pe.wait_ge(L.before, NT * L.x_steps)
    for t in range(1, GT):
        transpose_y(t, t)
    group(1)
    with pe.Fori(2, NG) as g:
        group(g)
    logits(NG - 1)
    pe.wait_ge(s.logitsT_ready, groups + NG)
    for t in range(NT):
        last = nc.tensor.transpose(m.context[:, t * E8:(t + 1) * E8], m.logitsT[0:E8, t * P:(t + 1) * P],
                                   m.ident[0:E8, 0:E8])
    last.then_inc(s.logits_in_psum, 1)


def router_scalar(nc, act, m, L, s):
    tiles, groups = L.round * NT, L.round * NG

    def yT(t, c):
        act.wait_ge(s.yT_in_psum, tiles + t + 1)
        nc.scalar.activation(m.yT_all[:, bass.ts(t, D)], m.ring[c % 2][:, 0:D], ACT.Identity).then_inc(s.yT_ready, 1)

    def logits(g):
        act.wait_ge(s.logitsT_in_psum, groups + g + 1)
        nc.scalar.activation(m.logitsT[0:E8, bass.ts(g, GT * P)], m.ring[2][0:E8, :],
                             ACT.Identity).then_inc(s.logitsT_ready, 1)

    for t in range(GT):
        yT(t, t)
    with act.Fori(1, NG) as g:
        for c in range(GT):
            yT(g * GT + c, c)
            if c == 1:
                logits(g - 1)
    logits(NG - 1)


def router_vector(nc, dve, m, L, s):
    tiles = L.round * NT
    for t in range(2, GT):
        y_vector(nc, dve, m, y_slot(m, t), t, L)
    with dve.Fori(1, NG) as g:
        for c in range(GT):
            dve.wait_ge(s.yT_in_psum, tiles + g * GT + c - 3)
            if L.stored is not None:
                dve.wait_ge(L.stored[c], g * 16)
            y_vector(nc, dve, m, y_slot(m, c), g * GT + c, L)
    dve.wait_ge(s.logits_in_psum, L.round + 1)
    grid = [P, NT, E8]
    nc.vector.tensor_tensor(m.logits[:, :].rearrange("p (t e) -> p t e", e=E8),
                            m.context[:, 0:NT * E8].rearrange("p (t e) -> p t e", e=E8),
                            bc(L.router_bias[:, None, :], grid), ALU.add).then_inc(s.logits_ready, 1)


def router_gpsimd(nc, pool, m, L, s):
    rstd_gpsimd(nc, pool, m, L.stats_before, 0, 2)
    rstd_gpsimd(nc, pool, m, L.stats_before, 2, NT)


MIX0 = ["route_chain", "exp_asked", "exp_done", "h_in_psum", "gelu_done", "out_in_psum", "x_done"]


def mix0_route_vector(nc, dve, m, s):
    link = Link(dve, s.route_chain, 0)
    v = nc.vector
    grid = [P, NT, E8]
    logits = m.logits[:, :].rearrange("p (t e) -> p t e", e=E8)
    biased, hit, best0, best1 = (m.route[:, n, :].rearrange("p (t e) -> p t e", e=E8) for n in range(4))
    top, low, high = m.route_col[:, 0, :], m.route_col[:, 1, :], m.route_col[:, 2, :]
    dve.wait_ge(m.logits_ready, 1)
    link(v.tensor_tensor(biased, logits, bc(m.aux_bias[:, None, :], grid), ALU.add))
    for n, best in enumerate((best0, best1)):
        link(v.tensor_reduce(top, biased, AX_X, ALU.max))
        link(v.tensor_tensor(hit, biased, bc(top[:, :, None], grid), ALU.is_equal))
        link(v.tensor_tensor(hit, hit, bc(m.order[:, None, :], grid), ALU.mult))
        link(v.tensor_reduce(top, hit, AX_X, ALU.max))
        link(v.tensor_tensor(best, hit, bc(top[:, :, None], grid), ALU.is_equal))
        if n == 0:
            link(v.scalar_tensor_tensor(biased, best, -3.0e38, biased, ALU.mult, ALU.add))
    for best, value in ((best0, low), (best1, high)):
        link(v.tensor_tensor(hit, best, logits, ALU.mult))
        link(v.tensor_reduce(value, hit, AX_X, ALU.add))
    link(v.tensor_tensor(top, low, high, ALU.max))
    link(v.tensor_tensor(low, low, top, ALU.subtract))
    v.tensor_tensor(high, high, top, ALU.subtract).then_inc(s.exp_asked, 1)
    dve.wait_ge(s.exp_done, 1)
    link(v.tensor_tensor(top, low, high, ALU.add))
    link(v.reciprocal(top, top))
    link(v.tensor_tensor(low, low, top, ALU.mult))
    link(v.tensor_tensor(high, high, top, ALU.mult))
    link(v.tensor_tensor(best0, best0, bc(low[:, :, None], grid), ALU.mult))
    link(v.tensor_tensor(best1, best1, bc(high[:, :, None], grid), ALU.mult))
    link(v.tensor_tensor(m.combine[:, :].rearrange("p (t e) -> p t e", e=E8), best0, best1, ALU.add))


def mix0_tensor(nc, pe, m, L, s):
    def hidden(t, e, first):
        n = t * E8 + e
        if not first or e >= 2:
            pe.wait_ge(s.gelu_done, n - 1)
        for f in range(DC):
            for d in range(DC):
                last = nc.tensor.matmul(m.ring[e % 2][:, f * P:(f + 1) * P], m.w1[:, e, d, f * P:(f + 1) * P],
                                        m.yT_all[:, bass.ts(t * DC + d, P)], start=d == 0, stop=d == DC - 1)
        last.then_inc(s.h_in_psum, 1)

    def out(t, e, first):
        n = t * E8 + e
        pe.wait_ge(s.gelu_done, n + 1)
        if not first or e >= 4:
            pe.wait_ge(s.x_done, n - 3)
        for f in range(DC):
            last = nc.tensor.matmul(m.scores[:, (e % 4) * 512:(e % 4) * 512 + D], m.hT[:, e % 2, f, :],
                                    m.w2[:, e, f, :], start=f == 0, stop=f == DC - 1)
        last.then_inc(s.out_in_psum, 1)

    def tile(t, first=False):
        for e in range(E8):
            hidden(t, e, first)
            if e > 0:
                out(t, e - 1, first)
            elif not first:
                out(t - 1, E8 - 1, False)

    pe.wait_ge(L.experts_loaded, 32)
    tile(0, True)
    with pe.Fori(1, NT) as t:
        tile(t)
    out(NT - 1, E8 - 1, False)


def mix0_scalar(nc, act, m, L, s):
    def gelu(t, e):
        act.wait_ge(s.h_in_psum, t * E8 + e + 1)
        nc.scalar.activation(m.hT[:, e % 2, :, :], m.ring[e % 2][:, 0:D], ACT.Gelu).then_inc(s.gelu_done, 1)

    for e in range(4):
        gelu(0, e)
    act.wait_ge(s.exp_asked, 1)
    nc.scalar.activation(m.route_col[:, 1:3, :], m.route_col[:, 1:3, :], ACT.Exp).then_inc(s.exp_done, 1)
    for e in range(4, E8):
        gelu(0, e)
    with act.Fori(1, NT) as t:
        for e in range(E8):
            gelu(t, e)


def mix0_vector(nc, dve, m, L, s, following):
    def tile(t):
        for e in range(E8):
            n = t * E8 + e
            dve.wait_ge(s.out_in_psum, n + 1)
            if e > 0:
                dve.wait_ge(s.x_done, n)
            x = m.x[:, bass.ts(t, D)]
            nc.vector.scalar_tensor_tensor(x, m.scores[:, (e % 4) * 512:(e % 4) * 512 + D],
                                           m.combine[:, bass.ds(n, 1)], x, ALU.mult, ALU.add).then_inc(s.x_done, 1)
        dve.wait_ge(s.x_done, t * E8 + E8)
        tile_stats_vector(nc, dve, m, L.stats + t, t)

    with dve.Fori(0, NT - 1) as t:
        tile(t)
    start_vector(nc, dve, m, following)
    tile(NT - 1)


CAP = N // E8
HALVES = CAP // P
F1 = 1024
FC1 = F1 // P
ROW = D + E8
TOP_PAIR = 28
SEARCH_STEPS = 5
SEARCH_LOOPS = (TOP_PAIR // 2 + 1) // SEARCH_STEPS
MIX1 = ["soft_chain", "exp_asked", "exp_done", "probs_ready", "cand_chain", "compare_ready", "count_in_psum",
        "pick_chain", "marks_ready", "ranks_in_psum", "onehot_ready", "onehot_used", "index_ready",
        "y_stored0", "y_stored1", "y_stored2", "y_stored3", "probs_stored", "x_stored", "gathered0",
        "gathered1", "xinT_in_psum", "xinT_ready", "gate_ready", "h_in_psum", "gelu_done", "out_in_psum",
        "bias_done", "out_ready", "weights_loaded0", "weights_loaded1", "scattered"]


def mix1_softmax_vector(nc, dve, m, s):
    link = Link(dve, s.soft_chain, 0)
    v = nc.vector
    grid = [P, NT, E8]
    logits = m.logits[:, :].rearrange("p (t e) -> p t e", e=E8)
    probs = m.combine[:, :].rearrange("p (t e) -> p t e", e=E8)
    col = m.route_col[:, 0, :]
    dve.wait_ge(m.logits_ready, 2)
    link(v.tensor_reduce(col, logits, AX_X, ALU.max))
    v.tensor_tensor(probs, logits, bc(col[:, :, None], grid), ALU.subtract).then_inc(s.exp_asked, 1)
    dve.wait_ge(s.exp_done, 1)
    link(v.tensor_reduce(col, probs, AX_X, ALU.add))
    link(v.reciprocal(col, col))
    v.tensor_tensor(probs, probs, bc(col[:, :, None], grid), ALU.mult).then_inc(s.probs_ready, 1)
    dve.wait_ge(s.probs_ready, 1)


def mix1_threshold_vector(nc, dve, m, s):
    v = nc.vector
    grid = [P, 3, NT, E8]
    probs = bc(m.combine[:, :].rearrange("p (o t e) -> p o t e", o=1, e=E8), grid)
    hit = m.hit3[:, :].rearrange("p (g t e) -> p g t e", g=3, e=E8)
    bits, cand, gain = (buf[:, :].rearrange("p (g e) -> p g e", g=3) for buf in (m.bits, m.cand, m.gain))
    with dve.Fori(0, SEARCH_LOOPS) as i:
        for k in range(SEARCH_STEPS):
            r = i * SEARCH_STEPS + k
            link = Link(dve, s.cand_chain, 6 * r)
            link(v.tensor_tensor(cand, bc(m.threshold[:, None, :], [P, 3, E8]), bits, ALU.bitwise_or))
            link(v.tensor_tensor(hit, probs, bc(cand[:, :, None, :].bitcast(F32), grid), ALU.is_ge))
            with nc.allow_low_precision(reason="counts up to NT are exact in bfloat16"):
                v.tensor_reduce(m.hits[:, :].rearrange("p (g e) -> p g e", g=3),
                                hit.rearrange("p g t e -> p g e t"), AX_X, ALU.add).then_inc(s.compare_ready, 1)
            dve.wait_ge(s.count_in_psum, r + 1)
            link(v.scalar_tensor_tensor(gain, m.ring[0][:, 0:3 * E8].rearrange("p (g e) -> p g e", g=3), float(CAP),
                                        bc(bits[:, 0:1, :], [P, 3, E8]), ALU.is_ge, ALU.mult))
            link.count_on(v.tensor_scalar(m.bits[:, :], m.bits[:, :], 0.25, None, ALU.mult))
            with nc.allow_low_precision(reason="a sum of equal powers of two is exact"):
                link(v.tensor_reduce(m.pair[:, :], gain.rearrange("p g e -> p e g"), AX_X, ALU.add))
            link(v.tensor_tensor(m.threshold[:, :], m.threshold[:, :], m.pair[:, :], ALU.bitwise_or))


def mix1_slots_vector(nc, dve, m, s):
    link = Link(dve, s.pick_chain, 0)
    v = nc.vector
    grid = [P, NT, E8]
    probs = m.combine[:, :].rearrange("p (t e) -> p t e", e=E8)
    level = bc(m.threshold[:, None, :].bitcast(F32), grid)
    cube = "p (t e) -> p t e"
    scan0, scan1 = m.scan0[:, :, :], m.scan1[:, :, :]
    for k, compare in enumerate((ALU.is_gt, ALU.is_equal)):
        v.tensor_tensor(m.marks[:, k, :].rearrange(cube, e=E8), probs, level, compare).then_inc(s.marks_ready, 1)
    above, equal = m.marks[:, 0, :], m.marks[:, 1, :]
    dve.wait_ge(s.ranks_in_psum, 1)
    totals, within = (m.ring[0][:, n * 2 * P:(n + 1) * 2 * P].rearrange("p (k n) -> p k n", k=2) for n in range(2))
    link(v.tensor_reduce(m.need[:, :], totals[:, 0, :].rearrange("p (t e) -> p e t", e=E8), AX_X, ALU.add))
    link(v.tensor_scalar(m.need[:, :], m.need[:, :], -1.0, float(CAP), ALU.mult, ALU.add))
    link(v.tensor_copy(scan0[:, :, 9 * E8:], totals[:, :, 0:(NT - 1) * E8]))
    for step, source, target in ((1, scan0, scan1), (2, scan1, scan0), (4, scan0, scan1), (8, scan1, scan0)):
        link(v.tensor_tensor(target[:, :, 8 * E8:], source[:, :, 8 * E8:], source[:, :, (8 - step) * E8:-step * E8],
                             ALU.add))
    ranks = m.route[:, 0:2, :]
    link(v.tensor_tensor(ranks, within, scan0[:, :, 8 * E8:], ALU.add))
    place, rank, taken = m.route[:, 0, :], m.route[:, 1, :], m.route[:, 2, :]
    need = bc(m.need[:, None, :], grid)
    link(v.tensor_tensor(taken.rearrange(cube, e=E8), rank.rearrange(cube, e=E8), need, ALU.is_lt))
    link(v.tensor_tensor(taken, taken, equal, ALU.mult))
    link(v.tensor_tensor(taken, taken, above, ALU.add))
    link(v.tensor_tensor(rank.rearrange(cube, e=E8), rank.rearrange(cube, e=E8), need, ALU.min))
    link(v.tensor_tensor(place, place, rank, ALU.add))
    link(v.scalar_tensor_tensor(place, place, -1000.0, taken, ALU.add, ALU.mult))
    link(v.tensor_scalar(m.slot[:, :], place, 1000.0, None, ALU.add))


def index_bank(m, half):
    return m.scores[:, (2 + half) * 512:(3 + half) * 512]


def mix1_index_vector(nc, dve, m, s, e, first=False):
    for t in range(NT):
        if not first:
            dve.wait_ge(s.onehot_used, e * NT + t - NT + 1)
        nc.vector.tensor_scalar(m.onehot[:, t, :], m.slots_row[:, :], m.slot[:, bass.ds(e + t * E8, 1)], None,
                                ALU.is_equal).then_inc(s.onehot_ready, 1)
    dve.wait_ge(s.onehot_used, e * NT + NT)
    for half in range(HALVES):
        with nc.allow_low_precision(reason="token indices are whole numbers"):
            last = nc.vector.tensor_reduce(m.index[:, bass.ds(e * HALVES + half, 1)],
                                           index_bank(m, half)[:, 0:2], AX_X, ALU.add)
    last.then_inc(s.index_ready, 1)


def mix1_sync(nc, sp, m, L, s, out):
    def weights(e, c):
        sp.dma_start(m.w1_slot[:, c, :, :], m.mix1_w1[bass.ds(e, 1), :, :, :].rearrange("o p c f -> p (o c) f")) \
            .then_inc([s.weights_loaded0, s.weights_loaded1][c], 16)
        sp.dma_start(m.w2_slot[:, c, :, :], m.mix1_w2[bass.ds(e, 1), :, :, :].rearrange("o p f d -> p (o f) d")) \
            .then_inc([s.weights_loaded0, s.weights_loaded1][c], 16)

    sp.wait_ge(L.mix0_done, NT * E8)
    weights(0, 0)
    weights(1, 1)
    stored = (s.y_stored0, s.y_stored1, s.y_stored2, s.y_stored3)

    def store_y(t, c):
        sp.wait_ge(m.norm.y_ready, L.ys + t + 1)
        sp.dma_start(m.y_rows[bass.ts(t, P), 0:D], y_slot(m, c)).then_inc(stored[c], 16)

    with sp.Fori(0, NT // 4) as i:
        for c in range(4):
            store_y(i * 4 + c, c)
    sp.wait_ge(L.x_done, NT)
    sp.dma_start(out.rearrange("(t p) d -> p t d", p=P),
                 m.x[:, :].rearrange("p (t d) -> p t d", d=D)).then_inc(s.x_stored, 16)
    sp.wait_ge(s.probs_ready, 1)
    sp.dma_start(m.y_rows[:, D:ROW].rearrange("(t p) e -> p t e", p=P),
                 m.combine[:, :].rearrange("p (t e) -> p t e", e=E8)).then_inc(s.probs_stored, 16)
    with sp.Fori(1, E8 // 2) as i:
        for c in range(2):
            sp.wait_ge(s.out_in_psum, (i * 2 + c) * HALVES - HALVES)
            weights(i * 2 + c, c)
    sp.wait_ge(s.scattered, 16 * E8 * HALVES)


def mix1_gpsimd(nc, pool, m, s, out):
    gathered = [s.gathered0, s.gathered1]

    def gather(e):
        c = e % 2
        pool.wait_ge(s.index_ready, e + 1)
        if e >= 2:
            pool.wait_ge(s.gate_ready, e - 1)
        for half in range(HALVES):
            n = e * HALVES + half
            pool.indirect_dma_start(m.xin[:, c, half, :], None, m.y_rows,
                                    bass.IndirectOffsetOnAxis(m.index[:, n:n + 1], 0)).then_inc(gathered[c], 16)

    def scatter(e):
        for half in range(HALVES):
            n = e * HALVES + half
            pool.wait_ge(s.out_ready, n + 1)
            if n:
                pool.wait_ge(s.scattered, 16 * n)
            pool.indirect_dma_start(out, bass.IndirectOffsetOnAxis(m.index[:, n:n + 1], 0),
                                    m.out_rows[:, e % 2, half, :], None, compute_op=ALU.add).then_inc(s.scattered, 16)

    for stored in (s.y_stored0, s.y_stored1, s.y_stored2, s.y_stored3):
        pool.wait_ge(stored, 16 * (NT // 4))
    pool.wait_ge(s.probs_stored, 16)
    gather(0)
    gather(1)
    pool.wait_ge(s.x_stored, 16)
    for e in range(E8):
        if e + 2 < E8:
            gather(e + 2)
        scatter(e)


def mix1_tensor(nc, pe, m, s):
    gathered = [s.gathered0, s.gathered1]
    weights_loaded = [s.weights_loaded0, s.weights_loaded1]

    with pe.Fori(0, SEARCH_LOOPS) as i:
        for k in range(SEARCH_STEPS):
            pe.wait_ge(s.compare_ready, i * SEARCH_STEPS + k + 1)
            nc.tensor.matmul(m.ring[0][:, 0:3 * E8], m.ones[:, :], m.hits[:, :], start=True,
                             stop=True).then_inc(s.count_in_psum, 1)
    pe.wait_ge(s.marks_ready, 2)
    for k, weight in enumerate((m.ones, m.earlier)):
        last = nc.tensor.matmul(m.ring[0][:, k * 2 * P:(k + 1) * 2 * P], weight[:, :], m.marks[:, :, :],
                                start=True, stop=True)
    last.then_inc(s.ranks_in_psum, 1)

    def index(e, first=False):
        if not first:
            pe.wait_ge(s.index_ready, e)
        for t in range(NT):
            pe.wait_ge(s.onehot_ready, e * NT + t + 1)
            for half in range(HALVES):
                last = nc.tensor.matmul(index_bank(m, half)[:, 0:2], m.onehot[:, t, half * P:(half + 1) * P],
                                        m.token[:, t, :], start=t == 0, stop=t == NT - 1)
            last.then_inc(s.onehot_used, 1)

    def transpose_rows(e, c):
        pe.wait_ge(gathered[c], (e - c) * 16 + 32)
        for d in range(DC):
            for half in range(HALVES):
                at = d * CAP + half * P
                last = nc.tensor.transpose(m.ring[0][:, at:at + P], m.xin[:, c, half, d * P:(d + 1) * P],
                                           m.ident[:, :])
        last.then_inc(s.xinT_in_psum, 1)

    def hidden(e, c, first=False):
        pe.wait_ge(weights_loaded[c], (e - c) * 16 + 32)
        pe.wait_ge(s.xinT_ready, e + 1)
        for f in range(FC1):
            n = e * FC1 + f
            if not first or f >= 2:
                pe.wait_ge(s.gelu_done, n - 1)
            for d in range(DC):
                last = nc.tensor.matmul(m.ring[1 + f % 2][:, 0:CAP], m.w1_slot[:, c, d, f * P:(f + 1) * P],
                                        m.xinT[:, d, :], start=d == 0, stop=d == DC - 1)
            last.then_inc(s.h_in_psum, 1)

    def out_rows(e, c, first=False):
        for half in range(HALVES):
            if not first:
                pe.wait_ge(s.out_ready, (e - 1) * HALVES + half + 1)
            for f in range(FC1):
                if half == 0:
                    pe.wait_ge(s.gelu_done, e * FC1 + f + 1)
                last = nc.tensor.matmul(m.scores[:, half * 512:half * 512 + D], m.h1T[:, f, half * P:(half + 1) * P],
                                        m.w2_slot[:, c, f, :], start=f == 0, stop=f == FC1 - 1)
            last.then_inc(s.out_in_psum, 1)

    def expert(e, c, indices=True, first=False):
        if indices and not first:
            index(e + 3)
        hidden(e, c, first)
        if first:
            index(e + 3)
        if not isinstance(e, int) or e < E8 - 1:
            transpose_rows(e + 1, 1 - c)
        out_rows(e, c, first)

    index(0, True)
    index(1)
    index(2)
    transpose_rows(0, 0)
    expert(0, 0, first=True)
    with pe.Fori(0, 2) as i:
        for c in range(2):
            expert(i * 2 + 1 + c, 1 - c)
    for e in range(5, E8):
        expert(e, e % 2, indices=False)


def mix1_scalar(nc, act, m, s):
    act.wait_ge(s.exp_asked, 1)
    nc.scalar.activation(m.combine[:, :], m.combine[:, :], ACT.Exp).then_inc(s.exp_done, 1)

    def rows(e, c):
        act.wait_ge(s.xinT_in_psum, e + 1)
        nc.scalar.activation(m.xinT[:, :, :], m.ring[0][:, :], ACT.Identity).then_inc(s.xinT_ready, 1)
        if not isinstance(e, int) or e >= 2:
            act.wait_ge(s.out_ready, (e - 1) * HALVES)
        nc.scalar.activation(m.gate[:, c, :], m.xin[:, c, :, bass.ds(e + D, 1)],
                             ACT.Identity).then_inc(s.gate_ready, 1)

    def hidden(e):
        for f in range(FC1):
            act.wait_ge(s.h_in_psum, e * FC1 + f + 1)
            nc.scalar.activation(m.h1T[:, f, :], m.ring[1 + f % 2][:, 0:CAP], ACT.Gelu_apprx_tanh,
                                 bias=m.b1[:, bass.ds(e * FC1 + f, 1)]).then_inc(s.gelu_done, 1)

    rows(0, 0)
    hidden(0)
    rows(1, 1)
    with act.Fori(0, E8 // 2 - 1) as i:
        for c in range(2):
            e = i * 2 + 1 + c
            hidden(e)
            rows(e + 1, c)
    hidden(E8 - 1)


def mix1_vector(nc, dve, m, s):
    def expert(e, c, first=False):
        for half in range(HALVES):
            n = e * HALVES + half
            link = Link(dve, s.bias_done, n)
            if not first:
                dve.wait_ge(s.scattered, 16 * n - 48)
            dve.wait_ge(s.out_in_psum, n + 1)
            link(nc.vector.tensor_tensor(m.out_rows[:, c, half, :], m.scores[:, half * 512:half * 512 + D],
                                         m.b2[:, bass.ts(e, D)], ALU.add))
            nc.vector.tensor_scalar(m.out_rows[:, c, half, :], m.out_rows[:, c, half, :],
                                    m.gate[:, c, half:half + 1], None, ALU.mult).then_inc(s.out_ready, 1)

    mix1_index_vector(nc, dve, m, s, 0, True)
    with dve.Fori(1, 4) as e:
        mix1_index_vector(nc, dve, m, s, e)
    for e in range(4):
        mix1_index_vector(nc, dve, m, s, e + 4)
        dve.wait_ge(s.gate_ready, e + 1)
        expert(e, e % 2, e < 2)
    with dve.Fori(2, E8 // 2) as i:
        for c in range(2):
            dve.wait_ge(s.gate_ready, i * 2 + c + 1)
            expert(i * 2 + c, c)
COL_BIAS = ["c0q", "c0k", "c0v", "c1q", "c1k", "c1v", "s1q", "s1k", "s1v", "zero"]
ROW_BIAS = ["c0o", "s0o", "c1o", "s1o", "gamma", "beta"]
N_COLS = DC * len(COL_BIAS) + FC1 * E8
FIRST_SHAPES = P + P + E8 + 2
LAYERS = ["c0", "s0", "c1", "s1"]
STAGES = ["c0", "s0", "r0", "c1", "s1", "r1"]


def perceiver(nc, x, ctxT, pad, src_mask, proj, cols, rows, small, shapes, mix0_w1, mix0_w2, mix0_router,
              mix1_w1, mix1_w2, mix1_router, mix1_b2, out):
    y_rows = nc.dram_tensor("y_rows", [N, ROW], F32, kind="Internal").ap()
    with ExitStack() as ctx:
        def sb(name, shape, dt=F32):
            return ctx.enter_context(nc.sbuf_tensor(f"sb_{name}", [P, *shape], dt))

        def by_name(stage, names):
            return {n: ctx.enter_context(nc.semaphore(f"{stage}_{n}")) for n in names}

        def sems(stage, names):
            return Named(**by_name(stage, names))

        m = Named(
            x=sb("x", [NT * D]), y=sb("y", [2, D]), z=sb("z", [2, D]), yT=sb("yT", [2, DC, P]),
            stats=sb("stats", [6]), moments=sb("moments", [NT * 2]), mean_var=sb("mean_var", [2]),
            rstd=sb("rstd", [NT]),
            z_moments=sb("z_moments", [2]), zero_eps=sb("zero_eps", [2]), z_rstd=sb("z_rstd", [1]),
            carrier=sb("carrier", [6]), drop=sb("drop", [2, S2]), big=sb("big", [1]),
            table=sb("table", [1]), minus_half=sb("minus_half", [1]), q=sb("q", [DC, P]),
            qbd=sb("qbd", [BT, NP, P]), K=sb("K", [2, DC, S2]),
            V=sb("V", [2, KT, D]), probs=sb("probs", [2, NP, S2]), pT=sb("pT", [4, 2, KT, P]),
            pT_blocks=sb("pT_blocks", [2, PG, BT, P]), contextT=sb("contextT", [DC, P]), half=sb("half", [DC, S]),
            halves=sb("halves", [DC, BT, S]), neg_max=sb("neg_max", [2, NP]), row_sum=sb("row_sum", [2, NP]),
            row_max=sb("row_max", [NP]), inv_sum=sb("inv_sum", [NP]), tile_max=sb("tile_max", [NP, BT]),
            tile_sum=sb("tile_sum", [NP * BT]), tile_inv=sb("tile_inv", [NP * BT]), ctxT=sb("ctxT", [2, DC, S2]),
            pad=sb("pad", [2, S2], I32), keep=sb("keep", [2, S2]), add_mask=sb("add_mask", [2, S2]),
            mask_part=sb("mask_part", [S2]), src_mask=sb("src_mask", [S2]), proj=sb("proj", [16, DC, D]),
            cols=sb("cols", [N_COLS]), cols4=sb("cols4", [DC * len(COL_BIAS)]), rows=sb("rows", [len(ROW_BIAS), D]),
            s0_row=sb("s0_row", [D]), shapes=sb("shapes", [P + P + E8 + 2 + 2 * S + CAP + 2 * NT]),
            yT_all=sb("yT_all", [NT * D]), router0=sb("router0", [DC, E8]), router1=sb("router1", [DC, E8]),
            small=sb("small", [2, E8]), zero_bias=sb("zero_bias", [E8]), logits=sb("logits", [NT * E8]),
            route=sb("route", [4, NT * E8]), route_col=sb("route_col", [3, NT]), combine=sb("combine", [NT * E8]),
            w1=sb("w1", [E8, DC, D]), w2=sb("w2", [E8, DC, D]), hT=sb("hT", [2, DC, P]),
            threshold=sb("threshold", [E8], I32), bits=sb("bits", [3 * E8], I32), cand=sb("cand", [3 * E8], I32),
            gain=sb("gain", [3 * E8]), pair=sb("pair", [E8], I32),
            hits=sb("hits", [3 * E8], BF16), need=sb("need", [E8]),
            marks=sb("marks", [2, NT * E8], BF16), scan0=sb("scan0", [2, (8 + NT) * E8]),
            scan1=sb("scan1", [2, (8 + NT) * E8]), slot=sb("slot", [NT * E8]),
            slots_row=sb("slots_row", [CAP], BF16), token=sb("token", [NT, 2], BF16), ones=sb("ones", [P], BF16),
            earlier=sb("earlier", [P], BF16), gate=sb("gate", [2, HALVES]), index=sb("index", [E8 * HALVES], I32),
            xin=sb("xin", [2, HALVES, ROW]), b2=sb("b2", [E8 * D]),
        )
        m.h1T = m.yT_all[:, 0:FC1 * CAP].rearrange("p (f k) -> p f k", k=CAP)
        m.xinT = m.yT_all[:, FC1 * CAP:(FC1 + DC) * CAP].rearrange("p (d k) -> p d k", k=CAP)
        m.out_rows = m.yT_all[:, (FC1 + DC) * CAP:(FC1 + DC + 4) * CAP].rearrange(
            "p (c h d) -> p c h d", c=2, d=D)
        m.w1_slot = m.w1[:, :, :, :].rearrange("p (c g) d f -> p c (g d f)", c=2).rearrange(
            "p c (d f) -> p c d f", d=DC)
        m.w2_slot = m.w2[:, :, :, :].rearrange("p (c g) d f -> p c (g d f)", c=2).rearrange(
            "p c (f d) -> p c f d", f=FC1)
        m.onehot = m.probs[:, 0, :, :].rearrange("p n k -> p (n k)").bitcast(BF16).rearrange("p (t k) -> p t k", k=CAP)
        m.logitsT = m.probs[:, 0, :, :].rearrange("p n k -> p (n k)")
        m.hit3 = m.probs[:, 1, 0:2, :].rearrange("p n k -> p (n k)")[:, 0:3 * NT * E8]
        m.y_rows, m.mix1_w1, m.mix1_w2 = y_rows, mix1_w1, mix1_w2
        m.b1 = m.cols[:, DC * len(COL_BIAS):]
        m.ring = [ctx.enter_context(nc.psum_tensor(f"ring{n}", [P, 512], F32)) for n in range(3)]
        m.context = ctx.enter_context(nc.psum_tensor("context", [P, 512], F32))
        m.scores = ctx.enter_context(nc.psum_tensor("scores", [P, 4 * 512], F32))
        m.ctxT_dram, m.pad_dram = ctxT.rearrange("(c p) n -> p c n", p=P), pad
        at = [0]

        def shape_part(width):
            at[0] += width
            return m.shapes[:, at[0] - width:at[0]]

        m.ident, m.before, m.order = shape_part(P), shape_part(P), shape_part(E8)
        m.even_head, m.odd_head = shape_part(1), shape_part(1)
        m.causal, m.causal_add = shape_part(S), shape_part(S)
        m.slots_row_f, m.token_f = shape_part(CAP), shape_part(2 * NT)
        m.head = sb("head", [E8])
        m.gamma = m.rows[:, ROW_BIAS.index("gamma"), :]
        m.aux_bias = m.small[:, 0, :]

        load = sems("load", ["x_first", "x_rest", "first_consts", "rows", "consts", "proj_query",
                             "proj0", "proj1", "proj2", "proj3",
                             "experts0", "routers", "consts_ready"])

        m.consts_ready = load.consts_ready

        def layer(n, before, x_steps, rstd_at, **more):
            name = LAYERS[n]
            wq, wk, wv, wo = (m.proj[:, 4 * n + k, :, :] for k in range(4))

            def col(kind, of=m.cols):
                i = COL_BIAS.index(name + kind if name + kind in COL_BIAS else "zero") * DC
                return of[:, i:i + DC]

            return Named(wq=wq, wk=wk, wv=wv, wo=wo, bq=col("q", m.cols4), bk=col("k"), bv=col("v"),
                         bo=m.s0_row[:, :] if n == 1 else m.rows[:, ROW_BIAS.index(name + "o"), :],
                         weights_loaded=[load.proj0, load.proj1, load.proj2, load.proj3][n],
                         before=before, x_steps=x_steps, masked=n == 2, causal=n == 3, normed=n == 1,
                         first=NT if n == 3 else 0, ys=STAGES.index(name) * NT, stats=(n + n // 2) * NT,
                         stats_before=(n + n // 2) * NT, first_norms=2 if n % 2 else 1,
                         rstd_at=rstd_at, rstd_rest=rstd_at and rstd_at + (3 if n == 1 else 1), **more)

        m.norm = sems("norm", NORM)
        self_sems = by_name("self", SELF)
        c0, router, m0 = sems("c0", CROSS), sems("router", ROUTER), sems("m0", MIX0)
        c1, m1 = sems("c1", CROSS + MASKED), sems("m1", MIX1)
        s0 = Named(**self_sems, **by_name("s0", ["x_done", "soft_chain", "z_chain"]))
        s1 = Named(**self_sems, **by_name("s1", ["x_done", "soft_chain", "shifted", "causal_ready"]))
        m.logits_ready = router.logits_ready
        C0 = layer(0, None, 1, None, x_first=load.x_first, x_rest=load.x_rest, rows=load.rows,
                   proj_query=load.proj_query, ctx_free=None)
        S0 = layer(1, c0.x_done, 1, NT + 1)
        R0 = Named(round=0, before=s0.x_done, x_steps=1, rstd_at=2 * NT + 3, rstd_rest=2 * NT + 4,
                   stats_before=2 * NT, first_norms=2, ys=2 * NT, router=m.router0,
                   router_bias=m.zero_bias, weights_loaded=load.routers, stored=None)
        M0 = Named(experts_loaded=load.experts0, stats=2 * NT)
        C1 = layer(2, m0.x_done, E8, 2 * NT + 5, rows=None, proj_query=None, ctx_free=c0.v_in_psum)
        S1 = layer(3, c1.x_done, 1, 2 * NT + 7)
        R1 = Named(round=1, before=s1.x_done, x_steps=1, rstd_at=2 * NT + 9, rstd_rest=2 * NT + 10,
                   stats_before=5 * NT, first_norms=2, ys=5 * NT, router=m.router1,
                   router_bias=m.small[:, 1, :], weights_loaded=load.routers,
                   stored=(m1.y_stored0, m1.y_stored1, m1.y_stored2, m1.y_stored3))
        M1 = Named(mix0_done=m0.x_done, x_done=s1.x_done, ys=5 * NT)

        block = ctx.enter_context(nc.Block())

        @block.sync
        def _(sp):
            sp.dma_start(m.x[:, 0:D], x[0:P, :]).then_inc(load.x_first, 16)
            sp.dma_start(m.shapes[:, 0:FIRST_SHAPES], shapes[:, 0:FIRST_SHAPES]).then_inc(load.first_consts, 16)
            sp.dma_start(m.cols[:, :], cols).then_inc(load.first_consts, 16)
            sp.dma_start(m.head[:, :], shapes[:, m.shapes.shape[1]:]).then_inc(load.first_consts, 16)
            sp.dma_start(m.proj[:, 0:1, :, :], proj[:, 0:1, :, :]).then_inc(load.proj_query, 16)
            sp.dma_start(m.proj[:, 1:4, :, :], proj[:, 1:4, :, :]).then_inc(load.proj0, 16)

            def x_and_bias():
                sp.dma_start(m.rows[:, :, :], bc(rows[None, :, :], [P, len(ROW_BIAS), D])).then_inc(load.rows, 16)
                sp.dma_start(m.x[:, D:].rearrange("p (t d) -> p t d", d=D),
                             x[P:, :].rearrange("(t p) d -> p t d", p=P)).then_inc(load.x_rest, 16)

            def later_loads():
                for n, sem in ((1, load.proj1), (2, load.proj2), (3, load.proj3)):
                    sp.dma_start(m.proj[:, 4 * n:4 * n + 4, :, :], proj[:, 4 * n:4 * n + 4, :, :]).then_inc(sem, 16)
                sp.dma_start(m.shapes[:, FIRST_SHAPES:], shapes[:, FIRST_SHAPES:m.shapes.shape[1]]) \
                    .then_inc(load.consts, 16)
                sp.dma_start(m.small[:, :, :], bc(small[None, :, :], [P, 2, E8])).then_inc(load.consts, 16)
                for a in range(2):
                    sp.dma_start(m.src_mask[a * S:(a + 1) * S, :], src_mask).then_inc(load.consts, 16)
                sp.dma_start(m.router0[:, :, :], mix0_router).then_inc(load.routers, 16)
                sp.dma_start(m.router1[:, :, :], mix1_router).then_inc(load.routers, 16)
                sp.dma_start(m.w1[:, :, :, :], mix0_w1).then_inc(load.experts0, 16)
                sp.dma_start(m.w2[:, :, :, :], mix0_w2).then_inc(load.experts0, 16)
                sp.dma_start(m.b2[:, :], bc(mix1_b2.rearrange("(o e) d -> o (e d)", o=1), [P, E8 * D])) \
                    .then_inc(load.consts, 16)

            cross_sync(nc, sp, m, C0, c0, x_and_bias, later_loads)
            cross_sync(nc, sp, m, C1, c1)
            mix1_sync(nc, sp, m, M1, m1, out)

        @block.tensor
        def _(pe):
            pe.wait_ge(load.consts_ready, 2)
            cross_tensor(nc, pe, m, C0, c0)
            self_tensor(nc, pe, m, S0, s0)
            router_tensor(nc, pe, m, R0, router)
            mix0_tensor(nc, pe, m, M0, m0)
            cross_tensor(nc, pe, m, C1, c1)
            self_tensor(nc, pe, m, S1, s1)
            router_tensor(nc, pe, m, R1, router)
            mix1_tensor(nc, pe, m, m1)

        @block.scalar
        def _(act):
            act.wait_ge(load.consts_ready, 1)
            nc.scalar.activation(m.table[:, :], m.zero_bias[:, 0:1], ACT.Exp)
            act.wait_ge(load.consts_ready, 2)
            cross_scalar(nc, act, m, C0, c0)
            self_scalar(nc, act, m, S0, s0)
            router_scalar(nc, act, m, R0, router)
            mix0_scalar(nc, act, m, M0, m0)
            cross_scalar(nc, act, m, C1, c1)
            self_scalar(nc, act, m, S1, s1)
            router_scalar(nc, act, m, R1, router)
            mix1_scalar(nc, act, m, m1)

        @block.vector
        def _(dve):
            nc.vector.memset(m.zero_bias[:, :], 0.0).then_inc(load.consts_ready, 1)
            nc.vector.memset(m.minus_half[:, :], -0.5)
            nc.vector.memset(m.zero_eps[:, 0:1], 0.0)
            nc.vector.memset(m.zero_eps[:, 1:2], EPS)
            nc.vector.memset(m.big[:, :], -NEG_PAD)
            nc.vector.memset(m.pT_blocks[:, :, :, :, :], 0.0)
            nc.vector.memset(m.threshold[:, :], 0)
            for g in range(3):
                nc.vector.memset(m.bits[:, g * E8:(g + 1) * E8], (g + 1) << TOP_PAIR)
            nc.vector.memset(m.scan0[:, :, :], 0.0)
            nc.vector.memset(m.scan1[:, :, :], 0.0)
            nc.vector.memset(m.ones[:, :], 1.0)
            dve.wait_ge(load.first_consts, 16 * 3)
            nc.vector.tensor_scalar(m.cols4[:, :], m.cols[:, 0:DC * len(COL_BIAS)], HD ** -0.5, None,
                                    ALU.mult).then_inc(load.consts_ready, 1)
            dve.wait_ge(load.consts_ready, 2)
            cross_vector(nc, dve, m, C0, c0, S0)
            dve.wait_ge(load.consts, 16 * 5)
            nc.vector.tensor_copy(m.earlier[:, :], m.before)
            nc.vector.tensor_copy(m.slots_row[:, :], m.slots_row_f)
            nc.vector.tensor_copy(m.token[:, :, :], m.token_f)
            nc.vector.tensor_tensor(m.s0_row[:, :], m.rows[:, ROW_BIAS.index("s0o"), :],
                                    m.rows[:, ROW_BIAS.index("beta"), :], ALU.add).then_inc(load.consts_ready, 1)
            dve.wait_ge(load.consts_ready, 3)
            self_vector(nc, dve, m, S0, s0, R0)
            router_vector(nc, dve, m, R0, router)
            mix0_route_vector(nc, dve, m, m0)
            mix0_vector(nc, dve, m, M0, m0, C1)
            cross_vector(nc, dve, m, C1, c1, S1)
            self_vector(nc, dve, m, S1, s1, R1)
            router_vector(nc, dve, m, R1, router)
            mix1_softmax_vector(nc, dve, m, m1)
            mix1_threshold_vector(nc, dve, m, m1)
            mix1_slots_vector(nc, dve, m, m1)
            mix1_vector(nc, dve, m, m1)

        @block.gpsimd
        def _(pool):
            pool.wait_ge(load.consts_ready, 2)
            cross_gpsimd(nc, pool, m, C0, c0)
            self_gpsimd(nc, pool, m, S0, s0)
            router_gpsimd(nc, pool, m, R0, router)
            cross_gpsimd(nc, pool, m, C1, c1)
            self_gpsimd(nc, pool, m, S1, s1)
            router_gpsimd(nc, pool, m, R1, router)
            mix1_gpsimd(nc, pool, m, m1, out)


def _constants(np):
    p = np.arange(P)
    q, k = np.arange(P)[:, None] % S, np.arange(S)[None, :]
    causal = (k <= q).astype(np.float32)
    return np.concatenate([
        np.eye(P, dtype=np.float32),
        (p[:, None] < p[None, :]).astype(np.float32),
        np.tile(E8 - np.arange(E8, dtype=np.float32), (P, 1)),
        ((p // HD) % 2 == 0).astype(np.float32)[:, None],
        ((p // HD) % 2 == 1).astype(np.float32)[:, None],
        causal,
        np.where(causal == 0, np.float32(NEG_CAUSAL), np.float32(0)),
        np.tile(np.arange(CAP, dtype=np.float32), (P, 1)),
        np.stack(np.broadcast_arrays(P * np.arange(NT)[None, :], p[:, None]), axis=2).reshape(P, 2 * NT),
        (p[:, None] // HD == np.arange(E8)[None, :]).astype(np.float32),
    ], axis=1).astype(np.float32)


def layout(np, i):
    def chunks(w):
        return np.ascontiguousarray(w.reshape(-1, P, w.shape[-1]).transpose(1, 0, 2))

    def col(v):
        return v.reshape(-1, P).T

    qkv = i["L0_attn_W_qkv"]
    proj = [i["L0_xattn_w_q"].T, i["L0_xattn_w_k"].T, i["L0_xattn_w_v"].T, i["L0_xattn_w_o"].T,
            qkv[0:D].T, qkv[D:2 * D].T, qkv[2 * D:].T, i["L0_attn_W_proj"].T,
            i["L1_xattn_Wq"].T, i["L1_xattn_Wk"].T, i["L1_xattn_Wv"].T, i["L1_xattn_Wo"].T,
            i["L1_attn_Wq"], i["L1_attn_Wk"], i["L1_attn_Wv"], i["L1_attn_Wo"]]
    biases = dict(c0q=i["L0_xattn_b_q"], c0k=i["L0_xattn_b_k"], c0v=i["L0_xattn_b_v"], c1q=i["L1_xattn_bq"],
                  c1k=i["L1_xattn_bk"], c1v=i["L1_xattn_bv"], s1q=i["L1_attn_bq"], s1k=i["L1_attn_bk"],
                  s1v=i["L1_attn_bv"], zero=np.zeros(D, np.float32))
    rows = dict(c0o=i["L0_xattn_b_o"], s0o=i["L0_attn_b_proj"], c1o=i["L1_xattn_bo"], s1o=i["L1_attn_bo"],
                gamma=i["L0_attn_ln_gamma"], beta=i["L0_attn_ln_beta"])
    return dict(
        x=i["x"].reshape(N, D),
        ctxT=np.ascontiguousarray(i["ctx_1024"].reshape(B * S2, D).T),
        pad=i["mask_BxS2_ik0"],
        src_mask=i["mask_1x1xSxS2_ff0"].reshape(S, S2),
        proj=np.ascontiguousarray(np.stack([chunks(w) for w in proj], axis=1)),
        cols=np.ascontiguousarray(np.concatenate(
            [col(biases[n]) for n in COL_BIAS] + [col(i["L1_ffn_b1"].reshape(-1))], axis=1)),
        rows=np.stack([rows[n] for n in ROW_BIAS]),
        small=np.stack([i["L0_ffn_auxfree_bias"], i["L1_ffn_bs"]]),
        shapes=_constants(np),
        mix0_w1=np.ascontiguousarray(i["L0_ffn_w1"].transpose(0, 2, 1).reshape(E8, DC, P, D).transpose(2, 0, 1, 3)),
        mix0_w2=np.ascontiguousarray(i["L0_ffn_w2"].transpose(0, 2, 1).reshape(E8, DC, P, D).transpose(2, 0, 1, 3)),
        mix0_router=chunks(i["L0_ffn_router_w"].T),
        mix1_w1=np.ascontiguousarray(i["L1_ffn_W1"].reshape(E8, DC, P, F1).transpose(0, 2, 1, 3)),
        mix1_w2=np.ascontiguousarray(i["L1_ffn_W2"].reshape(E8, FC1, P, D).transpose(0, 2, 1, 3)),
        mix1_router=chunks(i["L1_ffn_Ws"]),
        mix1_b2=i["L1_ffn_b2"],
    )


def kernel(**inputs):
    import numpy as np
    import concourse.bacc as bacc
    from concourse.bass_utils import run_bass_kernel_spmd

    nc = bacc.Bacc("TRN2", target_bir_lowering=False, num_devices=1)
    arrays = layout(np, {k: np.asarray(v) for k, v in inputs.items()})
    args = [nc.dram_tensor(f"in_{n}", a.shape, mybir.dt.from_np(a.dtype), kind="ExternalInput").ap()
            for n, a in arrays.items()]
    out = nc.dram_tensor("out_x", [N, D], F32, kind="ExternalOutput").ap()
    perceiver(nc, *args, out)
    r = run_bass_kernel_spmd(nc, [{f"in_{n}": a for n, a in arrays.items()}], core_ids=[0])
    return r.results[0]["out_x"].reshape(B, S, D)
```
